# Optimizing a Trainium2 kernel written in Bass

```python
import numpy as np
import jax
import jax.numpy as jnp

def _softmax(x, axis=-1):
    return jax.nn.softmax(x, axis=axis)

def _gelu(x):
    return jax.nn.gelu(x, approximate=True)

def _silu(x):
    return jax.nn.silu(x)

def _sigmoid(x):
    return jax.nn.sigmoid(x)

def _layernorm(x, axis=-1, eps=1e-05):
    m = jnp.mean(x, axis=axis, keepdims=True)
    v = jnp.var(x, axis=axis, keepdims=True)
    return (x - m) / jnp.sqrt(v + eps)

def _scatter_add(tgt, idx, src, axis=0):
    return tgt.at[idx].add(src)

def _segment_sum(src, seg, n):
    return jax.ops.segment_sum(src, seg, n)
kernel_name = 'mk_gnn_preln_d4_gnn_r32_bddfb6'

def setup_inputs(seed: int=0):
    np.random.seed(seed)
    _w = jnp.asarray

    def _rec_inputs():
        import jax
        import jax.numpy as jnp
        _gk = jax.random.key(seed)
        x = -8.776e-05 + 1 * jax.random.normal(jax.random.fold_in(_gk, 1), (50000, 128), jnp.float32)
        src = jax.random.randint(jax.random.fold_in(_gk, 2), (25000,), 0, 50000, jnp.int32)
        dst = jax.random.randint(jax.random.fold_in(_gk, 3), (25000,), 0, 50000, jnp.int32)
        _o = jnp.argsort(dst, stable=True)
        src = src[_o]
        dst = dst[_o]
        edge_attr_4 = 0.000714719 + 1.00021 * jax.random.normal(jax.random.fold_in(_gk, 11), (25000, 4), jnp.float32)
        edge_attr_64 = 0.000102155 + 1.00015 * jax.random.normal(jax.random.fold_in(_gk, 12), (25000, 64), jnp.float32)
        return (x, src, dst, edge_attr_4, edge_attr_64)
    x, src, dst, edge_attr_4, edge_attr_64 = _rec_inputs()

    def _L0_gnn_setup():
        import jax, jax.numpy as jnp
        import numpy as np
        N_NODES = 1250
        N_EDGES = 20000
        D_FEAT = 128
        key = jax.random.key(seed)
        k1, k2, k3, k4 = jax.random.split(key, 4)
        x = jax.random.normal(k1, (N_NODES, D_FEAT), dtype=jnp.float32)
        beta = jax.random.uniform(k2, (1,), dtype=jnp.float32)
        row = jax.random.randint(k3, (N_EDGES,), 0, N_NODES)
        col = (row + 1 + jax.random.randint(k4, (N_EDGES,), 0, N_NODES - 1)) % N_NODES
        edge_index = jnp.stack([row, col]).astype(jnp.int64)
        return {'x': x, 'beta': beta, 'edge_index': edge_index}
    _L0_gnn_all = _L0_gnn_setup()
    _L0_gnn_in = {k: v for k, v in _L0_gnn_all.items() if k in ('beta',)}
    del _L0_gnn_all

    def _L1_gnn_setup():
        import jax, jax.numpy as jnp
        import numpy as np
        N, H, E, DE = (50000, 128, 25000, 4)
        key = jax.random.key(seed)
        ks = jax.random.split(key, 16)

        def dense(k, din, dout):
            kw, kb = jax.random.split(k)
            W = jax.random.normal(kw, (din, dout), jnp.float32) / jnp.sqrt(jnp.float32(din))
            b = jnp.zeros((dout,), jnp.float32)
            return (W, b)
        node_feats = jax.random.normal(ks[0], (N, H), jnp.float32)
        edge_index = jax.random.randint(ks[1], (2, E), 0, N, jnp.int32)
        edge_feats = jax.random.normal(ks[2], (E, DE), jnp.float32)
        W_msg1, b_msg1 = dense(ks[3], 2 * H + DE, H)
        W_msg2, b_msg2 = dense(ks[4], H, H)
        W_z, b_z = dense(ks[5], 2 * H, H)
        W_r, b_r = dense(ks[6], 2 * H, H)
        W_h, b_h = dense(ks[7], 2 * H, H)
        return {'node_feats': node_feats, 'edge_index': edge_index, 'edge_feats': edge_feats, 'W_msg1': W_msg1, 'b_msg1': b_msg1, 'W_msg2': W_msg2, 'b_msg2': b_msg2, 'W_z': W_z, 'b_z': b_z, 'W_r': W_r, 'b_r': b_r, 'W_h': W_h, 'b_h': b_h}
    _L1_gnn_all = _L1_gnn_setup()
    _L1_gnn_in = {k: v for k, v in _L1_gnn_all.items() if k in ('W_msg1', 'b_msg1', 'W_msg2', 'b_msg2', 'W_z', 'b_z', 'W_r', 'b_r', 'W_h', 'b_h')}
    del _L1_gnn_all

    def _L2_gnn_setup():
        import jax, jax.numpy as jnp
        import numpy as np
        N_NODES = 50000
        N_EDGES = 15625
        N_SCALARS = 128
        DIST_EMB = 64
        LN_EPS = 1e-05
        NEG_SLOPE = 0.01

        def _layer_norm(x, g, b):
            mu = jnp.mean(x, axis=-1, keepdims=True)
            var = jnp.mean(jnp.square(x - mu), axis=-1, keepdims=True)
            return (x - mu) * jax.lax.rsqrt(var + LN_EPS) * g + b
        key = jax.random.key(seed)
        ks = jax.random.split(key, 12)
        d, e = (N_SCALARS, DIST_EMB)
        msg_in = 2 * d + e
        h = 3 * d

        def init_w(k, fan_in, fan_out):
            lim = 1.0 / np.sqrt(fan_in)
            return jax.random.uniform(k, (fan_in, fan_out), jnp.float32, -lim, lim)
        return {'x': jax.random.normal(ks[0], (N_NODES, d), jnp.float32), 'edge_index': jax.random.randint(ks[1], (2, N_EDGES), 0, N_NODES, jnp.int64), 'dist_embedding': jax.random.normal(ks[2], (N_EDGES, e), jnp.float32), 'ln1_g': jnp.ones((d,), jnp.float32), 'ln1_b': jnp.zeros((d,), jnp.float32), 'ln2_g': jnp.ones((d,), jnp.float32), 'ln2_b': jnp.zeros((d,), jnp.float32), 'conv_w1': init_w(ks[3], msg_in, h), 'conv_b1': jnp.zeros((h,), jnp.float32), 'conv_w2': init_w(ks[4], h, d), 'conv_b2': jnp.zeros((d,), jnp.float32), 'ff_w1': init_w(ks[5], d, h), 'ff_b1': jnp.zeros((h,), jnp.float32), 'ff_w2': init_w(ks[6], h, d), 'ff_b2': jnp.zeros((d,), jnp.float32)}
    _L2_gnn_all = _L2_gnn_setup()
    _L2_gnn_in = {k: v for k, v in _L2_gnn_all.items() if k in ('ln1_g', 'ln1_b', 'ln2_g', 'ln2_b', 'conv_w1', 'conv_b1', 'conv_w2', 'conv_b2', 'ff_w1', 'ff_b1', 'ff_w2', 'ff_b2')}
    del _L2_gnn_all

    def _L3_gnn_setup():
        import jax, jax.numpy as jnp
        import numpy as np
        N = 3125
        E = 50000
        C_IN = 128
        C_OUT = 128
        key = jax.random.key(seed)
        k1, k2, k3 = jax.random.split(key, 3)
        x = jax.random.normal(k1, (N, C_IN), dtype=jnp.float32)
        edge_index = jax.random.randint(k2, (2, E), 0, N, dtype=jnp.int64)
        W = jax.random.normal(k3, (C_OUT, C_IN), dtype=jnp.float32) * (1.0 / np.sqrt(C_IN))
        return {'x': x, 'edge_index': edge_index, 'W': W}
    _L3_gnn_all = _L3_gnn_setup()
    _L3_gnn_in = {k: v for k, v in _L3_gnn_all.items() if k in ('W',)}
    del _L3_gnn_all
    return {'x': x, 'src': src, 'dst': dst, 'edge_attr_4': edge_attr_4, 'edge_attr_64': edge_attr_64, 'L0_gnn_beta': _L0_gnn_in['beta'], 'L1_gnn_W_msg1': _L1_gnn_in['W_msg1'], 'L1_gnn_b_msg1': _L1_gnn_in['b_msg1'], 'L1_gnn_W_msg2': _L1_gnn_in['W_msg2'], 'L1_gnn_b_msg2': _L1_gnn_in['b_msg2'], 'L1_gnn_W_z': _L1_gnn_in['W_z'], 'L1_gnn_b_z': _L1_gnn_in['b_z'], 'L1_gnn_W_r': _L1_gnn_in['W_r'], 'L1_gnn_b_r': _L1_gnn_in['b_r'], 'L1_gnn_W_h': _L1_gnn_in['W_h'], 'L1_gnn_b_h': _L1_gnn_in['b_h'], 'L2_gnn_ln1_g': _L2_gnn_in['ln1_g'], 'L2_gnn_ln1_b': _L2_gnn_in['ln1_b'], 'L2_gnn_ln2_g': _L2_gnn_in['ln2_g'], 'L2_gnn_ln2_b': _L2_gnn_in['ln2_b'], 'L2_gnn_conv_w1': _L2_gnn_in['conv_w1'], 'L2_gnn_conv_b1': _L2_gnn_in['conv_b1'], 'L2_gnn_conv_w2': _L2_gnn_in['conv_w2'], 'L2_gnn_conv_b2': _L2_gnn_in['conv_b2'], 'L2_gnn_ff_w1': _L2_gnn_in['ff_w1'], 'L2_gnn_ff_b1': _L2_gnn_in['ff_b1'], 'L2_gnn_ff_w2': _L2_gnn_in['ff_w2'], 'L2_gnn_ff_b2': _L2_gnn_in['ff_b2'], 'L3_gnn_W': _L3_gnn_in['W']}

def reference(x, src, dst, edge_attr_4, edge_attr_64, L0_gnn_beta, L1_gnn_W_msg1, L1_gnn_b_msg1, L1_gnn_W_msg2, L1_gnn_b_msg2, L1_gnn_W_z, L1_gnn_b_z, L1_gnn_W_r, L1_gnn_b_r, L1_gnn_W_h, L1_gnn_b_h, L2_gnn_ln1_g, L2_gnn_ln1_b, L2_gnn_ln2_g, L2_gnn_ln2_b, L2_gnn_conv_w1, L2_gnn_conv_b1, L2_gnn_conv_w2, L2_gnn_conv_b2, L2_gnn_ff_w1, L2_gnn_ff_b1, L2_gnn_ff_w2, L2_gnn_ff_b2, L3_gnn_W):
    import jax
    import jax.numpy as jnp

    def _L0_gnn_ref(x, beta, edge_index):
        import jax, jax.numpy as jnp
        import numpy as np
        N_NODES = 1250
        N_EDGES = 20000
        D_FEAT = 128
        num_nodes = x.shape[0]
        row, col = (edge_index[0], edge_index[1])
        loop = jnp.arange(num_nodes, dtype=row.dtype)
        row = jnp.concatenate([row, loop])
        col = jnp.concatenate([col, loop])
        norm = jnp.linalg.norm(x, axis=1)
        alpha = jnp.sum(x[row] * x[col], axis=1) / (norm[row] * norm[col])
        alpha = alpha * beta[0]
        amax = jax.ops.segment_max(alpha, row, num_segments=num_nodes)
        alpha = jnp.exp(alpha - amax[row])
        denom = jax.ops.segment_sum(alpha, row, num_segments=num_nodes)
        alpha = alpha / denom[row]
        out = jax.ops.segment_sum(alpha[:, None] * x[col], row, num_segments=num_nodes)
        return out

    def _L1_gnn_ref(node_feats, edge_index, edge_feats, W_msg1, b_msg1, W_msg2, b_msg2, W_z, b_z, W_r, b_r, W_h, b_h):
        import jax, jax.numpy as jnp
        import numpy as np
        N, H, E, DE = (50000, 128, 25000, 4)
        n = node_feats.shape[0]
        src_idx = edge_index[0]
        dst_idx = edge_index[1]
        h_src = node_feats[src_idx]
        h_dst = node_feats[dst_idx]
        msg_input = jnp.concatenate([h_src, h_dst, edge_feats], axis=-1)
        messages = jax.nn.relu(msg_input @ W_msg1 + b_msg1)
        messages = messages @ W_msg2 + b_msg2
        agg = jax.ops.segment_sum(messages, dst_idx, num_segments=n)
        hx = jnp.concatenate([node_feats, agg], axis=-1)
        z = jax.nn.sigmoid(hx @ W_z + b_z)
        r = jax.nn.sigmoid(hx @ W_r + b_r)
        h_tilde = jnp.tanh(jnp.concatenate([r * node_feats, agg], axis=-1) @ W_h + b_h)
        return (1.0 - z) * node_feats + z * h_tilde

    def _L2_gnn_ref(x, edge_index, dist_embedding, ln1_g, ln1_b, ln2_g, ln2_b, conv_w1, conv_b1, conv_w2, conv_b2, ff_w1, ff_b1, ff_w2, ff_b2):
        import jax, jax.numpy as jnp
        import numpy as np
        N_NODES = 50000
        N_EDGES = 15625
        N_SCALARS = 128
        DIST_EMB = 64
        LN_EPS = 1e-05
        NEG_SLOPE = 0.01

        def _layer_norm(x, g, b):
            mu = jnp.mean(x, axis=-1, keepdims=True)
            var = jnp.mean(jnp.square(x - mu), axis=-1, keepdims=True)
            return (x - mu) * jax.lax.rsqrt(var + LN_EPS) * g + b
        src, dst = (edge_index[0], edge_index[1])
        x_ = _layer_norm(x, ln1_g, ln1_b)
        feat = jnp.concatenate([x_[dst], x_[src], dist_embedding], axis=-1)
        m = jax.nn.leaky_relu(feat @ conv_w1 + conv_b1, NEG_SLOPE)
        m = m @ conv_w2 + conv_b2
        agg = jax.ops.segment_sum(m, dst, num_segments=x.shape[0])
        x = x + agg
        x_ = _layer_norm(x, ln2_g, ln2_b)
        x_ = jax.nn.leaky_relu(x_ @ ff_w1 + ff_b1, NEG_SLOPE) @ ff_w2 + ff_b2
        return x + x_

    def _L3_gnn_ref(x, edge_index, W):
        import jax, jax.numpy as jnp
        import numpy as np
        N = 3125
        E = 50000
        C_IN = 128
        C_OUT = 128
        n_nodes = x.shape[0]
        row, col = (edge_index[0], edge_index[1])
        deg = jax.ops.segment_sum(jnp.ones((row.shape[0],), dtype=x.dtype), row, num_segments=n_nodes)
        inv_sqrt = jax.lax.rsqrt(deg + 1.0)
        xs = x * inv_sqrt[:, None]
        agg = jax.ops.segment_sum(xs[col], row, num_segments=n_nodes) + xs
        out = agg * inv_sqrt[:, None]
        return jnp.matmul(out, W.T)
    edge_index = jnp.stack([src, dst])
    h = jnp.maximum(_layernorm(x, axis=-1), 0.0)
    x = x + _L0_gnn_ref(h, L0_gnn_beta, edge_index)
    h = jnp.maximum(_layernorm(x, axis=-1), 0.0)
    x = x + _L1_gnn_ref(h, edge_index, edge_attr_4, L1_gnn_W_msg1, L1_gnn_b_msg1, L1_gnn_W_msg2, L1_gnn_b_msg2, L1_gnn_W_z, L1_gnn_b_z, L1_gnn_W_r, L1_gnn_b_r, L1_gnn_W_h, L1_gnn_b_h)
    h = jnp.maximum(_layernorm(x, axis=-1), 0.0)
    x = x + _L2_gnn_ref(h, edge_index, edge_attr_64, L2_gnn_ln1_g, L2_gnn_ln1_b, L2_gnn_ln2_g, L2_gnn_ln2_b, L2_gnn_conv_w1, L2_gnn_conv_b1, L2_gnn_conv_w2, L2_gnn_conv_b2, L2_gnn_ff_w1, L2_gnn_ff_b1, L2_gnn_ff_w2, L2_gnn_ff_b2)
    h = jnp.maximum(_layernorm(x, axis=-1), 0.0)
    x = x + _L3_gnn_ref(h, edge_index, L3_gnn_W)
    return x

_drawn_inputs = setup_inputs


def setup_inputs(seed=0):
    import zlib

    import numpy as np

    out = dict(_drawn_inputs(seed))
    spreads = {'L1_gnn_b_msg1': (0.0, 0.8),
     'L1_gnn_b_msg2': (0.0, 0.595),
     'L1_gnn_b_z': (0.0, 0.707),
     'L1_gnn_b_r': (0.0, 0.8),
     'L1_gnn_b_h': (0.0, 0.373),
     'L2_gnn_ln1_g': (1.0, 0.6),
     'L2_gnn_ln1_b': (0.0, 0.8),
     'L2_gnn_ln2_g': (1.0, 0.6),
     'L2_gnn_ln2_b': (0.0, 0.8),
     'L2_gnn_conv_b1': (0.0, 0.567),
     'L2_gnn_conv_b2': (0.0, 0.1),
     'L2_gnn_ff_b1': (0.0, 0.562),
     'L2_gnn_ff_b2': (0.0, 0.1)}
    factors = {'edge_attr_4': 5.577, 'L1_gnn_W_r': 3.359}
    for name, (base, spread) in spreads.items():
        noise = np.random.default_rng([zlib.crc32(name.encode()), seed]).standard_normal(out[name].shape)
        drawn = base * np.exp(spread * noise) if base else spread * noise
        out[name] = jnp.asarray(drawn.astype(out[name].dtype))
    for name, factor in factors.items():
        out[name] = (out[name] * factor).astype(out[name].dtype)
    return out
```

```python
import concourse.bass as bass
from concourse import mybir
from contextlib import ExitStack


P = 128
T = 4
D = 128
W = T * P
F = 3 * D
FC = F // D
D4 = 4
D64 = 64
A0 = D + 2
X3 = D + 1
LN_EPS = 1e-5
SLOPE = 0.01

fp32 = mybir.dt.float32
int32 = mybir.dt.int32
ALU = mybir.AluOpType
ACT = mybir.ActivationFunctionType


def past(g, back):
    return not isinstance(g, int) or g >= back


def sweep(eng, groups, step):
    for g in range(4):
        step(g, g // 2, g % 2)
    pairs = (groups - 1) // 2
    with eng.Fori(2, pairs) as k:
        for s in range(2):
            step(2 * k + s, k, s)
    for g in range(2 * pairs, groups):
        step(g, g // 2, g % 2)


def block_of(view, g):
    return view[bass.ds(g, 1), :, :].rearrange("o p f -> (o p) f")


class Scope:

    def __init__(self, nc, tag):
        self.nc, self.tag, self.ctx, self.sems = nc, tag, ExitStack(), []
        self.ticks = self.sem("ticks")

    def sb(self, name, shape, dt=fp32):
        return self.ctx.enter_context(self.nc.sbuf_tensor(f"{self.tag}_{name}", shape, dt))

    def ps(self, name, shape):
        return self.ctx.enter_context(self.nc.psum_tensor(f"{self.tag}_{name}", shape, fp32))

    def sem(self, name):
        s = self.nc.alloc_semaphore(f"{self.tag}_{name}")
        self.sems.append(s)
        return s

    def sem2(self, name):
        return [self.sem(f"{name}{s}") for s in range(2)]

    def close(self):
        self.ctx.close()
        self.nc.clear_and_free_semaphores(self.sems)
        self.nc.all_engine_barrier()


def setup(nc, c, loads, clears, beta_col):
    sc = Scope(nc, "setup")
    loaded = sc.sem("loaded")
    zero_ready = sc.sem("zero_ready")
    cleared = sc.sem("cleared")
    shift_ready = sc.sem("shift_ready")
    lead_ready = sc.sem("lead_ready")
    with nc.Block() as block:
        @block.sync
        def _(sp):
            sp.wait_ge(zero_ready, 1)
            piece = P * c["zero"].shape[1]
            n = 0
            for part in clears:
                flat = part.rearrange("r c -> (r c)")
                for at in range(0, flat.shape[0], piece):
                    size = min(piece, flat.shape[0] - at)
                    sp.dma_start(flat[at:at + size].rearrange("(p f) -> p f", p=P),
                                 c["zero"][:, 0:size // P]).then_inc(cleared, 16)
                    n += 1
            sp.wait_ge(cleared, 16 * n)

        @block.scalar
        def _(act):
            for dst, src in loads:
                act.dma_start(dst, src).then_inc(loaded, 16)
            act.wait_ge(loaded, 16 * len(loads))
            act.wait_ge(lead_ready, 1)
            nc.scalar.activation(c["w_self"][:, :], c["lead"][:, :], ACT.Exp)

        @block.vector
        def _(dve):
            nc.vector.memset(c["zero"][:, :], 0.0).then_inc(zero_ready, 1)
            nc.vector.memset(c["ln_eps"][:, :], LN_EPS)
            dve.wait_ge(loaded, 16 * len(loads))
            nc.vector.tensor_scalar_max(c["shift"][:, :], beta_col[:, :], 0.0).then_inc(shift_ready, 1)
            dve.wait_ge(shift_ready, 1)
            nc.vector.tensor_tensor(c["lead"][:, :], beta_col[:, :], c["shift"][:, :],
                                    ALU.subtract).then_inc(lead_ready, 1)
    sc.close()


class Keys:

    def __init__(self, sc, which):
        self.which = which
        self.ticks = sc.ticks
        self.idx = sc.sb("idx", [P, 2, 2 * T], int32)
        self.row = sc.sb("row", [P, 2, W], int32)
        self.same = sc.sb("same", [P, 2, T, P])
        self.junk = sc.sb("junk", [P, 2, T, P])
        self.earlier = sc.sb("earlier", [P, 2, T])
        self.away = sc.sb("away", [P, 2, T])
        self.moved = sc.sb("moved", [P, 2, T])
        self.target = sc.sb("target", [P, 2, T], int32)
        self.idx_in = sc.sem2("idx_in")
        self.row_in = sc.sem2("row_in")
        self.same_ready = sc.sem("same_ready")
        self.earlier_ready = sc.sem("earlier_ready")
        self.away_ready = sc.sem("away_ready")
        self.moved_ready = sc.sem("moved_ready")
        self.saved = sc.sem("saved")
        self.target_ready = sc.sem("target_ready")

    def key(self, s, j):
        at = j if self.which == "src" else T + j
        return self.idx[:, s, at:at + 1]

    def keys(self, s):
        at = 0 if self.which == "src" else T
        return self.idx[:, s, at:at + T]


def index_loads(sp, K, g, k, s, idx_d, row_d):
    sp.dma_start(K.idx[:, s, :], block_of(idx_d, g)).then_inc(K.idx_in[s], 16)
    sp.dma_start(K.row[:, s, :], row_d[bass.ds(g, 1), :].partition_broadcast(P)
                 .rearrange("p o f -> p (o f)")).then_inc(K.row_in[s], 16)


def index_work(nc, dve, K, c, g, k, s, summed, targets_all, make):
    dve.wait_ge(K.idx_in[s], 16 * (k + 1))
    dve.wait_ge(K.row_in[s], 16 * (k + 1))
    if past(g, 2):
        dve.wait_ge(summed, g - 1)
    for j in range(T):
        last = nc.vector.tensor_scalar(K.same[:, s, j, :], K.row[:, s, j * P:(j + 1) * P], K.key(s, j), None,
                                       ALU.is_equal)
    last.then_inc(K.same_ready, 1)
    if not make:
        return
    dve.wait_ge(K.same_ready, g + 1)
    for j in range(T):
        last = nc.vector.tensor_tensor_reduce(
            out=K.junk[:, s, j, :], in0=K.same[:, s, j, :], in1=c["below"][:, :], scale=1.0, scalar=0.0,
            op0=ALU.mult, op1=ALU.add, accum_out=K.earlier[:, s, j:j + 1])
    last.then_inc(K.earlier_ready, 1)
    nc.vector.tensor_scalar(K.away[:, s, :], K.keys(s), -1.0, c["spare"][:, :], ALU.mult,
                            ALU.add).then_inc(K.away_ready, 1)
    dve.wait_ge(K.earlier_ready, g + 1)
    dve.wait_ge(K.away_ready, g + 1)
    nc.vector.scalar_tensor_tensor(K.moved[:, s, :], K.earlier[:, s, :], 0.0, K.away[:, s, :], ALU.is_gt,
                                   ALU.mult).then_inc(K.moved_ready, 1)
    dve.wait_ge(K.moved_ready, g + 1)
    nc.vector.tensor_tensor(targets_all[:, bass.ds(T * g, T)], K.moved[:, s, :], K.keys(s),
                            ALU.add).then_inc(K.saved, 1)


def stage_targets(nc, dve, K, g, s, targets_all, added, make):
    if make:
        dve.wait_ge(K.saved, g + 1)
    if past(g, 2):
        dve.wait_ge(added, 16 * T * (g - 1))
    nc.vector.tensor_scalar(K.target[:, s, :], targets_all[:, bass.ds(T * g, T)], 0.0, None,
                            ALU.add).then_inc(K.target_ready, 1)


def add_rows(pool, K, table, out, out_ready, added, g, s, j):
    chained = not isinstance(g, int) or T * g + j > 0
    if j == 0:
        pool.wait_ge(K.target_ready, g + 1)
        pool.wait_ge(out_ready, g + 1)
    if chained:
        pool.wait_ge(added, 16 * (T * g + j))
        pool.sem_inc(K.ticks, 1)
    pool.indirect_dma_start(table[:, :], bass.IndirectOffsetOnAxis(ap=K.target[:, s, j:j + 1], axis=0),
                            out[:, s, j, :], None, compute_op=ALU.add).then_inc(added, 16)


def edge_pool(pool, K, groups, gathers, free, table, out, out_ready, added):
    def step(g, k, s):
        pool.wait_ge(K.idx_in[s], 16 * (k + 1))
        if past(g, 2):
            free(g)
            pool.sem_inc(K.ticks, 1)
        for j in range(T):
            for source, rows, at, landed in gathers:
                pool.indirect_dma_start(rows[:, s, j, :], None, source[:, :],
                                        bass.IndirectOffsetOnAxis(ap=K.idx[:, s, at + j:at + j + 1], axis=0)
                                        ).then_inc(landed[s], 16)
            if past(g, 2):
                add_rows(pool, K, table, out, out_ready, added, g - 2, s, j)

    sweep(pool, groups, step)
    for g in (groups - 2, groups - 1):
        for j in range(T):
            add_rows(pool, K, table, out, out_ready, added, g, g % 2, j)
    pool.wait_ge(added, 16 * T * groups)


def edges_attention(nc, c, x, idx_d, row_d, table, groups, targets_all, clears):
    sc = Scope(nc, "att")
    K = Keys(sc, "src")
    x_src = sc.sb("x_src", [P, 2, T, D])
    x_dst = sc.sb("x_dst", [P, 2, T, D])
    h = sc.sb("h", [P, 2, 2 * T, D])
    stats = sc.sb("stats", [P, 2, 2 * T, 6])
    mom = sc.sb("mom", [P, 2, 2 * T, 2])
    std = sc.sb("std", [P, 2, 2 * T])
    inv = sc.sb("inv", [P, 2, 2 * T])
    off = sc.sb("off", [P, 2, 2 * T])
    sq = sc.sb("sq", [P, 2, 2 * T])
    sq_junk = sc.sb("sq_junk", [P, 2, 2 * T, D])
    dot_junk = sc.sb("dot_junk", [P, 2, T, D])
    dot = sc.sb("dot", [P, 2, T])
    norm2 = sc.sb("norm2", [P, 2, T])
    norm = sc.sb("norm", [P, 2, T])
    rnorm = sc.sb("rnorm", [P, 2, T])
    cos = sc.sb("cos", [P, 2, T])
    score = sc.sb("score", [P, 2, T])
    val = sc.sb("val", [P, 2, T, A0])
    out = sc.sb("out", [P, 2, T, A0])
    sums = [sc.ps(f"sums{s}", [P, T, 256]) for s in range(2)]
    src_in, dst_in = sc.sem2("src_in"), sc.sem2("dst_in")
    cleared = sc.sem("cleared")
    ones_ready = sc.sem("ones_ready")
    stats_ready, mom_ready, std_ready = sc.sem("stats_ready"), sc.sem("mom_ready"), sc.sem("std_ready")
    inv_ready, off_ready = sc.sem("inv_ready"), sc.sem("off_ready")
    h_ready, sq_ready, dot_ready = sc.sem("h_ready"), sc.sem("sq_ready"), sc.sem("dot_ready")
    norm2_ready, norm_ready, rnorm_ready = sc.sem("norm2_ready"), sc.sem("norm_ready"), sc.sem("rnorm_ready")
    cos_ready, score_ready = sc.sem("cos_ready"), sc.sem("score_ready")
    weight_ready, val_ready = sc.sem("weight_ready"), sc.sem("val_ready")
    summed, out_ready, added = sc.sem("summed"), sc.sem("out_ready"), sc.sem("added")

    with nc.Block() as block:
        @block.sync
        def _(sp):
            def step(g, k, s):
                if past(g, 2):
                    sp.wait_ge(src_in[s], 16 * T * k)
                    sp.wait_ge(dst_in[s], 16 * T * k)
                    sp.wait_ge(K.same_ready, g - 1)
                    sp.wait_ge(K.saved, g - 1)
                    sp.sem_inc(sc.ticks, 1)
                index_loads(sp, K, g, k, s, idx_d, row_d)
                for view in clears:
                    sp.dma_start(block_of(view, g), c["zero"][:, 0:view.shape[2]]).then_inc(cleared, 16)
            sweep(sp, groups, step)
            sp.wait_ge(cleared, 16 * groups * len(clears))

        @block.gpsimd
        def _(pool):
            def free(g):
                pool.wait_ge(mom_ready, g - 1)
                pool.wait_ge(h_ready, g - 1)
            edge_pool(pool, K, groups, [(x, x_src, 0, src_in), (x, x_dst, T, dst_in)], free, table, out,
                      out_ready, added)

        @block.vector
        def _(dve):
            for s in range(2):
                last = nc.vector.memset(val[:, s, :, D + 1:D + 2], 1.0)
            last.then_inc(ones_ready, 1)

            def back(g, s):
                dve.wait_ge(h_ready, g + 1)
                for j in range(T):
                    last = nc.vector.tensor_tensor_reduce(
                        out=dot_junk[:, s, j, :], in0=h[:, s, j, :], in1=h[:, s, T + j, :], scale=1.0, scalar=0.0,
                        op0=ALU.mult, op1=ALU.add, accum_out=dot[:, s, j:j + 1])
                last.then_inc(dot_ready, 1)
                dve.wait_ge(sq_ready, g + 1)
                nc.vector.tensor_tensor(norm2[:, s, :], sq[:, s, 0:T], sq[:, s, T:2 * T],
                                        ALU.mult).then_inc(norm2_ready, 1)

            def scores(g, s):
                dve.wait_ge(norm_ready, g + 1)
                nc.vector.reciprocal(rnorm[:, s, :], norm[:, s, :]).then_inc(rnorm_ready, 1)
                dve.wait_ge(rnorm_ready, g + 1)
                dve.wait_ge(dot_ready, g + 1)
                nc.vector.tensor_tensor(cos[:, s, :], dot[:, s, :], rnorm[:, s, :], ALU.mult).then_inc(cos_ready, 1)
                dve.wait_ge(cos_ready, g + 1)
                nc.vector.tensor_scalar(score[:, s, :], cos[:, s, :], c["beta"][:, :], c["shift"][:, :],
                                        ALU.mult, ALU.subtract).then_inc(score_ready, 1)

            def step(g, k, s):
                if past(g, 1):
                    back(g - 1, 1 - s)
                dve.wait_ge(src_in[s], 16 * T * (k + 1))
                dve.wait_ge(dst_in[s], 16 * T * (k + 1))
                for j in range(T):
                    nc.vector.bn_stats(stats[:, s, j, :], x_src[:, s, j, :])
                    last = nc.vector.bn_stats(stats[:, s, T + j, :], x_dst[:, s, j, :])
                last.then_inc(stats_ready, 1)
                dve.wait_ge(stats_ready, g + 1)
                dve.sem_inc(sc.ticks, 1)
                for j in range(2 * T):
                    last = nc.vector.bn_aggr(mom[:, s, j, :], stats[:, s, j, :])
                last.then_inc(mom_ready, 1)
                index_work(nc, dve, K, c, g, k, s, summed, targets_all, True)
                if past(g, 1):
                    stage_targets(nc, dve, K, g - 1, 1 - s, targets_all, added, True)
                dve.wait_ge(std_ready, g + 1)
                nc.vector.reciprocal(inv[:, s, :], std[:, s, :]).then_inc(inv_ready, 1)
                dve.wait_ge(inv_ready, g + 1)
                nc.vector.scalar_tensor_tensor(off[:, s, :], mom[:, s, :, 0], -1.0, inv[:, s, :], ALU.mult,
                                               ALU.mult).then_inc(off_ready, 1)
                if past(g, 1):
                    scores(g - 1, 1 - s)
            sweep(dve, groups, step)
            stage_targets(nc, dve, K, groups - 1, (groups - 1) % 2, targets_all, added, True)
            back(groups - 1, (groups - 1) % 2)
            scores(groups - 1, (groups - 1) % 2)

        @block.scalar
        def _(act):
            act.wait_ge(ones_ready, 1)

            def norms(g, s):
                act.wait_ge(norm2_ready, g + 1)
                nc.scalar.activation(norm[:, s, :], norm2[:, s, :], ACT.Sqrt).then_inc(norm_ready, 1)

            def weights(g, s):
                act.wait_ge(score_ready, g + 1)
                if past(g, 2):
                    act.wait_ge(summed, g - 1)
                nc.scalar.activation(val[:, s, :, D], score[:, s, :], ACT.Exp).then_inc(weight_ready, 1)
                act.wait_ge(weight_ready, g + 1)
                for j in range(T):
                    last = nc.scalar.activation(val[:, s, j, 0:D], h[:, s, T + j, :], ACT.Copy,
                                                scale=val[:, s, j, D:D + 1])
                last.then_inc(val_ready, 1)

            def sums_out(g, s):
                act.wait_ge(summed, g + 1)
                if past(g, 2):
                    act.wait_ge(added, 16 * T * (g - 1))
                nc.scalar.activation(out[:, s, :, :], sums[s][:, :, 0:A0], ACT.Copy).then_inc(out_ready, 1)

            def step(g, k, s):
                if past(g, 2):
                    sums_out(g - 2, s)
                act.wait_ge(mom_ready, g + 1)
                nc.scalar.activation(std[:, s, :], mom[:, s, :, 1], ACT.Sqrt,
                                     bias=c["ln_eps"][:, :]).then_inc(std_ready, 1)
                if past(g, 1):
                    norms(g - 1, 1 - s)
                act.wait_ge(off_ready, g + 1)
                if past(g, 2):
                    act.wait_ge(dot_ready, g - 1)
                for j in range(T):
                    nc.scalar.activation(h[:, s, j, :], x_src[:, s, j, :], ACT.Relu,
                                         scale=inv[:, s, j:j + 1], bias=off[:, s, j:j + 1])
                    last = nc.scalar.activation(h[:, s, T + j, :], x_dst[:, s, j, :], ACT.Relu,
                                                scale=inv[:, s, T + j:T + j + 1], bias=off[:, s, T + j:T + j + 1])
                last.then_inc(h_ready, 1)
                act.wait_ge(h_ready, g + 1)
                for j in range(2 * T):
                    last = nc.scalar.activation(sq_junk[:, s, j, :], h[:, s, j, :], ACT.Square,
                                                accum_out=sq[:, s, j:j + 1])
                last.then_inc(sq_ready, 1)
                if past(g, 1):
                    weights(g - 1, 1 - s)
            sweep(act, groups, step)
            sums_out(groups - 2, (groups - 2) % 2)
            norms(groups - 1, (groups - 1) % 2)
            weights(groups - 1, (groups - 1) % 2)
            sums_out(groups - 1, (groups - 1) % 2)

        @block.tensor
        def _(pe):
            def step(g, k, s):
                pe.wait_ge(K.same_ready, g + 1)
                pe.wait_ge(val_ready, g + 1)
                if past(g, 2):
                    pe.wait_ge(out_ready, g - 1)
                for j in range(T):
                    last = nc.tensor.matmul(sums[s][:, j, 0:A0], K.same[:, s, j, :], val[:, s, j, :],
                                            start=True, stop=True)
                last.then_inc(summed, 1)
            sweep(pe, groups, step)
    sc.close()


def nodes_attention(nc, c, x_v, agg_v, x1_v, groups, isq_all, mom_all):
    sc = Scope(nc, "natt")
    x = sc.sb("x", [P, 2, T, D])
    agg = sc.sb("agg", [P, 2, T, A0])
    h = sc.sb("h", [P, 2, T, D])
    num = sc.sb("num", [P, 2, T, D])
    x1 = sc.sb("x1", [P, 2, T, D])
    stats = sc.sb("stats", [P, 2, T, 6])
    stats1 = sc.sb("stats1", [P, 2, T, 6])
    mom = sc.sb("mom", [P, 2, T, 2])
    mom1 = sc.sb("mom1", [P, 2, T, 2])
    std = sc.sb("std", [P, 2, T])
    inv = sc.sb("inv", [P, 2, T])
    off = sc.sb("off", [P, 2, T])
    den = sc.sb("den", [P, 2, T])
    rden = sc.sb("rden", [P, 2, T])
    sdeg = sc.sb("sdeg", [P, 2, T])
    isq = sc.sb("isq", [P, 2, T])
    x_in, agg_in, x1_out = sc.sem2("x_in"), sc.sem2("agg_in"), sc.sem2("x1_out")
    stats_ready, mom_ready, std_ready = sc.sem("stats_ready"), sc.sem("mom_ready"), sc.sem("std_ready")
    inv_ready, off_ready, h_ready = sc.sem("inv_ready"), sc.sem("off_ready"), sc.sem("h_ready")
    den_ready, rden_ready, num_ready = sc.sem("den_ready"), sc.sem("rden_ready"), sc.sem("num_ready")
    sdeg_ready, isq_ready, kept = sc.sem("sdeg_ready"), sc.sem("isq_ready"), sc.sem("kept")
    x1_ready, stats1_ready, mom1_ready = sc.sem("x1_ready"), sc.sem("stats1_ready"), sc.sem("mom1_ready")
    with nc.Block() as block:
        @block.sync
        def _(sp):
            def step(g, k, s):
                if past(g, 2):
                    sp.wait_ge(x1_ready, g - 1)
                    sp.wait_ge(sdeg_ready, g - 1)
                    sp.wait_ge(num_ready, g - 1)
                    sp.sem_inc(sc.ticks, 1)
                sp.dma_start(x[:, s, :, :].rearrange("p t d -> p (t d)"), block_of(x_v, g)).then_inc(x_in[s], 16)
                sp.dma_start(agg[:, s, :, :].rearrange("p t d -> p (t d)"), block_of(agg_v, g)).then_inc(agg_in[s], 16)
            sweep(sp, groups, step)

        @block.gpsimd
        def _(pool):
            def step(g, k, s):
                pool.wait_ge(x1_ready, g + 1)
                pool.dma_start(block_of(x1_v, g), x1[:, s, :, :].rearrange("p t d -> p (t d)")).then_inc(x1_out[s], 16)
            sweep(pool, groups, step)
            for s in range(2):
                pool.wait_ge(x1_out[s], 16 * ((groups + 1 - s) // 2))

        @block.vector
        def _(dve):
            def back(g, k, s):
                dve.wait_ge(h_ready, g + 1)
                nc.vector.scalar_tensor_tensor(num[:, s, :, :], h[:, s, :, :], c["w_self"][:, :],
                                               agg[:, s, :, 0:D], ALU.mult, ALU.add).then_inc(num_ready, 1)
                dve.wait_ge(num_ready, g + 1)
                dve.wait_ge(rden_ready, g + 1)
                if past(g, 2):
                    dve.wait_ge(x1_out[s], 16 * k)
                for j in range(T):
                    last = nc.vector.scalar_tensor_tensor(x1[:, s, j, :], num[:, s, j, :], rden[:, s, j:j + 1],
                                                          x[:, s, j, :], ALU.mult, ALU.add)
                last.then_inc(x1_ready, 1)
                dve.wait_ge(x1_ready, g + 1)
                for j in range(T):
                    last = nc.vector.bn_stats(stats1[:, s, j, :], x1[:, s, j, :])
                last.then_inc(stats1_ready, 1)
                dve.wait_ge(stats1_ready, g + 1)
                dve.sem_inc(sc.ticks, 1)
                for j in range(T):
                    last = nc.vector.bn_aggr(mom1[:, s, j, :], stats1[:, s, j, :])
                last.then_inc(mom1_ready, 1)
                dve.wait_ge(mom1_ready, g + 1)
                nc.vector.tensor_scalar(mom_all[:, bass.ds(T * g, T), :], mom1[:, s, :, :], 0.0, None,
                                        ALU.add).then_inc(kept, 1)

            def step(g, k, s):
                dve.wait_ge(x_in[s], 16 * (k + 1))
                for j in range(T):
                    last = nc.vector.bn_stats(stats[:, s, j, :], x[:, s, j, :])
                last.then_inc(stats_ready, 1)
                dve.wait_ge(stats_ready, g + 1)
                dve.sem_inc(sc.ticks, 1)
                for j in range(T):
                    last = nc.vector.bn_aggr(mom[:, s, j, :], stats[:, s, j, :])
                last.then_inc(mom_ready, 1)
                dve.wait_ge(agg_in[s], 16 * (k + 1))
                nc.vector.tensor_scalar(den[:, s, :], agg[:, s, :, D], c["w_self"][:, :], None,
                                        ALU.add).then_inc(den_ready, 1)
                dve.wait_ge(den_ready, g + 1)
                nc.vector.reciprocal(rden[:, s, :], den[:, s, :]).then_inc(rden_ready, 1)
                dve.wait_ge(std_ready, g + 1)
                nc.vector.reciprocal(inv[:, s, :], std[:, s, :]).then_inc(inv_ready, 1)
                dve.wait_ge(inv_ready, g + 1)
                nc.vector.scalar_tensor_tensor(off[:, s, :], mom[:, s, :, 0], -1.0, inv[:, s, :], ALU.mult,
                                               ALU.mult).then_inc(off_ready, 1)
                dve.wait_ge(sdeg_ready, g + 1)
                nc.vector.reciprocal(isq[:, s, :], sdeg[:, s, :]).then_inc(isq_ready, 1)
                dve.wait_ge(isq_ready, g + 1)
                nc.vector.tensor_scalar(isq_all[:, bass.ds(T * g, T)], isq[:, s, :], 0.0, None,
                                        ALU.add).then_inc(kept, 1)
                if past(g, 1):
                    back(g - 1, k - 1 + s, 1 - s)
            sweep(dve, groups, step)
            back(groups - 1, (groups - 1) // 2, (groups - 1) % 2)

        @block.scalar
        def _(act):
            def step(g, k, s):
                act.wait_ge(mom_ready, g + 1)
                nc.scalar.activation(std[:, s, :], mom[:, s, :, 1], ACT.Sqrt,
                                     bias=c["ln_eps"][:, :]).then_inc(std_ready, 1)
                act.wait_ge(agg_in[s], 16 * (k + 1))
                if past(g, 2):
                    act.wait_ge(isq_ready, g - 1)
                nc.scalar.activation(sdeg[:, s, :], agg[:, s, :, D + 1], ACT.Sqrt, bias=c["one"][:, :]
                                     ).then_inc(sdeg_ready, 1)
                act.wait_ge(off_ready, g + 1)
                if past(g, 2):
                    act.wait_ge(num_ready, g - 1)
                for j in range(T):
                    last = nc.scalar.activation(h[:, s, j, :], x[:, s, j, :], ACT.Relu,
                                                scale=inv[:, s, j:j + 1], bias=off[:, s, j:j + 1])
                last.then_inc(h_ready, 1)
            sweep(act, groups, step)
    sc.close()


def ln_of_all(nc, c, layer, mom_all, inv_all, off_all):
    sc = Scope(nc, f"ln{layer}")
    std_ready, inv_ready = sc.sem("std_ready"), sc.sem("inv_ready")
    with nc.Block() as block:
        @block.scalar
        def _(act):
            nc.scalar.activation(off_all[:, :], mom_all[:, :, 1], ACT.Sqrt,
                                 bias=c["ln_eps"][:, :]).then_inc(std_ready, 1)

        @block.vector
        def _(dve):
            dve.wait_ge(std_ready, 1)
            nc.vector.reciprocal(inv_all[:, :], off_all[:, :]).then_inc(inv_ready, 1)
            dve.wait_ge(inv_ready, 1)
            nc.vector.scalar_tensor_tensor(off_all[:, :], mom_all[:, :, 0], -1.0, inv_all[:, :], ALU.mult,
                                           ALU.mult)
    sc.close()


def edges_message(nc, c, x, idx_d, row_d, attr_d, table, groups, targets_all, layer):
    two = layer == 2
    DE = D64 if two else D4
    C = FC if two else 1
    if two:
        w_src, w_dst, w_attr, w_out = c["cw1_src"], c["cw1_dst"], c["cw1_attr"], c["cw2"]
        b_hidden, b_out = c["cb1"], c["cb2_row"]
    else:
        w_src, w_dst, w_attr, w_out = c["m1_src"], c["m1_dst"], c["m1_attr"], c["m2"]
        b_hidden, b_out = c["mb1"], c["mb2_row"]
    sc = Scope(nc, f"msg{layer}")
    K = Keys(sc, "dst")
    x_src = sc.sb("x_src", [P, 2, T, D])
    x_dst = sc.sb("x_dst", [P, 2, T, D])
    attr = sc.sb("attr", [DE, 2, W])
    stats = sc.sb("stats", [P, 2, 2 * T, 6])
    mom = sc.sb("mom", [P, 2, 2 * T, 2])
    std = sc.sb("std", [P, 2, 2 * T])
    inv = sc.sb("inv", [P, 2, 2 * T])
    off = sc.sb("off", [P, 2, 2 * T])
    u = sc.sb("u", [P, 2, 2 * T, D])
    if two:
        h = sc.sb("h", [P, 2, 2 * T, D])
        pre = sc.sb("pre", [P, C, W])
        pre_ready = sc.sem("pre_ready")
        stats_b = sc.sb("stats_b", [P, 2, 2 * T, 6])
        mom_b = sc.sb("mom_b", [P, 2, 2 * T, 2])
        std_b = sc.sb("std_b", [P, 2, 2 * T])
        inv_b = sc.sb("inv_b", [P, 2, 2 * T])
        off_b = sc.sb("off_b", [P, 2, 2 * T])
        h_ready, stats_b_ready, mom_b_ready = sc.sem("h_ready"), sc.sem("stats_b_ready"), sc.sem("mom_b_ready")
        std_b_ready, inv_b_ready, off_b_ready = sc.sem("std_b_ready"), sc.sem("inv_b_ready"), sc.sem("off_b_ready")
    src_t = sc.sb("src_t", [P, 2, W])
    dst_t = sc.sb("dst_t", [P, 2, W])
    hid = sc.sb("hid", [P, 2, C, W])
    msg = sc.sb("msg", [P, 2, T, D])
    out = sc.sb("out", [P, 2, T, D])
    p_src = sc.ps("p_src", [P, W])
    p_dst = sc.ps("p_dst", [P, W])
    p_hid = [sc.ps(f"p_hid{i}", [P, W]) for i in range(C)]
    p_msg = sc.ps("p_msg", [P, T, D])
    p_sum = sc.ps("p_sum", [P, T, D])
    attr_in, src_in, dst_in = sc.sem2("attr_in"), sc.sem2("src_in"), sc.sem2("dst_in")
    stats_ready, mom_ready, std_ready = sc.sem("stats_ready"), sc.sem("mom_ready"), sc.sem("std_ready")
    inv_ready, off_ready, u_ready = sc.sem("inv_ready"), sc.sem("off_ready"), sc.sem("u_ready")
    flipped, src_t_ready, dst_t_ready = sc.sem("flipped"), sc.sem("src_t_ready"), sc.sem("dst_t_ready")
    hid_made, hid_ready = sc.sem("hid_made"), sc.sem("hid_ready")
    msg_made, msg_ready = sc.sem("msg_made"), sc.sem("msg_ready")
    summed, out_ready, added = sc.sem("summed"), sc.sem("out_ready"), sc.sem("added")

    with nc.Block() as block:
        @block.sync
        def _(sp):
            def step(g, k, s):
                if past(g, 2):
                    sp.wait_ge(hid_made, C * (g - 1))
                    sp.sem_inc(sc.ticks, 1)
                    sp.wait_ge(src_in[s], 16 * T * k)
                    sp.wait_ge(dst_in[s], 16 * T * k)
                    sp.wait_ge(K.same_ready, g - 1)
                    if not two:
                        sp.wait_ge(K.saved, g - 1)
                    sp.sem_inc(sc.ticks, 1)
                index_loads(sp, K, g, k, s, idx_d, row_d)
                sp.dma_start(attr[:, s, :], block_of(attr_d, g)).then_inc(attr_in[s], 16)
            sweep(sp, groups, step)

        @block.gpsimd
        def _(pool):
            def free(g):
                pool.wait_ge(mom_ready, g - 1)
                pool.wait_ge(h_ready if two else u_ready, g - 1)
            edge_pool(pool, K, groups, [(x, x_src, 0, src_in), (x, x_dst, T, dst_in)], free, table, out,
                      out_ready, added)

        @block.vector
        def _(dve):
            def moments(g, s, rows_of, stats, stats_ready, mom, mom_ready):
                for j in range(2 * T):
                    last = nc.vector.bn_stats(stats[:, s, j, :], rows_of(s, j))
                last.then_inc(stats_ready, 1)
                dve.wait_ge(stats_ready, g + 1)
                dve.sem_inc(sc.ticks, 1)
                for j in range(2 * T):
                    last = nc.vector.bn_aggr(mom[:, s, j, :], stats[:, s, j, :])
                last.then_inc(mom_ready, 1)

            def affine(g, s, std, std_ready, inv, inv_ready, mom, off, off_ready):
                dve.wait_ge(std_ready, g + 1)
                nc.vector.reciprocal(inv[:, s, :], std[:, s, :]).then_inc(inv_ready, 1)
                dve.wait_ge(inv_ready, g + 1)
                nc.vector.scalar_tensor_tensor(off[:, s, :], mom[:, s, :, 0], -1.0, inv[:, s, :], ALU.mult,
                                               ALU.mult).then_inc(off_ready, 1)

            def gathered(s, j):
                return x_src[:, s, j, :] if j < T else x_dst[:, s, j - T, :]

            def leak(g, s):
                if past(g, 2):
                    dve.wait_ge(msg_made, g - 1)
                for i in range(C):
                    dve.wait_ge(pre_ready, C * g + i + 1)
                    nc.vector.scalar_tensor_tensor(hid[:, s, i, :], pre[:, i, :], SLOPE, pre[:, i, :], ALU.mult,
                                                   ALU.max).then_inc(hid_ready, 1)

            def step(g, k, s):
                if two and past(g, 1):
                    leak(g - 1, 1 - s)
                dve.wait_ge(src_in[s], 16 * T * (k + 1))
                dve.wait_ge(dst_in[s], 16 * T * (k + 1))
                moments(g, s, gathered, stats, stats_ready, mom, mom_ready)
                index_work(nc, dve, K, c, g, k, s, summed, targets_all, not two)
                if past(g, 1):
                    stage_targets(nc, dve, K, g - 1, 1 - s, targets_all, added, not two)
                affine(g, s, std, std_ready, inv, inv_ready, mom, off, off_ready)
                if past(g, 2):
                    dve.wait_ge(flipped, g - 1)
                if two:
                    dve.wait_ge(h_ready, g + 1)
                    moments(g, s, lambda s, j: h[:, s, j, :], stats_b, stats_b_ready, mom_b, mom_b_ready)
                    affine(g, s, std_b, std_b_ready, inv_b, inv_b_ready, mom_b, off_b, off_b_ready)
                    dve.wait_ge(off_b_ready, g + 1)
                    for j in range(2 * T):
                        last = nc.vector.tensor_scalar(u[:, s, j, :], h[:, s, j, :], inv_b[:, s, j:j + 1],
                                                       off_b[:, s, j:j + 1], ALU.mult, ALU.add)
                    last.then_inc(u_ready, 1)
                else:
                    dve.wait_ge(off_ready, g + 1)
                    for j in range(2 * T):
                        last = nc.vector.tensor_scalar(u[:, s, j, :], gathered(s, j), inv[:, s, j:j + 1],
                                                       off[:, s, j:j + 1], ALU.mult, ALU.add)
                    last.then_inc(u_ready, 1)
                    dve.wait_ge(flipped, g + 1)
                    if past(g, 2):
                        dve.wait_ge(hid_made, C * (g - 1))
                    nc.vector.tensor_scalar_max(src_t[:, s, :], p_src[:, :], 0.0).then_inc(src_t_ready, 1)
                if past(g, 1):
                    messages(g - 1, 1 - s)

            def messages(g, s):
                dve.wait_ge(msg_made, g + 1)
                if past(g, 2):
                    dve.wait_ge(summed, g - 1)
                nc.vector.tensor_tensor(msg[:, s, :, :], p_msg[:, :, :], b_out[:, :, :],
                                        ALU.add).then_inc(msg_ready, 1)
            sweep(dve, groups, step)
            stage_targets(nc, dve, K, groups - 1, (groups - 1) % 2, targets_all, added, not two)
            if two:
                leak(groups - 1, (groups - 1) % 2)
            messages(groups - 1, (groups - 1) % 2)

        @block.scalar
        def _(act):
            def sums_out(g, s):
                act.wait_ge(summed, g + 1)
                if past(g, 2):
                    act.wait_ge(added, 16 * T * (g - 1))
                nc.scalar.activation(out[:, s, :, :], p_sum[:, :, :], ACT.Copy).then_inc(out_ready, 1)

            def step(g, k, s):
                act.wait_ge(mom_ready, g + 1)
                nc.scalar.activation(std[:, s, :], mom[:, s, :, 1], ACT.Sqrt,
                                     bias=c["ln_eps"][:, :]).then_inc(std_ready, 1)
                if two:
                    act.wait_ge(off_ready, g + 1)
                    if past(g, 2):
                        act.wait_ge(u_ready, g - 1)
                    for j in range(2 * T):
                        rows = x_src[:, s, j, :] if j < T else x_dst[:, s, j - T, :]
                        last = nc.scalar.activation(h[:, s, j, :], rows, ACT.Relu, scale=inv[:, s, j:j + 1],
                                                    bias=off[:, s, j:j + 1])
                    last.then_inc(h_ready, 1)
                    act.wait_ge(mom_b_ready, g + 1)
                    nc.scalar.activation(std_b[:, s, :], mom_b[:, s, :, 1], ACT.Sqrt,
                                         bias=c["ln_eps"][:, :]).then_inc(std_b_ready, 1)
                act.wait_ge(flipped, g + 1)
                if past(g, 2):
                    act.wait_ge(hid_made, C * (g - 1))
                if two:
                    nc.scalar.activation(src_t[:, s, :], p_src[:, :], ACT.Identity, scale=c["ln1_g"][:, :],
                                         bias=c["ln1_b"][:, :]).then_inc(src_t_ready, 1)
                    nc.scalar.activation(dst_t[:, s, :], p_dst[:, :], ACT.Identity, scale=c["ln1_g"][:, :],
                                         bias=c["ln1_b"][:, :]).then_inc(dst_t_ready, 1)
                else:
                    nc.scalar.activation(dst_t[:, s, :], p_dst[:, :], ACT.Relu).then_inc(dst_t_ready, 1)
                if past(g, 1):
                    sums_out(g - 1, 1 - s)
                if past(g, 2) and not two:
                    act.wait_ge(msg_made, g - 1)
                for i in range(C):
                    act.wait_ge(hid_made, C * g + i + 1)
                    if two:
                        if past(g, 1):
                            act.wait_ge(hid_ready, C * g)
                        nc.scalar.activation(pre[:, i, :], p_hid[i][:, :], ACT.Identity,
                                             bias=b_hidden[:, i:i + 1]).then_inc(pre_ready, 1)
                    else:
                        nc.scalar.activation(hid[:, s, i, :], p_hid[i][:, :], ACT.Relu,
                                             bias=b_hidden[:, i:i + 1]).then_inc(hid_ready, 1)
            sweep(act, groups, step)
            sums_out(groups - 1, (groups - 1) % 2)

        @block.tensor
        def _(pe):
            def to_messages(g, s):
                pe.wait_ge(hid_ready, C * (g + 1))
                if past(g, 1):
                    pe.wait_ge(msg_ready, g)
                for j in range(T):
                    for i in range(C):
                        last = nc.tensor.matmul(p_msg[:, j, :], hid[:, s, i, j * P:(j + 1) * P], w_out[:, i, :],
                                                start=(i == 0), stop=(i == C - 1))
                last.then_inc(msg_made, 1)

            def sum_equal(g, s):
                pe.wait_ge(msg_ready, g + 1)
                pe.wait_ge(K.same_ready, g + 1)
                if past(g, 1):
                    pe.wait_ge(out_ready, g)
                for j in range(T):
                    last = nc.tensor.matmul(p_sum[:, j, :], K.same[:, s, j, :], msg[:, s, j, :], start=True,
                                            stop=True)
                last.then_inc(summed, 1)

            def step(g, k, s):
                if two and past(g, 1):
                    to_messages(g - 1, 1 - s)
                pe.wait_ge(u_ready, g + 1)
                if past(g, 1):
                    pe.wait_ge(src_t_ready, g)
                    pe.wait_ge(dst_t_ready, g)
                for j in range(T):
                    nc.tensor.transpose(p_src[:, j * P:(j + 1) * P], u[:, s, j, :], c["ident"][:, :])
                    last = nc.tensor.transpose(p_dst[:, j * P:(j + 1) * P], u[:, s, T + j, :], c["ident"][:, :])
                last.then_inc(flipped, 1)
                if not two and past(g, 1):
                    to_messages(g - 1, 1 - s)
                pe.wait_ge(src_t_ready, g + 1)
                pe.wait_ge(dst_t_ready, g + 1)
                pe.wait_ge(attr_in[s], 16 * (k + 1))
                if past(g, 1):
                    pe.wait_ge(pre_ready if two else hid_ready, C * g)
                for i in range(C):
                    cols = slice(i * D, (i + 1) * D)
                    nc.tensor.matmul(p_hid[i][:, :], w_src[:, cols], src_t[:, s, :], start=True, stop=False)
                    nc.tensor.matmul(p_hid[i][:, :], w_dst[:, cols], dst_t[:, s, :], start=False, stop=False)
                    nc.tensor.matmul(p_hid[i][:, :], w_attr[:, cols], attr[:, s, :], start=False,
                                     stop=True).then_inc(hid_made, 1)
                if past(g, 1):
                    sum_equal(g - 1, 1 - s)
            sweep(pe, groups, step)
            to_messages(groups - 1, (groups - 1) % 2)
            sum_equal(groups - 1, (groups - 1) % 2)
    sc.close()


def nodes_gated(nc, c, x1_v, agg_v, x2_v, groups, inv_all, off_all, mom_all):
    sc = Scope(nc, "gru")
    x = sc.sb("x", [P, 3, T, D])
    agg = sc.sb("agg", [P, 2, T, D])
    ln = sc.sb("ln", [P, 2, 2, T])
    u = sc.sb("u", [P, 2, T, D])
    h_t = sc.sb("h_t", [P, 2, W])
    a_t = sc.sb("a_t", [P, 2, W])
    z = sc.sb("z", [P, 2, W])
    r = sc.sb("r", [P, 2, W])
    rh = sc.sb("rh", [P, 2, W])
    cand = sc.sb("cand", [P, 2, W])
    step_t = sc.sb("step_t", [P, 2, W])
    gated = sc.sb("gated", [P, 2, W])
    o_t = sc.sb("o_t", [P, 2, W])
    x2 = sc.sb("x2", [P, 2, T, D])
    stats = sc.sb("stats", [P, 2, T, 6])
    mom = sc.sb("mom", [P, 2, T, 2])
    p_h, p_a, p_z, p_r, p_c = (sc.ps(n, [P, W]) for n in ("p_h", "p_a", "p_z", "p_r", "p_c"))
    p_o = sc.ps("p_o", [P, T, D])
    x_in, agg_in, x2_out = sc.sem2("x_in"), sc.sem2("agg_in"), sc.sem2("x2_out")
    ln_ready, u_ready, flipped = sc.sem("ln_ready"), sc.sem("u_ready"), sc.sem("flipped")
    h_t_ready, a_t_ready = sc.sem("h_t_ready"), sc.sem("a_t_ready")
    r_made, r_ready, z_made, z_ready = sc.sem("r_made"), sc.sem("r_ready"), sc.sem("z_made"), sc.sem("z_ready")
    rh_ready, c_made, c_ready = sc.sem("rh_ready"), sc.sem("c_made"), sc.sem("c_ready")
    step_ready, gated_ready, o_t_ready = sc.sem("step_ready"), sc.sem("gated_ready"), sc.sem("o_t_ready")
    back_made, x2_ready = sc.sem("back_made"), sc.sem("x2_ready")
    stats_ready, mom_ready, kept = sc.sem("stats_ready"), sc.sem("mom_ready"), sc.sem("kept")
    with nc.Block() as block:
        @block.sync
        def _(sp):
            def step(g, k, s):
                if past(g, 2):
                    sp.wait_ge(x2_ready, g - 1)
                    sp.wait_ge(flipped, g - 1)
                    sp.sem_inc(sc.ticks, 1)
                sp.dma_start(x[:, s, :, :].rearrange("p t d -> p (t d)"), block_of(x1_v, g)).then_inc(x_in[s], 16)
                sp.dma_start(agg[:, s, :, :].rearrange("p t d -> p (t d)"), block_of(agg_v, g)).then_inc(agg_in[s], 16)
            sweep(sp, groups, step)

        @block.gpsimd
        def _(pool):
            def blend(g, s):
                pool.wait_ge(c_ready, g + 1)
                nc.gpsimd.tensor_tensor(step_t[:, s, :], cand[:, s, :], h_t[:, s, :],
                                        ALU.subtract).then_inc(step_ready, 1)
                pool.wait_ge(step_ready, g + 1)
                pool.wait_ge(z_ready, g + 1)
                if past(g, 2):
                    pool.wait_ge(o_t_ready, g - 1)
                nc.gpsimd.tensor_tensor(gated[:, s, :], z[:, s, :], step_t[:, s, :],
                                        ALU.mult).then_inc(gated_ready, 1)

            def store(g, s):
                pool.wait_ge(x2_ready, g + 1)
                pool.dma_start(block_of(x2_v, g), x2[:, s, :, :].rearrange("p t d -> p (t d)")).then_inc(x2_out[s], 16)

            def step(g, k, s):
                blend(g, s)
                if past(g, 1):
                    store(g - 1, 1 - s)
            sweep(pool, groups, step)
            store(groups - 1, (groups - 1) % 2)
            for s in range(2):
                pool.wait_ge(x2_out[s], 16 * ((groups + 1 - s) // 2))

        @block.vector
        def _(dve):
            def back(g, k, s):
                dve.wait_ge(gated_ready, g + 1)
                if past(g, 2):
                    dve.wait_ge(back_made, g - 1)
                nc.vector.tensor_tensor(o_t[:, s, :], gated[:, s, :], h_t[:, s, :], ALU.add).then_inc(o_t_ready, 1)

            def finish(g, k, s):
                dve.wait_ge(back_made, g + 1)
                if past(g, 2):
                    dve.wait_ge(x2_out[s], 16 * k)
                nc.vector.tensor_tensor(x2[:, s, :, :], p_o[:, :, :], x[:, s, :, :], ALU.add).then_inc(x2_ready, 1)
                dve.wait_ge(x2_ready, g + 1)
                for j in range(T):
                    last = nc.vector.bn_stats(stats[:, s, j, :], x2[:, s, j, :])
                last.then_inc(stats_ready, 1)
                dve.wait_ge(stats_ready, g + 1)
                dve.sem_inc(sc.ticks, 1)
                for j in range(T):
                    last = nc.vector.bn_aggr(mom[:, s, j, :], stats[:, s, j, :])
                last.then_inc(mom_ready, 1)
                dve.wait_ge(mom_ready, g + 1)
                nc.vector.tensor_scalar(mom_all[:, bass.ds(T * g, T), :], mom[:, s, :, :], 0.0, None,
                                        ALU.add).then_inc(kept, 1)

            def step(g, k, s):
                nc.vector.tensor_scalar(ln[:, s, 0, :], inv_all[:, bass.ds(T * g, T)], 0.0, None, ALU.add)
                nc.vector.tensor_scalar(ln[:, s, 1, :], off_all[:, bass.ds(T * g, T)], 0.0, None,
                                        ALU.add).then_inc(ln_ready, 1)
                dve.wait_ge(ln_ready, g + 1)
                dve.wait_ge(x_in[s], 16 * (k + 1))
                if past(g, 2):
                    dve.wait_ge(flipped, g - 1)
                for j in range(T):
                    last = nc.vector.tensor_scalar(u[:, s, j, :], x[:, s, j, :], ln[:, s, 0, j:j + 1],
                                                   ln[:, s, 1, j:j + 1], ALU.mult, ALU.add)
                last.then_inc(u_ready, 1)
                dve.wait_ge(flipped, g + 1)
                nc.vector.tensor_scalar_max(h_t[:, s, :], p_h[:, :], 0.0).then_inc(h_t_ready, 1)
                if past(g, 1):
                    back(g - 1, k - 1 + s, 1 - s)
                dve.wait_ge(r_ready, g + 1)
                dve.wait_ge(h_t_ready, g + 1)
                if past(g, 2):
                    dve.wait_ge(c_made, g - 1)
                nc.vector.tensor_tensor(rh[:, s, :], r[:, s, :], h_t[:, s, :], ALU.mult).then_inc(rh_ready, 1)
                if past(g, 1):
                    finish(g - 1, k - 1 + s, 1 - s)
            sweep(dve, groups, step)
            back(groups - 1, (groups - 1) // 2, (groups - 1) % 2)
            finish(groups - 1, (groups - 1) // 2, (groups - 1) % 2)

        @block.scalar
        def _(act):
            def candidate(g, s):
                act.wait_ge(c_made, g + 1)
                if past(g, 2):
                    act.wait_ge(step_ready, g - 1)
                nc.scalar.activation(cand[:, s, :], p_c[:, :], ACT.Tanh, bias=c["gb_h"][:, :]).then_inc(c_ready, 1)

            def step(g, k, s):
                act.wait_ge(flipped, g + 1)
                if past(g, 2):
                    act.wait_ge(c_made, g - 1)
                nc.scalar.activation(a_t[:, s, :], p_a[:, :], ACT.Copy).then_inc(a_t_ready, 1)
                if past(g, 1):
                    candidate(g - 1, 1 - s)
                act.wait_ge(r_made, g + 1)
                if past(g, 2):
                    act.wait_ge(rh_ready, g - 1)
                nc.scalar.activation(r[:, s, :], p_r[:, :], ACT.Sigmoid, bias=c["gb_r"][:, :]).then_inc(r_ready, 1)
                act.wait_ge(z_made, g + 1)
                if past(g, 2):
                    act.wait_ge(gated_ready, g - 1)
                nc.scalar.activation(z[:, s, :], p_z[:, :], ACT.Sigmoid, bias=c["gb_z"][:, :]).then_inc(z_ready, 1)
            sweep(act, groups, step)
            candidate(groups - 1, (groups - 1) % 2)

        @block.tensor
        def _(pe):
            def candidate(g, s):
                pe.wait_ge(rh_ready, g + 1)
                if past(g, 1):
                    pe.wait_ge(c_ready, g)
                nc.tensor.matmul(p_c[:, :], c["gw_h"][:, 1, :], a_t[:, s, :], start=True, stop=False)
                nc.tensor.matmul(p_c[:, :], c["gw_h"][:, 0, :], rh[:, s, :], start=False,
                                 stop=True).then_inc(c_made, 1)

            def turn_back(g, s):
                pe.wait_ge(o_t_ready, g + 1)
                if past(g, 1):
                    pe.wait_ge(x2_ready, g)
                for j in range(T):
                    last = nc.tensor.transpose(p_o[:, j, :], o_t[:, s, j * P:(j + 1) * P], c["ident"][:, :])
                last.then_inc(back_made, 1)

            def step(g, k, s):
                pe.wait_ge(u_ready, g + 1)
                pe.wait_ge(agg_in[s], 16 * (k + 1))
                if past(g, 1):
                    pe.wait_ge(h_t_ready, g)
                    pe.wait_ge(a_t_ready, g)
                for j in range(T):
                    nc.tensor.transpose(p_h[:, j * P:(j + 1) * P], u[:, s, j, :], c["ident"][:, :])
                    last = nc.tensor.transpose(p_a[:, j * P:(j + 1) * P], agg[:, s, j, :], c["ident"][:, :])
                last.then_inc(flipped, 1)
                if past(g, 1):
                    candidate(g - 1, 1 - s)
                pe.wait_ge(h_t_ready, g + 1)
                pe.wait_ge(a_t_ready, g + 1)
                if past(g, 1):
                    pe.wait_ge(r_ready, g)
                    pe.wait_ge(z_ready, g)
                nc.tensor.matmul(p_r[:, :], c["gw_r"][:, 0, :], h_t[:, s, :], start=True, stop=False)
                nc.tensor.matmul(p_r[:, :], c["gw_r"][:, 1, :], a_t[:, s, :], start=False,
                                 stop=True).then_inc(r_made, 1)
                nc.tensor.matmul(p_z[:, :], c["gw_z"][:, 0, :], h_t[:, s, :], start=True, stop=False)
                nc.tensor.matmul(p_z[:, :], c["gw_z"][:, 1, :], a_t[:, s, :], start=False,
                                 stop=True).then_inc(z_made, 1)
                if past(g, 1):
                    turn_back(g - 1, 1 - s)
            sweep(pe, groups, step)
            candidate(groups - 1, (groups - 1) % 2)
            turn_back(groups - 1, (groups - 1) % 2)
    sc.close()


def nodes_feedforward(nc, c, x2_v, agg_v, x3_v, groups, inv_all, off_all, isq_all):
    sc = Scope(nc, "ff")
    x = sc.sb("x", [P, 2, T, D])
    agg = sc.sb("agg", [P, 2, T, D])
    ln = sc.sb("ln", [P, 2, 3, T])
    h = sc.sb("h", [P, 2, T, D])
    y = sc.sb("y", [P, 2, T, D])
    stats = sc.sb("stats", [P, 2, T, 6])
    mom = sc.sb("mom", [P, 2, T, 2])
    std = sc.sb("std", [P, 2, T])
    inv = sc.sb("inv", [P, 2, T])
    off = sc.sb("off", [P, 2, T])
    u = sc.sb("u", [P, 2, T, D])
    u_t = sc.sb("u_t", [P, 2, W])
    pre = sc.sb("pre", [P, FC, W])
    hid = sc.sb("hid", [P, 2, FC, W])
    rest = sc.sb("rest", [P, 3, T, D])
    rest_b = sc.sb("rest_b", [P, 2, T, D])
    x3 = sc.sb("x3", [P, 2, T, X3])
    p_t = sc.ps("p_t", [P, W])
    p_hid = [sc.ps(f"p_hid{i}", [P, W]) for i in range(FC)]
    p_o = [sc.ps(f"p_o{s}", [P, T, D]) for s in range(2)]
    x_in, agg_in, x3_out = sc.sem2("x_in"), sc.sem2("agg_in"), sc.sem2("x3_out")
    ln_ready, h_ready, y_ready = sc.sem("ln_ready"), sc.sem("h_ready"), sc.sem("y_ready")
    stats_ready, mom_ready, std_ready = sc.sem("stats_ready"), sc.sem("mom_ready"), sc.sem("std_ready")
    inv_ready, off_ready, u_ready = sc.sem("inv_ready"), sc.sem("off_ready"), sc.sem("u_ready")
    flipped, u_t_ready = sc.sem("flipped"), sc.sem("u_t_ready")
    hid_made, pre_ready, hid_ready = sc.sem("hid_made"), sc.sem("pre_ready"), sc.sem("hid_ready")
    rest_ready, rest_b_ready, out_made, x3_ready = (sc.sem("rest_ready"), sc.sem("rest_b_ready"),
                                                    sc.sem("out_made"), sc.sem("x3_ready"))
    with nc.Block() as block:
        @block.sync
        def _(sp):
            def step(g, k, s):
                if past(g, 2):
                    sp.wait_ge(rest_ready, g - 1)
                    sp.wait_ge(h_ready, g - 1)
                    sp.wait_ge(y_ready, g - 1)
                    sp.sem_inc(sc.ticks, 1)
                sp.dma_start(x[:, s, :, :].rearrange("p t d -> p (t d)"), block_of(x2_v, g)).then_inc(x_in[s], 16)
                sp.dma_start(agg[:, s, :, :].rearrange("p t d -> p (t d)"), block_of(agg_v, g)).then_inc(agg_in[s], 16)
            sweep(sp, groups, step)

        @block.gpsimd
        def _(pool):
            def store(g, s):
                pool.wait_ge(x3_ready, g + 1)
                pool.dma_start(block_of(x3_v, g), x3[:, s, :, :].rearrange("p t d -> p (t d)")).then_inc(x3_out[s], 16)

            def step(g, k, s):
                pool.wait_ge(x_in[s], 16 * (k + 1))
                if past(g, 2):
                    pool.wait_ge(rest_b_ready, g - 1)
                pool.wait_ge(y_ready, g + 1)
                nc.gpsimd.tensor_tensor(rest[:, s, :, :], x[:, s, :, :], y[:, s, :, :],
                                        ALU.add).then_inc(rest_ready, 1)
                pool.wait_ge(rest_ready, g + 1)
                if past(g, 2):
                    pool.wait_ge(x3_ready, g - 1)
                nc.gpsimd.tensor_tensor(rest_b[:, s, :, :], rest[:, s, :, :], c["fb2_row"][:, :, :],
                                        ALU.add).then_inc(rest_b_ready, 1)
                if past(g, 2):
                    store(g - 2, s)
            sweep(pool, groups, step)
            store(groups - 2, (groups - 2) % 2)
            store(groups - 1, (groups - 1) % 2)
            for s in range(2):
                pool.wait_ge(x3_out[s], 16 * ((groups + 1 - s) // 2))

        @block.vector
        def _(dve):
            def finish(g, k, s):
                dve.wait_ge(out_made, g + 1)
                dve.wait_ge(rest_b_ready, g + 1)
                if past(g, 2):
                    dve.wait_ge(x3_out[s], 16 * k)
                nc.vector.tensor_scalar(x3[:, s, :, D], isq_all[:, bass.ds(T * g, T)], 0.0, None, ALU.add)
                nc.vector.tensor_tensor(x3[:, s, :, 0:D], p_o[s][:, :, :], rest_b[:, s, :, :],
                                        ALU.add).then_inc(x3_ready, 1)

            def step(g, k, s):
                if past(g, 2):
                    dve.wait_ge(h_ready, g - 1)
                nc.vector.tensor_scalar(ln[:, s, 0, :], inv_all[:, bass.ds(T * g, T)], 0.0, None, ALU.add)
                nc.vector.tensor_scalar(ln[:, s, 1, :], off_all[:, bass.ds(T * g, T)], 0.0, None,
                                        ALU.add).then_inc(ln_ready, 1)
                if past(g, 2):
                    finish(g - 2, k - 1, s)
                dve.wait_ge(h_ready, g + 1)
                dve.wait_ge(agg_in[s], 16 * (k + 1))
                if past(g, 2):
                    dve.wait_ge(rest_ready, g - 1)
                nc.vector.tensor_tensor(y[:, s, :, :], h[:, s, :, :], agg[:, s, :, :], ALU.add).then_inc(y_ready, 1)
                dve.wait_ge(y_ready, g + 1)
                for j in range(T):
                    last = nc.vector.bn_stats(stats[:, s, j, :], y[:, s, j, :])
                last.then_inc(stats_ready, 1)
                dve.wait_ge(stats_ready, g + 1)
                dve.sem_inc(sc.ticks, 1)
                for j in range(T):
                    last = nc.vector.bn_aggr(mom[:, s, j, :], stats[:, s, j, :])
                last.then_inc(mom_ready, 1)
                dve.wait_ge(std_ready, g + 1)
                nc.vector.reciprocal(inv[:, s, :], std[:, s, :]).then_inc(inv_ready, 1)
                dve.wait_ge(inv_ready, g + 1)
                nc.vector.scalar_tensor_tensor(off[:, s, :], mom[:, s, :, 0], -1.0, inv[:, s, :], ALU.mult,
                                               ALU.mult).then_inc(off_ready, 1)
                dve.wait_ge(off_ready, g + 1)
                if past(g, 2):
                    dve.wait_ge(flipped, g - 1)
                for j in range(T):
                    last = nc.vector.tensor_scalar(u[:, s, j, :], y[:, s, j, :], inv[:, s, j:j + 1],
                                                   off[:, s, j:j + 1], ALU.mult, ALU.add)
                last.then_inc(u_ready, 1)
                if past(g, 1):
                    leak(g - 1, 1 - s)

            def leak(g, s):
                if past(g, 2):
                    dve.wait_ge(out_made, g - 1)
                for i in range(FC):
                    dve.wait_ge(pre_ready, FC * g + i + 1)
                    nc.vector.scalar_tensor_tensor(hid[:, s, i, :], pre[:, i, :], SLOPE, pre[:, i, :], ALU.mult,
                                                   ALU.max).then_inc(hid_ready, 1)
            sweep(dve, groups, step)
            leak(groups - 1, (groups - 1) % 2)
            for g in (groups - 2, groups - 1):
                finish(g, g // 2, g % 2)

        @block.scalar
        def _(act):
            def flip_out(g, s):
                act.wait_ge(flipped, g + 1)
                if past(g, 2):
                    act.wait_ge(hid_made, FC * (g - 1))
                nc.scalar.activation(u_t[:, s, :], p_t[:, :], ACT.Identity, scale=c["ln2_g"][:, :],
                                     bias=c["ln2_b"][:, :]).then_inc(u_t_ready, 1)

            def hidden(g, s):
                if past(g, 1):
                    act.wait_ge(hid_ready, FC * g)
                for i in range(FC):
                    act.wait_ge(hid_made, FC * g + i + 1)
                    nc.scalar.activation(pre[:, i, :], p_hid[i][:, :], ACT.Identity,
                                         bias=c["fb1"][:, i:i + 1]).then_inc(pre_ready, 1)

            def step(g, k, s):
                act.wait_ge(ln_ready, g + 1)
                act.wait_ge(x_in[s], 16 * (k + 1))
                if past(g, 2):
                    act.wait_ge(y_ready, g - 1)
                for j in range(T):
                    last = nc.scalar.activation(h[:, s, j, :], x[:, s, j, :], ACT.Relu, scale=ln[:, s, 0, j:j + 1],
                                                bias=ln[:, s, 1, j:j + 1])
                last.then_inc(h_ready, 1)
                if past(g, 1):
                    flip_out(g - 1, 1 - s)
                act.wait_ge(mom_ready, g + 1)
                nc.scalar.activation(std[:, s, :], mom[:, s, :, 1], ACT.Sqrt,
                                     bias=c["ln_eps"][:, :]).then_inc(std_ready, 1)
                if past(g, 1):
                    hidden(g - 1, 1 - s)
            sweep(act, groups, step)
            flip_out(groups - 1, (groups - 1) % 2)
            hidden(groups - 1, (groups - 1) % 2)

        @block.tensor
        def _(pe):
            def outputs(g, s):
                pe.wait_ge(hid_ready, FC * (g + 1))
                if past(g, 2):
                    pe.wait_ge(x3_ready, g - 1)
                for j in range(T):
                    for i in range(FC):
                        last = nc.tensor.matmul(p_o[s][:, j, :], hid[:, s, i, j * P:(j + 1) * P], c["fw2"][:, i, :],
                                                start=(i == 0), stop=(i == FC - 1))
                last.then_inc(out_made, 1)

            def step(g, k, s):
                pe.wait_ge(u_ready, g + 1)
                if past(g, 1):
                    pe.wait_ge(u_t_ready, g)
                for j in range(T):
                    last = nc.tensor.transpose(p_t[:, j * P:(j + 1) * P], u[:, s, j, :], c["ident"][:, :])
                last.then_inc(flipped, 1)
                if past(g, 1):
                    outputs(g - 1, 1 - s)
                pe.wait_ge(u_t_ready, g + 1)
                if past(g, 1):
                    pe.wait_ge(pre_ready, FC * g)
                for i in range(FC):
                    nc.tensor.matmul(p_hid[i][:, :], c["fw1"][:, i * D:(i + 1) * D], u_t[:, s, :], start=True,
                                     stop=True).then_inc(hid_made, 1)
            sweep(pe, groups, step)
            outputs(groups - 1, (groups - 1) % 2)
    sc.close()


def edges_convolution(nc, c, x3, idx_d, row_d, table, groups, targets_all):
    sc = Scope(nc, "conv")
    K = Keys(sc, "src")
    x_dst = sc.sb("x_dst", [P, 2, T, X3])
    stats = sc.sb("stats", [P, 2, T, 6])
    mom = sc.sb("mom", [P, 2, T, 2])
    std = sc.sb("std", [P, 2, T])
    inv = sc.sb("inv", [P, 2, T])
    scale = sc.sb("scale", [P, 2, T])
    off = sc.sb("off", [P, 2, T])
    val = sc.sb("val", [P, 2, T, D])
    out = sc.sb("out", [P, 2, T, D])
    sums = [sc.ps(f"sums{s}", [P, T, D]) for s in range(2)]
    dst_in = sc.sem2("dst_in")
    stats_ready, mom_ready, std_ready = sc.sem("stats_ready"), sc.sem("mom_ready"), sc.sem("std_ready")
    inv_ready, scale_ready, off_ready = sc.sem("inv_ready"), sc.sem("scale_ready"), sc.sem("off_ready")
    val_ready, summed, out_ready, added = (sc.sem("val_ready"), sc.sem("summed"), sc.sem("out_ready"),
                                           sc.sem("added"))
    with nc.Block() as block:
        @block.sync
        def _(sp):
            def step(g, k, s):
                if past(g, 2):
                    sp.wait_ge(dst_in[s], 16 * T * k)
                    sp.wait_ge(K.same_ready, g - 1)
                    sp.sem_inc(sc.ticks, 1)
                index_loads(sp, K, g, k, s, idx_d, row_d)
            sweep(sp, groups, step)

        @block.gpsimd
        def _(pool):
            def free(g):
                pool.wait_ge(scale_ready, g - 1)
                pool.wait_ge(val_ready, g - 1)
            edge_pool(pool, K, groups, [(x3, x_dst, T, dst_in)], free, table, out, out_ready, added)

        @block.vector
        def _(dve):
            def step(g, k, s):
                dve.wait_ge(dst_in[s], 16 * T * (k + 1))
                for j in range(T):
                    last = nc.vector.bn_stats(stats[:, s, j, :], x_dst[:, s, j, 0:D])
                last.then_inc(stats_ready, 1)
                dve.wait_ge(stats_ready, g + 1)
                dve.sem_inc(sc.ticks, 1)
                for j in range(T):
                    last = nc.vector.bn_aggr(mom[:, s, j, :], stats[:, s, j, :])
                last.then_inc(mom_ready, 1)
                index_work(nc, dve, K, c, g, k, s, summed, targets_all, False)
                if past(g, 1):
                    stage_targets(nc, dve, K, g - 1, 1 - s, targets_all, added, False)
                dve.wait_ge(std_ready, g + 1)
                nc.vector.reciprocal(inv[:, s, :], std[:, s, :]).then_inc(inv_ready, 1)
                dve.wait_ge(inv_ready, g + 1)
                nc.vector.tensor_tensor(scale[:, s, :], inv[:, s, :], x_dst[:, s, :, D], ALU.mult
                                        ).then_inc(scale_ready, 1)
                dve.wait_ge(scale_ready, g + 1)
                nc.vector.scalar_tensor_tensor(off[:, s, :], mom[:, s, :, 0], -1.0, scale[:, s, :], ALU.mult,
                                               ALU.mult).then_inc(off_ready, 1)
            sweep(dve, groups, step)
            stage_targets(nc, dve, K, groups - 1, (groups - 1) % 2, targets_all, added, False)

        @block.scalar
        def _(act):
            def sums_out(g, s):
                act.wait_ge(summed, g + 1)
                if past(g, 2):
                    act.wait_ge(added, 16 * T * (g - 1))
                nc.scalar.activation(out[:, s, :, :], sums[s][:, :, :], ACT.Copy).then_inc(out_ready, 1)

            def step(g, k, s):
                act.wait_ge(mom_ready, g + 1)
                nc.scalar.activation(std[:, s, :], mom[:, s, :, 1], ACT.Sqrt,
                                     bias=c["ln_eps"][:, :]).then_inc(std_ready, 1)
                if past(g, 1):
                    sums_out(g - 1, 1 - s)
                act.wait_ge(off_ready, g + 1)
                if past(g, 2):
                    act.wait_ge(summed, g - 1)
                for j in range(T):
                    last = nc.scalar.activation(val[:, s, j, :], x_dst[:, s, j, 0:D], ACT.Relu,
                                                scale=scale[:, s, j:j + 1], bias=off[:, s, j:j + 1])
                last.then_inc(val_ready, 1)
            sweep(act, groups, step)
            sums_out(groups - 1, (groups - 1) % 2)

        @block.tensor
        def _(pe):
            def step(g, k, s):
                pe.wait_ge(K.same_ready, g + 1)
                pe.wait_ge(val_ready, g + 1)
                if past(g, 2):
                    pe.wait_ge(out_ready, g - 1)
                for j in range(T):
                    last = nc.tensor.matmul(sums[s][:, j, :], K.same[:, s, j, :], val[:, s, j, :], start=True,
                                            stop=True)
                last.then_inc(summed, 1)
            sweep(pe, groups, step)
    sc.close()


def nodes_convolution(nc, c, x3_v, agg_v, out_v, groups):
    sc = Scope(nc, "nconv")
    x = sc.sb("x", [P, 3, T, X3])
    agg = sc.sb("agg", [P, 2, T, D])
    stats = sc.sb("stats", [P, 2, T, 6])
    mom = sc.sb("mom", [P, 2, T, 2])
    std = sc.sb("std", [P, 2, T])
    inv = sc.sb("inv", [P, 2, T])
    scale = sc.sb("scale", [P, 2, T])
    off = sc.sb("off", [P, 2, T])
    own = sc.sb("own", [P, 2, T, D])
    both = sc.sb("both", [P, 2, T, D])
    both_t = sc.sb("both_t", [P, 2, W])
    res = sc.sb("res", [P, 2, T, D])
    p_t = [sc.ps(f"p_t{s}", [P, W]) for s in range(2)]
    p_o = [sc.ps(f"p_o{s}", [P, T, D]) for s in range(2)]
    x_in, agg_in, res_out = sc.sem2("x_in"), sc.sem2("agg_in"), sc.sem2("res_out")
    stats_ready, mom_ready, std_ready = sc.sem("stats_ready"), sc.sem("mom_ready"), sc.sem("std_ready")
    inv_ready, scale_ready, off_ready = sc.sem("inv_ready"), sc.sem("scale_ready"), sc.sem("off_ready")
    own_ready, both_ready, flipped = sc.sem("own_ready"), sc.sem("both_ready"), sc.sem("flipped")
    both_t_ready, out_made, res_ready = sc.sem("both_t_ready"), sc.sem("out_made"), sc.sem("res_ready")
    with nc.Block() as block:
        @block.sync
        def _(sp):
            def step(g, k, s):
                if past(g, 2):
                    sp.wait_ge(res_ready, g - 1)
                    sp.sem_inc(sc.ticks, 1)
                sp.dma_start(x[:, s, :, :].rearrange("p t d -> p (t d)"), block_of(x3_v, g)).then_inc(x_in[s], 16)
                sp.dma_start(agg[:, s, :, :].rearrange("p t d -> p (t d)"), block_of(agg_v, g)).then_inc(agg_in[s], 16)
            sweep(sp, groups, step)

        @block.gpsimd
        def _(pool):
            def step(g, k, s):
                pool.wait_ge(res_ready, g + 1)
                pool.dma_start(block_of(out_v, g), res[:, s, :, :].rearrange("p t d -> p (t d)")).then_inc(res_out[s], 16)
            sweep(pool, groups, step)
            for s in range(2):
                pool.wait_ge(res_out[s], 16 * ((groups + 1 - s) // 2))

        @block.vector
        def _(dve):
            def back(g, k, s):
                dve.wait_ge(own_ready, g + 1)
                dve.wait_ge(agg_in[s], 16 * (k + 1))
                if past(g, 2):
                    dve.wait_ge(flipped, g - 1)
                nc.vector.tensor_tensor(both[:, s, :, :], agg[:, s, :, :], own[:, s, :, :],
                                        ALU.add).then_inc(both_ready, 1)

            def finish(g, k, s):
                dve.wait_ge(out_made, g + 1)
                if past(g, 2):
                    dve.wait_ge(res_out[s], 16 * k)
                for j in range(T):
                    last = nc.vector.scalar_tensor_tensor(res[:, s, j, :], p_o[s][:, j, :], x[:, s, j, D:D + 1],
                                                          x[:, s, j, 0:D], ALU.mult, ALU.add)
                last.then_inc(res_ready, 1)

            def step(g, k, s):
                dve.wait_ge(x_in[s], 16 * (k + 1))
                for j in range(T):
                    last = nc.vector.bn_stats(stats[:, s, j, :], x[:, s, j, 0:D])
                last.then_inc(stats_ready, 1)
                dve.wait_ge(stats_ready, g + 1)
                dve.sem_inc(sc.ticks, 1)
                for j in range(T):
                    last = nc.vector.bn_aggr(mom[:, s, j, :], stats[:, s, j, :])
                last.then_inc(mom_ready, 1)
                if past(g, 1):
                    finish(g - 1, k - 1 + s, 1 - s)
                dve.wait_ge(std_ready, g + 1)
                nc.vector.reciprocal(inv[:, s, :], std[:, s, :]).then_inc(inv_ready, 1)
                dve.wait_ge(inv_ready, g + 1)
                nc.vector.tensor_tensor(scale[:, s, :], inv[:, s, :], x[:, s, :, D], ALU.mult
                                        ).then_inc(scale_ready, 1)
                dve.wait_ge(scale_ready, g + 1)
                nc.vector.scalar_tensor_tensor(off[:, s, :], mom[:, s, :, 0], -1.0, scale[:, s, :], ALU.mult,
                                               ALU.mult).then_inc(off_ready, 1)
                back(g, k, s)
            sweep(dve, groups, step)
            finish(groups - 1, (groups - 1) // 2, (groups - 1) % 2)

        @block.scalar
        def _(act):
            def step(g, k, s):
                act.wait_ge(mom_ready, g + 1)
                nc.scalar.activation(std[:, s, :], mom[:, s, :, 1], ACT.Sqrt,
                                     bias=c["ln_eps"][:, :]).then_inc(std_ready, 1)
                act.wait_ge(off_ready, g + 1)
                if past(g, 2):
                    act.wait_ge(both_ready, g - 1)
                for j in range(T):
                    last = nc.scalar.activation(own[:, s, j, :], x[:, s, j, 0:D], ACT.Relu,
                                                scale=scale[:, s, j:j + 1], bias=off[:, s, j:j + 1])
                last.then_inc(own_ready, 1)
                act.wait_ge(flipped, g + 1)
                if past(g, 2):
                    act.wait_ge(out_made, g - 1)
                nc.scalar.activation(both_t[:, s, :], p_t[s][:, :], ACT.Copy).then_inc(both_t_ready, 1)
            sweep(act, groups, step)

        @block.tensor
        def _(pe):
            def step(g, k, s):
                pe.wait_ge(both_ready, g + 1)
                if past(g, 2):
                    pe.wait_ge(both_t_ready, g - 1)
                for j in range(T):
                    last = nc.tensor.transpose(p_t[s][:, j * P:(j + 1) * P], both[:, s, j, :], c["ident"][:, :])
                last.then_inc(flipped, 1)
                pe.wait_ge(both_t_ready, g + 1)
                if past(g, 2):
                    pe.wait_ge(res_ready, g - 1)
                for j in range(T):
                    last = nc.tensor.matmul(p_o[s][:, j, :], both_t[:, s, j * P:(j + 1) * P], c["w3"][:, :],
                                            start=True, stop=True)
                last.then_inc(out_made, 1)
            sweep(pe, groups, step)
    sc.close()


def build(nc, a):
    n_nodes, n_edges = a["x"].shape[0], a["idx"].shape[0] * W
    NG, EG = n_nodes // W, n_edges // W
    table_rows = n_nodes + P
    ctx = ExitStack()

    def sb(name, shape, dt=fp32):
        return ctx.enter_context(nc.sbuf_tensor(name, shape, dt))

    def dram(name, shape):
        return nc.dram_tensor(name, shape, fp32, kind="Internal").ap()

    def groups_of(t, rows):
        return t[0:rows, :].rearrange("(g p t) d -> g p (t d)", p=P, t=T)

    with ctx:
        agg0 = dram("agg0", (table_rows, A0))
        clear_rows = -(-n_nodes // EG // P) * P
        agg = [dram(f"agg{i}", (max(table_rows, clear_rows * EG), D)) for i in (1, 2, 3)]
        x1, x2, x3 = dram("x1", (n_nodes, D)), dram("x2", (n_nodes, D)), dram("x3", (n_nodes, X3))

        c = {}
        loads = []
        for name, shape, src in (
                ("ident", [P, P], a["ident"]), ("below", [P, P], a["below"]), ("spare", [P, 1], a["spare"]),
                ("one", [P, 1], a["one"]),
                ("beta", [P, 1], a["beta"].partition_broadcast(P)),
                ("m1_src", [P, D], a["m1"][0:D, :]), ("m1_dst", [P, D], a["m1"][D:2 * D, :]),
                ("m1_attr", [D4, D], a["m1"][2 * D:2 * D + D4, :]),
                ("mb1", [P, 1], a["mb1"]), ("mb2_row", [P, W], a["mb2_row"].partition_broadcast(P)),
                ("gb_z", [P, 1], a["gb_z"]), ("gb_r", [P, 1], a["gb_r"]), ("gb_h", [P, 1], a["gb_h"]),
                ("ln1_g", [P, 1], a["ln1_g"]), ("ln1_b", [P, 1], a["ln1_b"]),
                ("ln2_g", [P, 1], a["ln2_g"]), ("ln2_b", [P, 1], a["ln2_b"]),
                ("cw1_dst", [P, F], a["cw1"][0:D, :]), ("cw1_src", [P, F], a["cw1"][D:2 * D, :]),
                ("cw1_attr", [D64, F], a["cw1"][2 * D:2 * D + D64, :]),
                ("cb1", [P, FC], a["cb1"]), ("cb2_row", [P, W], a["cb2_row"].partition_broadcast(P)),
                ("fw1", [P, F], a["fw1"]), ("fb1", [P, FC], a["fb1"]),
                ("fb2_row", [P, W], a["fb2_row"].partition_broadcast(P)), ("w3", [P, D], a["w3"])):
            t = sb(name, shape)
            loads.append((t[:, :], src))
            c[name] = t
        for name, chunks, src in (("m2", 1, a["m2"]), ("gw_z", 2, a["gw_z"]), ("gw_r", 2, a["gw_r"]),
                                  ("gw_h", 2, a["gw_h"]), ("cw2", FC, a["cw2"]), ("fw2", FC, a["fw2"])):
            t = sb(name, [P, chunks, D])
            loads.append((t[:, :, :], src.rearrange("(c k) n -> k c n", k=P)))
            c[name] = t
        for name in ("mb2_row", "cb2_row", "fb2_row"):
            c[name] = c[name][:, :].rearrange("p (t d) -> p t d", t=T)
        c["zero"] = sb("zero", [P, clear_rows * D // P])
        for name in ("ln_eps", "shift", "lead", "w_self"):
            c[name] = sb(name, [P, 1])
        targets_src = sb("targets_src", [P, T * EG], int32)
        targets_dst = sb("targets_dst", [P, T * EG], int32)
        isq_all = sb("isq_all", [P, T * NG])
        mom_all = sb("mom_all", [P, T * NG, 2])
        inv_all = sb("inv_all", [P, T * NG])
        off_all = sb("off_all", [P, T * NG])

        beyond = clear_rows * EG
        setup(nc, c, loads, [agg0] + [t[beyond:, :] for t in agg if t.shape[0] > beyond], c["beta"])
        clears = [t[0:clear_rows * EG, :].rearrange("(g p r) d -> g p (r d)", g=EG, p=P) for t in agg]
        edges_attention(nc, c, a["x"], a["idx"], a["src_row"], agg0, EG, targets_src, clears)
        nodes_attention(nc, c, groups_of(a["x"], n_nodes), groups_of(agg0, n_nodes), groups_of(x1, n_nodes), NG,
                        isq_all, mom_all)
        ln_of_all(nc, c, 1, mom_all, inv_all, off_all)
        edges_message(nc, c, x1, a["idx"], a["dst_row"], a["attr4"], agg[0], EG, targets_dst, 1)
        nodes_gated(nc, c, groups_of(x1, n_nodes), groups_of(agg[0], n_nodes), groups_of(x2, n_nodes), NG,
                    inv_all, off_all, mom_all)
        ln_of_all(nc, c, 2, mom_all, inv_all, off_all)
        edges_message(nc, c, x2, a["idx"], a["dst_row"], a["attr64"], agg[1], EG, targets_dst, 2)
        nodes_feedforward(nc, c, groups_of(x2, n_nodes), groups_of(agg[1], n_nodes), groups_of(x3, n_nodes), NG,
                          inv_all, off_all, isq_all)
        edges_convolution(nc, c, x3, a["idx"], a["src_row"], agg[2], EG, targets_src)
        nodes_convolution(nc, c, groups_of(x3, n_nodes), groups_of(agg[2], n_nodes), groups_of(a["out"], n_nodes), NG)


def kernel(x, src, dst, edge_attr_4, edge_attr_64, L0_gnn_beta, L1_gnn_W_msg1, L1_gnn_b_msg1, L1_gnn_W_msg2,
           L1_gnn_b_msg2, L1_gnn_W_z, L1_gnn_b_z, L1_gnn_W_r, L1_gnn_b_r, L1_gnn_W_h, L1_gnn_b_h, L2_gnn_ln1_g,
           L2_gnn_ln1_b, L2_gnn_ln2_g, L2_gnn_ln2_b, L2_gnn_conv_w1, L2_gnn_conv_b1, L2_gnn_conv_w2,
           L2_gnn_conv_b2, L2_gnn_ff_w1, L2_gnn_ff_b1, L2_gnn_ff_w2, L2_gnn_ff_b2, L3_gnn_W):
    import numpy as np
    import concourse.bacc as bacc
    from concourse.bass_utils import run_bass_kernel_spmd

    x, src, dst = np.asarray(x), np.asarray(src), np.asarray(dst)
    N, E = x.shape[0], src.shape[0]
    extra_edges = -E % W
    extra_nodes = -N % W
    if extra_edges and not extra_nodes:
        extra_nodes = W
    own = (N + np.arange(extra_edges) % max(extra_nodes, 1)).astype(src.dtype)

    def more(v, n):
        return np.concatenate([v, v[:n]]) if n else v

    def column(v):
        return np.asarray(v).reshape(-1, D).T

    def row4(v):
        return np.tile(np.asarray(v), T)

    def edge_columns(v):
        v = more(np.asarray(v), extra_edges)
        return v.reshape(-1, W, v.shape[1]).transpose(0, 2, 1)

    xp = more(x, extra_nodes)
    src, dst = np.concatenate([src, own]), np.concatenate([dst, own])
    ends = np.stack([src.reshape(-1, T, P), dst.reshape(-1, T, P)], axis=1)
    arrays = {
        "x": xp, "idx": ends.transpose(0, 3, 1, 2).reshape(-1, P, 2 * T),
        "src_row": src.reshape(-1, W), "dst_row": dst.reshape(-1, W),
        "attr4": edge_columns(edge_attr_4), "attr64": edge_columns(edge_attr_64),
        "beta": np.asarray(L0_gnn_beta),
        "m1": L1_gnn_W_msg1, "mb1": column(L1_gnn_b_msg1), "m2": L1_gnn_W_msg2, "mb2_row": row4(L1_gnn_b_msg2),
        "gw_z": L1_gnn_W_z, "gw_r": L1_gnn_W_r, "gw_h": L1_gnn_W_h,
        "gb_z": column(L1_gnn_b_z), "gb_r": column(L1_gnn_b_r), "gb_h": column(L1_gnn_b_h),
        "ln1_g": column(L2_gnn_ln1_g), "ln1_b": column(L2_gnn_ln1_b),
        "ln2_g": column(L2_gnn_ln2_g), "ln2_b": column(L2_gnn_ln2_b),
        "cw1": L2_gnn_conv_w1, "cb1": column(L2_gnn_conv_b1), "cw2": L2_gnn_conv_w2, "cb2_row": row4(L2_gnn_conv_b2),
        "fw1": L2_gnn_ff_w1, "fb1": column(L2_gnn_ff_b1), "fw2": L2_gnn_ff_w2, "fb2_row": row4(L2_gnn_ff_b2),
        "w3": np.asarray(L3_gnn_W).T,
        "ident": np.eye(P, dtype=np.float32), "below": np.tril(np.ones((P, P), np.float32), -1),
        "spare": (xp.shape[0] + np.arange(P, dtype=np.float32)).reshape(P, 1), "one": np.ones((P, 1), np.float32),
    }
    nc = bacc.Bacc("TRN2", target_bir_lowering=False, num_devices=1)
    feeds, aps = {}, {}
    for name, v in arrays.items():
        v = np.ascontiguousarray(v)
        feeds[f"in_{name}"] = v
        aps[name] = nc.dram_tensor(f"in_{name}", v.shape, mybir.dt.from_np(v.dtype), kind="ExternalInput").ap()
    aps["out"] = nc.dram_tensor("out_rows", xp.shape, fp32, kind="ExternalOutput").ap()
    build(nc, aps)
    run = run_bass_kernel_spmd(nc, [feeds], core_ids=[0])
    return run.results[0]["out_rows"][:N]
```

```python
import concourse.bass as bass
from concourse import mybir
from contextlib import ExitStack


P = 128
T = 4
D = 128
W = T * P
F = 3 * D
FC = F // D
D4 = 4
D64 = 64
A0 = D + 2
X3 = D + 1
LN_EPS = 1e-5
SLOPE = 0.01
HEAD = 6
RING = 4

fp32 = mybir.dt.float32
int32 = mybir.dt.int32
ALU = mybir.AluOpType
ACT = mybir.ActivationFunctionType


def past(g, back):
    return not isinstance(g, int) or g >= back


def sweep(eng, groups, step, ring=2):
    head = -(-HEAD // ring)
    for g in range(ring * head):
        step(g, g // ring, g % ring)
    rounds = (groups - 1) // ring
    with eng.Fori(head, rounds) as k:
        for s in range(ring):
            step(ring * k + s, k, s)
    for g in range(ring * rounds, groups):
        step(g, g // ring, g % ring)


def before(k, s, n):
    return (k - 1 if s < n else k), (s - n) % RING


def after(k, s):
    return (k + 1 if s == RING - 1 else k), (s + 1) % RING


def ahead(g, groups):
    return not isinstance(g, int) or g + 1 < groups


def rounds_of(groups, s):
    return (groups + RING - 1 - s) // RING


def block_of(view, g):
    return view[bass.ds(g, 1), :, :].rearrange("o p f -> (o p) f")


class Scope:

    def __init__(self, nc, tag):
        self.nc, self.tag, self.ctx, self.sems = nc, tag, ExitStack(), []
        self.ticks = self.sem("ticks")

    def sb(self, name, shape, dt=fp32):
        return self.ctx.enter_context(self.nc.sbuf_tensor(f"{self.tag}_{name}", shape, dt))

    def ps(self, name, shape):
        return self.ctx.enter_context(self.nc.psum_tensor(f"{self.tag}_{name}", shape, fp32))

    def sem(self, name):
        s = self.nc.alloc_semaphore(f"{self.tag}_{name}")
        self.sems.append(s)
        return s

    def sem2(self, name, n=2):
        return [self.sem(f"{name}{s}") for s in range(n)]

    def close(self):
        self.ctx.close()
        self.nc.clear_and_free_semaphores(self.sems)
        self.nc.all_engine_barrier()


def setup(nc, c, loads, clears, beta_col):
    sc = Scope(nc, "setup")
    loaded = sc.sem("loaded")
    zero_ready = sc.sem("zero_ready")
    cleared = sc.sem("cleared")
    shift_ready = sc.sem("shift_ready")
    lead_ready = sc.sem("lead_ready")
    with nc.Block() as block:
        @block.sync
        def _(sp):
            sp.wait_ge(zero_ready, 1)
            piece = P * c["zero"].shape[1]
            n = 0
            for part in clears:
                flat = part.rearrange("r c -> (r c)")
                for at in range(0, flat.shape[0], piece):
                    size = min(piece, flat.shape[0] - at)
                    sp.dma_start(flat[at:at + size].rearrange("(p f) -> p f", p=P),
                                 c["zero"][:, 0:size // P]).then_inc(cleared, 16)
                    n += 1
            sp.wait_ge(cleared, 16 * n)

        @block.scalar
        def _(act):
            for dst, src in loads:
                act.dma_start(dst, src).then_inc(loaded, 16)
            act.wait_ge(loaded, 16 * len(loads))
            act.wait_ge(lead_ready, 1)
            nc.scalar.activation(c["w_self"][:, :], c["lead"][:, :], ACT.Exp)

        @block.vector
        def _(dve):
            nc.vector.memset(c["zero"][:, :], 0.0).then_inc(zero_ready, 1)
            nc.vector.memset(c["ln_eps"][:, :], LN_EPS)
            dve.wait_ge(loaded, 16 * len(loads))
            nc.vector.tensor_scalar_max(c["shift"][:, :], beta_col[:, :], 0.0).then_inc(shift_ready, 1)
            dve.wait_ge(shift_ready, 1)
            nc.vector.tensor_tensor(c["lead"][:, :], beta_col[:, :], c["shift"][:, :],
                                    ALU.subtract).then_inc(lead_ready, 1)
    sc.close()


class Keys:

    def __init__(self, sc, which):
        self.which = which
        self.ticks = sc.ticks
        self.idx = sc.sb("idx", [P, 2, 2 * T], int32)
        self.row = sc.sb("row", [P, 2, W], int32)
        self.same = sc.sb("same", [P, 2, T, P])
        self.junk = sc.sb("junk", [P, 2, T, P])
        self.earlier = sc.sb("earlier", [P, 2, T])
        self.away = sc.sb("away", [P, 2, T])
        self.moved = sc.sb("moved", [P, 2, T])
        self.target = sc.sb("target", [P, 2, T], int32)
        self.idx_in = sc.sem2("idx_in")
        self.row_in = sc.sem2("row_in")
        self.same_ready = sc.sem("same_ready")
        self.earlier_ready = sc.sem("earlier_ready")
        self.away_ready = sc.sem("away_ready")
        self.moved_ready = sc.sem("moved_ready")
        self.saved = sc.sem("saved")
        self.target_ready = sc.sem("target_ready")

    def key(self, s, j):
        at = j if self.which == "src" else T + j
        return self.idx[:, s, at:at + 1]

    def keys(self, s):
        at = 0 if self.which == "src" else T
        return self.idx[:, s, at:at + T]


def index_loads(sp, K, g, k, s, idx_d, row_d):
    sp.dma_start(K.idx[:, s, :], block_of(idx_d, g)).then_inc(K.idx_in[s], 16)
    sp.dma_start(K.row[:, s, :], row_d[bass.ds(g, 1), :].partition_broadcast(P)
                 .rearrange("p o f -> p (o f)")).then_inc(K.row_in[s], 16)


def index_work(nc, dve, K, c, g, k, s, summed, targets_all, make):
    dve.wait_ge(K.idx_in[s], 16 * (k + 1))
    dve.wait_ge(K.row_in[s], 16 * (k + 1))
    if past(g, 2):
        dve.wait_ge(summed, g - 1)
    for j in range(T):
        last = nc.vector.tensor_scalar(K.same[:, s, j, :], K.row[:, s, j * P:(j + 1) * P], K.key(s, j), None,
                                       ALU.is_equal)
    last.then_inc(K.same_ready, 1)
    if not make:
        return
    dve.wait_ge(K.same_ready, g + 1)
    for j in range(T):
        last = nc.vector.tensor_tensor_reduce(
            out=K.junk[:, s, j, :], in0=K.same[:, s, j, :], in1=c["below"][:, :], scale=1.0, scalar=0.0,
            op0=ALU.mult, op1=ALU.add, accum_out=K.earlier[:, s, j:j + 1])
    last.then_inc(K.earlier_ready, 1)
    nc.vector.tensor_scalar(K.away[:, s, :], K.keys(s), -1.0, c["spare"][:, :], ALU.mult,
                            ALU.add).then_inc(K.away_ready, 1)
    dve.wait_ge(K.earlier_ready, g + 1)
    dve.wait_ge(K.away_ready, g + 1)
    nc.vector.scalar_tensor_tensor(K.moved[:, s, :], K.earlier[:, s, :], 0.0, K.away[:, s, :], ALU.is_gt,
                                   ALU.mult).then_inc(K.moved_ready, 1)
    dve.wait_ge(K.moved_ready, g + 1)
    nc.vector.tensor_tensor(targets_all[:, bass.ds(T * g, T)], K.moved[:, s, :], K.keys(s),
                            ALU.add).then_inc(K.saved, 1)


def stage_targets(nc, dve, K, g, s, targets_all, added, make):
    if make:
        dve.wait_ge(K.saved, g + 1)
    if past(g, 2):
        dve.wait_ge(added, 16 * T * (g - 1))
    nc.vector.tensor_scalar(K.target[:, s, :], targets_all[:, bass.ds(T * g, T)], 0.0, None,
                            ALU.add).then_inc(K.target_ready, 1)


def add_rows(pool, K, table, out, out_ready, added, g, s, j):
    chained = not isinstance(g, int) or T * g + j > 0
    if j == 0:
        pool.wait_ge(K.target_ready, g + 1)
        pool.wait_ge(out_ready, g + 1)
    if chained:
        pool.wait_ge(added, 16 * (T * g + j))
        pool.sem_inc(K.ticks, 1)
    pool.indirect_dma_start(table[:, :], bass.IndirectOffsetOnAxis(ap=K.target[:, s, j:j + 1], axis=0),
                            out[:, s, j, :], None, compute_op=ALU.add).then_inc(added, 16)


def edge_pool(pool, K, groups, gathers, free, table, out, out_ready, added, lag):
    def step(g, k, s):
        pool.wait_ge(K.idx_in[s], 16 * (k + 1))
        if past(g, 2):
            free(g)
            pool.sem_inc(K.ticks, 1)
        for j in range(T):
            for source, rows, at, landed in gathers:
                pool.indirect_dma_start(rows[:, s, j, :], None, source[:, :],
                                        bass.IndirectOffsetOnAxis(ap=K.idx[:, s, at + j:at + j + 1], axis=0)
                                        ).then_inc(landed[s], 16)
            if past(g, lag):
                add_rows(pool, K, table, out, out_ready, added, g - lag, (s + lag) % 2, j)

    sweep(pool, groups, step)
    for g in range(groups - lag, groups):
        for j in range(T):
            add_rows(pool, K, table, out, out_ready, added, g, g % 2, j)
    pool.wait_ge(added, 16 * T * groups)


def edges_attention(nc, c, x, idx_d, row_d, table, groups, targets_all, clears):
    sc = Scope(nc, "att")
    K = Keys(sc, "src")
    x_src = sc.sb("x_src", [P, 2, T, D])
    x_dst = sc.sb("x_dst", [P, 2, T, D])
    h = sc.sb("h", [P, 2, 2 * T, D])
    stats = sc.sb("stats", [P, 2, 2 * T, 6])
    mom = sc.sb("mom", [P, 2, 2 * T, 2])
    std = sc.sb("std", [P, 2, 2 * T])
    inv = sc.sb("inv", [P, 2, 2 * T])
    off = sc.sb("off", [P, 2, 2 * T])
    sq = sc.sb("sq", [P, 2, 2 * T])
    sq_junk = sc.sb("sq_junk", [P, 2, 2 * T, D])
    dot_junk = sc.sb("dot_junk", [P, 2, T, D])
    dot = sc.sb("dot", [P, 2, T])
    norm2 = sc.sb("norm2", [P, 2, T])
    norm = sc.sb("norm", [P, 2, T])
    rnorm = sc.sb("rnorm", [P, 2, T])
    cos = sc.sb("cos", [P, 2, T])
    score = sc.sb("score", [P, 2, T])
    val = sc.sb("val", [P, 2, T, A0])
    out = sc.sb("out", [P, 2, T, A0])
    sums = [sc.ps(f"sums{s}", [P, T, 256]) for s in range(2)]
    src_in, dst_in = sc.sem2("src_in"), sc.sem2("dst_in")
    cleared = sc.sem("cleared")
    ones_ready = sc.sem("ones_ready")
    stats_ready, mom_ready, std_ready = sc.sem("stats_ready"), sc.sem("mom_ready"), sc.sem("std_ready")
    inv_ready, off_ready = sc.sem("inv_ready"), sc.sem("off_ready")
    h_ready, sq_ready, dot_ready = sc.sem("h_ready"), sc.sem("sq_ready"), sc.sem("dot_ready")
    norm2_ready, norm_ready, rnorm_ready = sc.sem("norm2_ready"), sc.sem("norm_ready"), sc.sem("rnorm_ready")
    cos_ready, score_ready = sc.sem("cos_ready"), sc.sem("score_ready")
    weight_ready, val_ready = sc.sem("weight_ready"), sc.sem("val_ready")
    summed, out_ready, added = sc.sem("summed"), sc.sem("out_ready"), sc.sem("added")

    with nc.Block() as block:
        @block.sync
        def _(sp):
            def step(g, k, s):
                if past(g, 2):
                    sp.wait_ge(src_in[s], 16 * T * k)
                    sp.wait_ge(dst_in[s], 16 * T * k)
                    sp.wait_ge(K.same_ready, g - 1)
                    sp.wait_ge(K.saved, g - 1)
                    sp.sem_inc(sc.ticks, 1)
                index_loads(sp, K, g, k, s, idx_d, row_d)
                for view in clears:
                    sp.dma_start(block_of(view, g), c["zero"][:, 0:view.shape[2]]).then_inc(cleared, 16)
            sweep(sp, groups, step)
            sp.wait_ge(cleared, 16 * groups * len(clears))

        @block.gpsimd
        def _(pool):
            def free(g):
                pool.wait_ge(mom_ready, g - 1)
                pool.wait_ge(h_ready, g - 1)
            edge_pool(pool, K, groups, [(x, x_src, 0, src_in), (x, x_dst, T, dst_in)], free, table, out,
                      out_ready, added, 3)

        @block.vector
        def _(dve):
            for s in range(2):
                last = nc.vector.memset(val[:, s, :, D + 1:D + 2], 1.0)
            last.then_inc(ones_ready, 1)

            def back(g, s):
                dve.wait_ge(h_ready, g + 1)
                for j in range(T):
                    last = nc.vector.tensor_tensor_reduce(
                        out=dot_junk[:, s, j, :], in0=h[:, s, j, :], in1=h[:, s, T + j, :], scale=1.0, scalar=0.0,
                        op0=ALU.mult, op1=ALU.add, accum_out=dot[:, s, j:j + 1])
                last.then_inc(dot_ready, 1)
                dve.wait_ge(sq_ready, g + 1)
                nc.vector.tensor_tensor(norm2[:, s, :], sq[:, s, 0:T], sq[:, s, T:2 * T],
                                        ALU.mult).then_inc(norm2_ready, 1)

            def scores(g, s):
                dve.wait_ge(norm_ready, g + 1)
                nc.vector.reciprocal(rnorm[:, s, :], norm[:, s, :]).then_inc(rnorm_ready, 1)
                dve.wait_ge(rnorm_ready, g + 1)
                dve.wait_ge(dot_ready, g + 1)
                nc.vector.tensor_tensor(cos[:, s, :], dot[:, s, :], rnorm[:, s, :], ALU.mult).then_inc(cos_ready, 1)
                dve.wait_ge(cos_ready, g + 1)
                nc.vector.tensor_scalar(score[:, s, :], cos[:, s, :], c["beta"][:, :], c["shift"][:, :],
                                        ALU.mult, ALU.subtract).then_inc(score_ready, 1)

            def step(g, k, s):
                if past(g, 1):
                    back(g - 1, 1 - s)
                dve.wait_ge(src_in[s], 16 * T * (k + 1))
                dve.wait_ge(dst_in[s], 16 * T * (k + 1))
                for j in range(T):
                    nc.vector.bn_stats(stats[:, s, j, :], x_src[:, s, j, :])
                    last = nc.vector.bn_stats(stats[:, s, T + j, :], x_dst[:, s, j, :])
                last.then_inc(stats_ready, 1)
                dve.wait_ge(stats_ready, g + 1)
                dve.sem_inc(sc.ticks, 1)
                for j in range(2 * T):
                    last = nc.vector.bn_aggr(mom[:, s, j, :], stats[:, s, j, :])
                last.then_inc(mom_ready, 1)
                index_work(nc, dve, K, c, g, k, s, summed, targets_all, True)
                if past(g, 1):
                    stage_targets(nc, dve, K, g - 1, 1 - s, targets_all, added, True)
                dve.wait_ge(std_ready, g + 1)
                nc.vector.reciprocal(inv[:, s, :], std[:, s, :]).then_inc(inv_ready, 1)
                dve.wait_ge(inv_ready, g + 1)
                nc.vector.scalar_tensor_tensor(off[:, s, :], mom[:, s, :, 0], -1.0, inv[:, s, :], ALU.mult,
                                               ALU.mult).then_inc(off_ready, 1)
                if past(g, 1):
                    scores(g - 1, 1 - s)
            sweep(dve, groups, step)
            stage_targets(nc, dve, K, groups - 1, (groups - 1) % 2, targets_all, added, True)
            back(groups - 1, (groups - 1) % 2)
            scores(groups - 1, (groups - 1) % 2)

        @block.scalar
        def _(act):
            act.wait_ge(ones_ready, 1)

            def norms(g, s):
                act.wait_ge(norm2_ready, g + 1)
                nc.scalar.activation(norm[:, s, :], norm2[:, s, :], ACT.Sqrt).then_inc(norm_ready, 1)

            def weights(g, s):
                act.wait_ge(score_ready, g + 1)
                if past(g, 2):
                    act.wait_ge(summed, g - 1)
                nc.scalar.activation(val[:, s, :, D], score[:, s, :], ACT.Exp).then_inc(weight_ready, 1)
                act.wait_ge(weight_ready, g + 1)
                for j in range(T):
                    last = nc.scalar.activation(val[:, s, j, 0:D], h[:, s, T + j, :], ACT.Copy,
                                                scale=val[:, s, j, D:D + 1])
                last.then_inc(val_ready, 1)

            def sums_out(g, s):
                act.wait_ge(summed, g + 1)
                if past(g, 2):
                    act.wait_ge(added, 16 * T * (g - 1))
                nc.scalar.activation(out[:, s, :, :], sums[s][:, :, 0:A0], ACT.Copy).then_inc(out_ready, 1)

            def step(g, k, s):
                if past(g, 2):
                    sums_out(g - 2, s)
                act.wait_ge(mom_ready, g + 1)
                nc.scalar.activation(std[:, s, :], mom[:, s, :, 1], ACT.Sqrt,
                                     bias=c["ln_eps"][:, :]).then_inc(std_ready, 1)
                if past(g, 1):
                    norms(g - 1, 1 - s)
                act.wait_ge(off_ready, g + 1)
                if past(g, 2):
                    act.wait_ge(dot_ready, g - 1)
                for j in range(T):
                    nc.scalar.activation(h[:, s, j, :], x_src[:, s, j, :], ACT.Relu,
                                         scale=inv[:, s, j:j + 1], bias=off[:, s, j:j + 1])
                    last = nc.scalar.activation(h[:, s, T + j, :], x_dst[:, s, j, :], ACT.Relu,
                                                scale=inv[:, s, T + j:T + j + 1], bias=off[:, s, T + j:T + j + 1])
                last.then_inc(h_ready, 1)
                act.wait_ge(h_ready, g + 1)
                for j in range(2 * T):
                    last = nc.scalar.activation(sq_junk[:, s, j, :], h[:, s, j, :], ACT.Square,
                                                accum_out=sq[:, s, j:j + 1])
                last.then_inc(sq_ready, 1)
                if past(g, 1):
                    weights(g - 1, 1 - s)
            sweep(act, groups, step)
            sums_out(groups - 2, (groups - 2) % 2)
            norms(groups - 1, (groups - 1) % 2)
            weights(groups - 1, (groups - 1) % 2)
            sums_out(groups - 1, (groups - 1) % 2)

        @block.tensor
        def _(pe):
            def step(g, k, s):
                pe.wait_ge(K.same_ready, g + 1)
                pe.wait_ge(val_ready, g + 1)
                if past(g, 2):
                    pe.wait_ge(out_ready, g - 1)
                for j in range(T):
                    last = nc.tensor.matmul(sums[s][:, j, 0:A0], K.same[:, s, j, :], val[:, s, j, :],
                                            start=True, stop=True)
                last.then_inc(summed, 1)
            sweep(pe, groups, step)
    sc.close()


def nodes_attention(nc, c, x_v, agg_v, x1_v, groups, isq_all, mom_all):
    sc = Scope(nc, "natt")
    x = sc.sb("x", [P, RING, T, D])
    agg = sc.sb("agg", [P, RING, T, A0])
    h = sc.sb("h", [P, 2, T, D])
    num = sc.sb("num", [P, 2, T, D])
    x1 = sc.sb("x1", [P, RING, T, D])
    stats = sc.sb("stats", [P, 2, T, 6])
    stats1 = sc.sb("stats1", [P, 2, T, 6])
    mom = sc.sb("mom", [P, 2, T, 2])
    mom1 = sc.sb("mom1", [P, 2, T, 2])
    std = sc.sb("std", [P, 2, T])
    inv = sc.sb("inv", [P, 2, T])
    off = sc.sb("off", [P, 2, T])
    den = sc.sb("den", [P, 2, T])
    rden = sc.sb("rden", [P, 2, T])
    sdeg = sc.sb("sdeg", [P, 2, T])
    isq = sc.sb("isq", [P, 2, T])
    x_in, agg_in, x1_out = sc.sem2("x_in", RING), sc.sem2("agg_in", RING), sc.sem2("x1_out", RING)
    stats_ready, mom_ready, std_ready = sc.sem("stats_ready"), sc.sem("mom_ready"), sc.sem("std_ready")
    inv_ready, off_ready, h_ready = sc.sem("inv_ready"), sc.sem("off_ready"), sc.sem("h_ready")
    den_ready, rden_ready, num_ready = sc.sem("den_ready"), sc.sem("rden_ready"), sc.sem("num_ready")
    sdeg_ready, isq_ready, kept = sc.sem("sdeg_ready"), sc.sem("isq_ready"), sc.sem("kept")
    x1_ready, stats1_ready, mom1_ready = sc.sem("x1_ready"), sc.sem("stats1_ready"), sc.sem("mom1_ready")
    with nc.Block() as block:
        @block.sync
        def _(sp):
            def step(g, k, s):
                if past(g, RING):
                    sp.wait_ge(x1_ready, g - RING + 1)
                    sp.wait_ge(sdeg_ready, g - RING + 1)
                    sp.wait_ge(num_ready, g - RING + 1)
                    sp.sem_inc(sc.ticks, 1)
                sp.dma_start(x[:, s, :, :].rearrange("p t d -> p (t d)"), block_of(x_v, g)).then_inc(x_in[s], 16)
                sp.dma_start(agg[:, s, :, :].rearrange("p t d -> p (t d)"), block_of(agg_v, g)).then_inc(agg_in[s], 16)
            sweep(sp, groups, step, RING)

        @block.gpsimd
        def _(pool):
            def step(g, k, s):
                pool.wait_ge(x1_ready, g + 1)
                pool.dma_start(block_of(x1_v, g), x1[:, s, :, :].rearrange("p t d -> p (t d)")).then_inc(x1_out[s], 16)
            sweep(pool, groups, step, RING)
            for s in range(RING):
                pool.wait_ge(x1_out[s], 16 * rounds_of(groups, s))

        @block.vector
        def _(dve):
            def back(g, k, s):
                dve.wait_ge(h_ready, g + 1)
                nc.vector.scalar_tensor_tensor(num[:, s % 2, :, :], h[:, s % 2, :, :], c["w_self"][:, :],
                                               agg[:, s, :, 0:D], ALU.mult, ALU.add).then_inc(num_ready, 1)
                dve.wait_ge(num_ready, g + 1)
                dve.wait_ge(rden_ready, g + 1)
                if past(g, RING):
                    dve.wait_ge(x1_out[s], 16 * k)
                for j in range(T):
                    last = nc.vector.scalar_tensor_tensor(x1[:, s, j, :], num[:, s % 2, j, :], rden[:, s % 2, j:j + 1],
                                                          x[:, s, j, :], ALU.mult, ALU.add)
                last.then_inc(x1_ready, 1)
                dve.wait_ge(x1_ready, g + 1)
                for j in range(T):
                    last = nc.vector.bn_stats(stats1[:, s % 2, j, :], x1[:, s, j, :])
                last.then_inc(stats1_ready, 1)
                dve.wait_ge(stats1_ready, g + 1)
                dve.sem_inc(sc.ticks, 1)
                for j in range(T):
                    last = nc.vector.bn_aggr(mom1[:, s % 2, j, :], stats1[:, s % 2, j, :])
                last.then_inc(mom1_ready, 1)
                dve.wait_ge(mom1_ready, g + 1)
                nc.vector.tensor_scalar(mom_all[:, bass.ds(T * g, T), :], mom1[:, s % 2, :, :], 0.0, None,
                                        ALU.add).then_inc(kept, 1)

            def step(g, k, s):
                dve.wait_ge(x_in[s], 16 * (k + 1))
                for j in range(T):
                    last = nc.vector.bn_stats(stats[:, s % 2, j, :], x[:, s, j, :])
                last.then_inc(stats_ready, 1)
                dve.wait_ge(stats_ready, g + 1)
                dve.sem_inc(sc.ticks, 1)
                for j in range(T):
                    last = nc.vector.bn_aggr(mom[:, s % 2, j, :], stats[:, s % 2, j, :])
                last.then_inc(mom_ready, 1)
                dve.wait_ge(agg_in[s], 16 * (k + 1))
                nc.vector.tensor_scalar(den[:, s % 2, :], agg[:, s, :, D], c["w_self"][:, :], None,
                                        ALU.add).then_inc(den_ready, 1)
                dve.wait_ge(den_ready, g + 1)
                nc.vector.reciprocal(rden[:, s % 2, :], den[:, s % 2, :]).then_inc(rden_ready, 1)
                dve.wait_ge(std_ready, g + 1)
                nc.vector.reciprocal(inv[:, s % 2, :], std[:, s % 2, :]).then_inc(inv_ready, 1)
                dve.wait_ge(inv_ready, g + 1)
                nc.vector.scalar_tensor_tensor(off[:, s % 2, :], mom[:, s % 2, :, 0], -1.0, inv[:, s % 2, :], ALU.mult,
                                               ALU.mult).then_inc(off_ready, 1)
                dve.wait_ge(sdeg_ready, g + 1)
                nc.vector.reciprocal(isq[:, s % 2, :], sdeg[:, s % 2, :]).then_inc(isq_ready, 1)
                dve.wait_ge(isq_ready, g + 1)
                nc.vector.tensor_scalar(isq_all[:, bass.ds(T * g, T)], isq[:, s % 2, :], 0.0, None,
                                        ALU.add).then_inc(kept, 1)
                if past(g, 1):
                    back(g - 1, *before(k, s, 1))
            sweep(dve, groups, step, RING)
            back(groups - 1, (groups - 1) // RING, (groups - 1) % RING)

        @block.scalar
        def _(act):
            def step(g, k, s):
                act.wait_ge(mom_ready, g + 1)
                nc.scalar.activation(std[:, s % 2, :], mom[:, s % 2, :, 1], ACT.Sqrt,
                                     bias=c["ln_eps"][:, :]).then_inc(std_ready, 1)
                act.wait_ge(agg_in[s], 16 * (k + 1))
                if past(g, 2):
                    act.wait_ge(isq_ready, g - 1)
                nc.scalar.activation(sdeg[:, s % 2, :], agg[:, s, :, D + 1], ACT.Sqrt, bias=c["one"][:, :]
                                     ).then_inc(sdeg_ready, 1)
                act.wait_ge(off_ready, g + 1)
                if past(g, 2):
                    act.wait_ge(num_ready, g - 1)
                for j in range(T):
                    last = nc.scalar.activation(h[:, s % 2, j, :], x[:, s, j, :], ACT.Relu,
                                                scale=inv[:, s % 2, j:j + 1], bias=off[:, s % 2, j:j + 1])
                last.then_inc(h_ready, 1)
            sweep(act, groups, step, RING)
    sc.close()


def ln_of_all(nc, c, layer, mom_all, inv_all, off_all):
    sc = Scope(nc, f"ln{layer}")
    std_ready, inv_ready = sc.sem("std_ready"), sc.sem("inv_ready")
    with nc.Block() as block:
        @block.scalar
        def _(act):
            nc.scalar.activation(off_all[:, :], mom_all[:, :, 1], ACT.Sqrt,
                                 bias=c["ln_eps"][:, :]).then_inc(std_ready, 1)

        @block.vector
        def _(dve):
            dve.wait_ge(std_ready, 1)
            nc.vector.reciprocal(inv_all[:, :], off_all[:, :]).then_inc(inv_ready, 1)
            dve.wait_ge(inv_ready, 1)
            nc.vector.scalar_tensor_tensor(off_all[:, :], mom_all[:, :, 0], -1.0, inv_all[:, :], ALU.mult,
                                           ALU.mult)
    sc.close()


def edges_message(nc, c, x, idx_d, row_d, attr_d, table, groups, targets_all, layer):
    two = layer == 2
    DE = D64 if two else D4
    C = FC if two else 1
    if two:
        w_src, w_dst, w_attr, w_out = c["cw1_src"], c["cw1_dst"], c["cw1_attr"], c["cw2"]
        b_hidden, b_out = c["cb1"], c["cb2_row"]
    else:
        w_src, w_dst, w_attr, w_out = c["m1_src"], c["m1_dst"], c["m1_attr"], c["m2"]
        b_hidden, b_out = c["mb1"], c["mb2_row"]
    sc = Scope(nc, f"msg{layer}")
    K = Keys(sc, "dst")
    x_src = sc.sb("x_src", [P, 2, T, D])
    x_dst = sc.sb("x_dst", [P, 2, T, D])
    attr = sc.sb("attr", [DE, 2, W])
    stats = sc.sb("stats", [P, 2, 2 * T, 6])
    mom = sc.sb("mom", [P, 2, 2 * T, 2])
    std = sc.sb("std", [P, 2, 2 * T])
    inv = sc.sb("inv", [P, 2, 2 * T])
    off = sc.sb("off", [P, 2, 2 * T])
    u = sc.sb("u", [P, 2, 2 * T, D])
    if two:
        h = sc.sb("h", [P, 2, 2 * T, D])
        pre = sc.sb("pre", [P, C, W])
        pre_ready = sc.sem("pre_ready")
        stats_b = sc.sb("stats_b", [P, 2, 2 * T, 6])
        mom_b = sc.sb("mom_b", [P, 2, 2 * T, 2])
        std_b = sc.sb("std_b", [P, 2, 2 * T])
        inv_b = sc.sb("inv_b", [P, 2, 2 * T])
        off_b = sc.sb("off_b", [P, 2, 2 * T])
        h_ready, stats_b_ready, mom_b_ready = sc.sem("h_ready"), sc.sem("stats_b_ready"), sc.sem("mom_b_ready")
        std_b_ready, inv_b_ready, off_b_ready = sc.sem("std_b_ready"), sc.sem("inv_b_ready"), sc.sem("off_b_ready")
    src_t = sc.sb("src_t", [P, 2, W])
    dst_t = sc.sb("dst_t", [P, 2, W])
    hid = sc.sb("hid", [P, 2, C, W])
    msg = sc.sb("msg", [P, 2, T, D])
    out = sc.sb("out", [P, 2, T, D])
    p_src = sc.ps("p_src", [P, W])
    p_dst = sc.ps("p_dst", [P, W])
    p_hid = [sc.ps(f"p_hid{i}", [P, W]) for i in range(C)]
    p_msg = sc.ps("p_msg", [P, T, D])
    p_sum = sc.ps("p_sum", [P, T, D])
    attr_in, src_in, dst_in = sc.sem2("attr_in"), sc.sem2("src_in"), sc.sem2("dst_in")
    stats_ready, mom_ready, std_ready = sc.sem("stats_ready"), sc.sem("mom_ready"), sc.sem("std_ready")
    inv_ready, off_ready, u_ready = sc.sem("inv_ready"), sc.sem("off_ready"), sc.sem("u_ready")
    flipped, src_t_ready, dst_t_ready = sc.sem("flipped"), sc.sem("src_t_ready"), sc.sem("dst_t_ready")
    hid_made, hid_ready = sc.sem("hid_made"), sc.sem("hid_ready")
    msg_made, msg_ready = sc.sem("msg_made"), sc.sem("msg_ready")
    summed, out_ready, added = sc.sem("summed"), sc.sem("out_ready"), sc.sem("added")

    with nc.Block() as block:
        @block.sync
        def _(sp):
            def step(g, k, s):
                if past(g, 2):
                    sp.wait_ge(src_in[s], 16 * T * k)
                    sp.wait_ge(dst_in[s], 16 * T * k)
                    sp.wait_ge(K.same_ready, g - 1)
                    if not two:
                        sp.wait_ge(K.saved, g - 1)
                    sp.sem_inc(sc.ticks, 1)
                index_loads(sp, K, g, k, s, idx_d, row_d)
            sweep(sp, groups, step)

        @block.gpsimd
        def _(pool):
            def free(g):
                pool.wait_ge(mom_ready, g - 1)
                pool.wait_ge(h_ready, 2 * T * (g - 1)) if two else pool.wait_ge(u_ready, g - 1)
            edge_pool(pool, K, groups, [(x, x_src, 0, src_in), (x, x_dst, T, dst_in)], free, table, out,
                      out_ready, added, 4)

        @block.vector
        def _(dve):
            def moments(g, s, rows_of, stats, stats_ready, mom, mom_ready):
                for j in range(2 * T):
                    rows = rows_of(g, s, j)
                    last = nc.vector.bn_stats(stats[:, s, j, :], rows)
                last.then_inc(stats_ready, 1)
                dve.wait_ge(stats_ready, g + 1)
                dve.sem_inc(sc.ticks, 1)
                for j in range(2 * T):
                    last = nc.vector.bn_aggr(mom[:, s, j, :], stats[:, s, j, :])
                last.then_inc(mom_ready, 1)

            def affine(g, s, std, std_ready, inv, inv_ready, mom, off, off_ready):
                dve.wait_ge(std_ready, g + 1)
                nc.vector.reciprocal(inv[:, s, :], std[:, s, :]).then_inc(inv_ready, 1)
                dve.wait_ge(inv_ready, g + 1)
                nc.vector.scalar_tensor_tensor(off[:, s, :], mom[:, s, :, 0], -1.0, inv[:, s, :], ALU.mult,
                                               ALU.mult).then_inc(off_ready, 1)

            def gathered(g, s, j):
                return x_src[:, s, j, :] if j < T else x_dst[:, s, j - T, :]

            def rectified(g, s, j):
                dve.wait_ge(h_ready, 2 * T * g + j + 1)
                return h[:, s, j, :]

            def messages(g, s):
                dve.wait_ge(msg_made, g + 1)
                if past(g, 2):
                    dve.wait_ge(summed, g - 1)
                nc.vector.tensor_tensor(msg[:, s, :, :], p_msg[:, :, :], b_out[:, :, :],
                                        ALU.add).then_inc(msg_ready, 1)

            def leak(g, s):
                if past(g, 2):
                    dve.wait_ge(msg_made, g - 1)
                for i in range(C):
                    dve.wait_ge(pre_ready, C * g + i + 1)
                    nc.vector.scalar_tensor_tensor(hid[:, s, i, :], pre[:, i, :], SLOPE, pre[:, i, :], ALU.mult,
                                                   ALU.max).then_inc(hid_ready, 1)

            def step(g, k, s):
                dve.wait_ge(src_in[s], 16 * T * (k + 1))
                dve.wait_ge(dst_in[s], 16 * T * (k + 1))
                moments(g, s, gathered, stats, stats_ready, mom, mom_ready)
                if past(g, 2):
                    messages(g - 2, s)
                affine(g, s, std, std_ready, inv, inv_ready, mom, off, off_ready)
                if past(g, 2):
                    dve.wait_ge(flipped, g - 1)
                if two:
                    moments(g, s, rectified, stats_b, stats_b_ready, mom_b, mom_b_ready)
                    affine(g, s, std_b, std_b_ready, inv_b, inv_b_ready, mom_b, off_b, off_b_ready)
                    dve.wait_ge(off_b_ready, g + 1)
                    for j in range(2 * T):
                        last = nc.vector.tensor_scalar(u[:, s, j, :], h[:, s, j, :], inv_b[:, s, j:j + 1],
                                                       off_b[:, s, j:j + 1], ALU.mult, ALU.add)
                    last.then_inc(u_ready, 1)
                    if past(g, 1):
                        leak(g - 1, 1 - s)
                else:
                    dve.wait_ge(off_ready, g + 1)
                    for j in range(2 * T):
                        last = nc.vector.tensor_scalar(u[:, s, j, :], gathered(g, s, j), inv[:, s, j:j + 1],
                                                       off[:, s, j:j + 1], ALU.mult, ALU.add)
                    last.then_inc(u_ready, 1)
                index_work(nc, dve, K, c, g, k, s, summed, targets_all, not two)
                if past(g, 2):
                    stage_targets(nc, dve, K, g - 2, s, targets_all, added, not two)
            sweep(dve, groups, step)
            messages(groups - 2, (groups - 2) % 2)
            if two:
                leak(groups - 1, (groups - 1) % 2)
            messages(groups - 1, (groups - 1) % 2)
            for g in (groups - 2, groups - 1):
                stage_targets(nc, dve, K, g, g % 2, targets_all, added, not two)

        @block.scalar
        def _(act):
            def sums_out(g, s):
                act.wait_ge(summed, g + 1)
                if past(g, 2):
                    act.wait_ge(added, 16 * T * (g - 1))
                nc.scalar.activation(out[:, s, :, :], p_sum[:, :, :], ACT.Copy).then_inc(out_ready, 1)

            def hidden(g, s):
                if past(g, 2) and not two:
                    act.wait_ge(msg_made, g - 1)
                for i in range(C):
                    act.wait_ge(hid_made, C * g + i + 1)
                    if two:
                        if past(g, 1):
                            act.wait_ge(hid_ready, C * g)
                        nc.scalar.activation(pre[:, i, :], p_hid[i][:, :], ACT.Identity,
                                             bias=b_hidden[:, i:i + 1]).then_inc(pre_ready, 1)
                    else:
                        nc.scalar.activation(hid[:, s, i, :], p_hid[i][:, :], ACT.Relu,
                                             bias=b_hidden[:, i:i + 1]).then_inc(hid_ready, 1)

            def attributes(g, s):
                act.dma_start(attr[:, s, :], block_of(attr_d, g)).then_inc(attr_in[s], 16)

            def step(g, k, s):
                act.wait_ge(mom_ready, g + 1)
                nc.scalar.activation(std[:, s, :], mom[:, s, :, 1], ACT.Sqrt,
                                     bias=c["ln_eps"][:, :]).then_inc(std_ready, 1)
                if two:
                    act.wait_ge(off_ready, g + 1)
                    if past(g, 2):
                        act.wait_ge(u_ready, g - 1)
                    for j in range(2 * T):
                        rows = x_src[:, s, j, :] if j < T else x_dst[:, s, j - T, :]
                        nc.scalar.activation(h[:, s, j, :], rows, ACT.Relu, scale=inv[:, s, j:j + 1],
                                             bias=off[:, s, j:j + 1]).then_inc(h_ready, 1)
                if past(g, 1):
                    hidden(g - 1, 1 - s)
                    if ahead(g, groups):
                        attributes(g + 1, 1 - s)
                if two:
                    act.wait_ge(mom_b_ready, g + 1)
                    nc.scalar.activation(std_b[:, s, :], mom_b[:, s, :, 1], ACT.Sqrt,
                                         bias=c["ln_eps"][:, :]).then_inc(std_b_ready, 1)
                if past(g, 2):
                    sums_out(g - 2, s)
                act.wait_ge(flipped, g + 1)
                if past(g, 2):
                    act.wait_ge(hid_made, C * (g - 1))
                if two:
                    nc.scalar.activation(src_t[:, s, :], p_src[:, :], ACT.Identity, scale=c["ln1_g"][:, :],
                                         bias=c["ln1_b"][:, :]).then_inc(src_t_ready, 1)
                    nc.scalar.activation(dst_t[:, s, :], p_dst[:, :], ACT.Identity, scale=c["ln1_g"][:, :],
                                         bias=c["ln1_b"][:, :]).then_inc(dst_t_ready, 1)
                else:
                    nc.scalar.activation(src_t[:, s, :], p_src[:, :], ACT.Relu).then_inc(src_t_ready, 1)
                    nc.scalar.activation(dst_t[:, s, :], p_dst[:, :], ACT.Relu).then_inc(dst_t_ready, 1)
            attributes(0, 0)
            attributes(1, 1)
            sweep(act, groups, step)
            hidden(groups - 1, (groups - 1) % 2)
            sums_out(groups - 2, (groups - 2) % 2)
            sums_out(groups - 1, (groups - 1) % 2)

        @block.tensor
        def _(pe):
            def to_messages(g, s):
                pe.wait_ge(hid_ready, C * (g + 1))
                if past(g, 1):
                    pe.wait_ge(msg_ready, g)
                for j in range(T):
                    for i in range(C):
                        last = nc.tensor.matmul(p_msg[:, j, :], hid[:, s, i, j * P:(j + 1) * P], w_out[:, i, :],
                                                start=(i == 0), stop=(i == C - 1))
                last.then_inc(msg_made, 1)

            def sum_equal(g, s):
                pe.wait_ge(msg_ready, g + 1)
                pe.wait_ge(K.same_ready, g + 1)
                if past(g, 1):
                    pe.wait_ge(out_ready, g)
                for j in range(T):
                    last = nc.tensor.matmul(p_sum[:, j, :], K.same[:, s, j, :], msg[:, s, j, :], start=True,
                                            stop=True)
                last.then_inc(summed, 1)

            def step(g, k, s):
                if past(g, 2):
                    sum_equal(g - 2, s)
                pe.wait_ge(u_ready, g + 1)
                if past(g, 1):
                    pe.wait_ge(src_t_ready, g)
                    pe.wait_ge(dst_t_ready, g)
                for j in range(T):
                    nc.tensor.transpose(p_src[:, j * P:(j + 1) * P], u[:, s, j, :], c["ident"][:, :])
                    last = nc.tensor.transpose(p_dst[:, j * P:(j + 1) * P], u[:, s, T + j, :], c["ident"][:, :])
                last.then_inc(flipped, 1)
                if past(g, 1):
                    to_messages(g - 1, 1 - s)
                pe.wait_ge(src_t_ready, g + 1)
                pe.wait_ge(dst_t_ready, g + 1)
                pe.wait_ge(attr_in[s], 16 * (k + 1))
                if past(g, 1):
                    pe.wait_ge(pre_ready if two else hid_ready, C * g)
                for i in range(C):
                    cols = slice(i * D, (i + 1) * D)
                    nc.tensor.matmul(p_hid[i][:, :], w_src[:, cols], src_t[:, s, :], start=True, stop=False)
                    nc.tensor.matmul(p_hid[i][:, :], w_dst[:, cols], dst_t[:, s, :], start=False, stop=False)
                    nc.tensor.matmul(p_hid[i][:, :], w_attr[:, cols], attr[:, s, :], start=False,
                                     stop=True).then_inc(hid_made, 1)
            sweep(pe, groups, step)
            sum_equal(groups - 2, (groups - 2) % 2)
            to_messages(groups - 1, (groups - 1) % 2)
            sum_equal(groups - 1, (groups - 1) % 2)
    sc.close()


def nodes_gated(nc, c, x1_v, agg_v, x2_v, groups, inv_all, off_all, mom_all):
    sc = Scope(nc, "gru")
    x = sc.sb("x", [P, RING, T, D])
    agg = sc.sb("agg", [P, RING, T, D])
    ln = sc.sb("ln", [P, 2, 2, T])
    u = sc.sb("u", [P, 2, T, D])
    h_t = sc.sb("h_t", [P, 2, W])
    a_t = sc.sb("a_t", [P, 2, W])
    z = sc.sb("z", [P, 2, W])
    r = sc.sb("r", [P, 2, W])
    rh = sc.sb("rh", [P, 2, W])
    cand = sc.sb("cand", [P, 2, W])
    step_t = sc.sb("step_t", [P, 2, W])
    gated = sc.sb("gated", [P, 2, W])
    o_t = sc.sb("o_t", [P, 2, W])
    x2 = sc.sb("x2", [P, RING, T, D])
    stats = sc.sb("stats", [P, 2, T, 6])
    mom = sc.sb("mom", [P, 2, T, 2])
    p_h, p_a, p_z, p_r, p_c = (sc.ps(n, [P, W]) for n in ("p_h", "p_a", "p_z", "p_r", "p_c"))
    p_o = sc.ps("p_o", [P, T, D])
    x_in, agg_in, x2_out = sc.sem2("x_in", RING), sc.sem2("agg_in", RING), sc.sem2("x2_out", RING)
    ln_ready, u_ready, flipped = sc.sem("ln_ready"), sc.sem("u_ready"), sc.sem("flipped")
    h_t_ready, a_t_ready = sc.sem("h_t_ready"), sc.sem("a_t_ready")
    r_made, r_ready, z_made, z_ready = sc.sem("r_made"), sc.sem("r_ready"), sc.sem("z_made"), sc.sem("z_ready")
    rh_ready, c_made, c_ready = sc.sem("rh_ready"), sc.sem("c_made"), sc.sem("c_ready")
    step_ready, gated_ready, o_t_ready = sc.sem("step_ready"), sc.sem("gated_ready"), sc.sem("o_t_ready")
    back_made, x2_ready = sc.sem("back_made"), sc.sem("x2_ready")
    stats_ready, mom_ready, kept = sc.sem("stats_ready"), sc.sem("mom_ready"), sc.sem("kept")
    with nc.Block() as block:
        @block.sync
        def _(sp):
            def step(g, k, s):
                if past(g, RING):
                    sp.wait_ge(x2_ready, g - RING + 1)
                    sp.wait_ge(flipped, g - RING + 1)
                    sp.sem_inc(sc.ticks, 1)
                sp.dma_start(x[:, s, :, :].rearrange("p t d -> p (t d)"), block_of(x1_v, g)).then_inc(x_in[s], 16)
                sp.dma_start(agg[:, s, :, :].rearrange("p t d -> p (t d)"), block_of(agg_v, g)).then_inc(agg_in[s], 16)
            sweep(sp, groups, step, RING)

        @block.gpsimd
        def _(pool):
            def blend(g, s):
                pool.wait_ge(c_ready, g + 1)
                nc.gpsimd.tensor_tensor(step_t[:, s % 2, :], cand[:, s % 2, :], h_t[:, s % 2, :],
                                        ALU.subtract).then_inc(step_ready, 1)
                pool.wait_ge(step_ready, g + 1)
                pool.wait_ge(z_ready, g + 1)
                if past(g, 2):
                    pool.wait_ge(o_t_ready, g - 1)
                nc.gpsimd.tensor_tensor(gated[:, s % 2, :], z[:, s % 2, :], step_t[:, s % 2, :],
                                        ALU.mult).then_inc(gated_ready, 1)

            def store(g, s):
                pool.wait_ge(x2_ready, g + 1)
                pool.dma_start(block_of(x2_v, g), x2[:, s, :, :].rearrange("p t d -> p (t d)")).then_inc(x2_out[s], 16)

            def step(g, k, s):
                blend(g, s)
                if past(g, 1):
                    store(g - 1, (s - 1) % RING)
            sweep(pool, groups, step, RING)
            store(groups - 1, (groups - 1) % RING)
            for s in range(RING):
                pool.wait_ge(x2_out[s], 16 * rounds_of(groups, s))

        @block.vector
        def _(dve):
            def back(g, k, s):
                dve.wait_ge(gated_ready, g + 1)
                if past(g, 2):
                    dve.wait_ge(back_made, g - 1)
                nc.vector.tensor_tensor(o_t[:, s % 2, :], gated[:, s % 2, :], h_t[:, s % 2, :], ALU.add).then_inc(o_t_ready, 1)

            def finish(g, k, s):
                dve.wait_ge(back_made, g + 1)
                if past(g, RING):
                    dve.wait_ge(x2_out[s], 16 * k)
                nc.vector.tensor_tensor(x2[:, s, :, :], p_o[:, :, :], x[:, s, :, :], ALU.add).then_inc(x2_ready, 1)
                dve.wait_ge(x2_ready, g + 1)
                for j in range(T):
                    last = nc.vector.bn_stats(stats[:, s % 2, j, :], x2[:, s, j, :])
                last.then_inc(stats_ready, 1)
                dve.wait_ge(stats_ready, g + 1)
                dve.sem_inc(sc.ticks, 1)
                for j in range(T):
                    last = nc.vector.bn_aggr(mom[:, s % 2, j, :], stats[:, s % 2, j, :])
                last.then_inc(mom_ready, 1)
                dve.wait_ge(mom_ready, g + 1)
                nc.vector.tensor_scalar(mom_all[:, bass.ds(T * g, T), :], mom[:, s % 2, :, :], 0.0, None,
                                        ALU.add).then_inc(kept, 1)

            def front(g, k, s):
                nc.vector.tensor_scalar(ln[:, s % 2, 0, :], inv_all[:, bass.ds(T * g, T)], 0.0, None, ALU.add)
                nc.vector.tensor_scalar(ln[:, s % 2, 1, :], off_all[:, bass.ds(T * g, T)], 0.0, None,
                                        ALU.add).then_inc(ln_ready, 1)
                dve.wait_ge(ln_ready, g + 1)
                dve.wait_ge(x_in[s], 16 * (k + 1))
                if past(g, 2):
                    dve.wait_ge(flipped, g - 1)
                for j in range(T):
                    last = nc.vector.tensor_scalar(u[:, s % 2, j, :], x[:, s, j, :], ln[:, s % 2, 0, j:j + 1],
                                                   ln[:, s % 2, 1, j:j + 1], ALU.mult, ALU.add)
                last.then_inc(u_ready, 1)

            def step(g, k, s):
                dve.wait_ge(flipped, g + 1)
                if past(g, 2):
                    dve.wait_ge(o_t_ready, g - 1)
                nc.vector.tensor_scalar_max(h_t[:, s % 2, :], p_h[:, :], 0.0).then_inc(h_t_ready, 1)
                if ahead(g, groups):
                    front(g + 1, *after(k, s))
                if past(g, 1):
                    back(g - 1, *before(k, s, 1))
                dve.wait_ge(r_ready, g + 1)
                dve.wait_ge(h_t_ready, g + 1)
                if past(g, 2):
                    dve.wait_ge(c_made, g - 1)
                nc.vector.tensor_tensor(rh[:, s % 2, :], r[:, s % 2, :], h_t[:, s % 2, :], ALU.mult).then_inc(rh_ready, 1)
                if past(g, 1):
                    finish(g - 1, *before(k, s, 1))
            front(0, 0, 0)
            sweep(dve, groups, step, RING)
            back(groups - 1, (groups - 1) // RING, (groups - 1) % RING)
            finish(groups - 1, (groups - 1) // RING, (groups - 1) % RING)

        @block.scalar
        def _(act):
            def candidate(g, s):
                act.wait_ge(c_made, g + 1)
                if past(g, 2):
                    act.wait_ge(step_ready, g - 1)
                nc.scalar.activation(cand[:, s % 2, :], p_c[:, :], ACT.Tanh, bias=c["gb_h"][:, :]).then_inc(c_ready, 1)

            def step(g, k, s):
                act.wait_ge(flipped, g + 1)
                if past(g, 2):
                    act.wait_ge(c_made, g - 1)
                nc.scalar.activation(a_t[:, s % 2, :], p_a[:, :], ACT.Copy).then_inc(a_t_ready, 1)
                if past(g, 1):
                    candidate(g - 1, (s - 1) % RING)
                act.wait_ge(r_made, g + 1)
                if past(g, 2):
                    act.wait_ge(rh_ready, g - 1)
                nc.scalar.activation(r[:, s % 2, :], p_r[:, :], ACT.Sigmoid, bias=c["gb_r"][:, :]).then_inc(r_ready, 1)
                act.wait_ge(z_made, g + 1)
                if past(g, 2):
                    act.wait_ge(gated_ready, g - 1)
                nc.scalar.activation(z[:, s % 2, :], p_z[:, :], ACT.Sigmoid, bias=c["gb_z"][:, :]).then_inc(z_ready, 1)
            sweep(act, groups, step, RING)
            candidate(groups - 1, (groups - 1) % RING)

        @block.tensor
        def _(pe):
            def candidate(g, s):
                pe.wait_ge(rh_ready, g + 1)
                if past(g, 1):
                    pe.wait_ge(c_ready, g)
                nc.tensor.matmul(p_c[:, :], c["gw_h"][:, 1, :], a_t[:, s % 2, :], start=True, stop=False)
                nc.tensor.matmul(p_c[:, :], c["gw_h"][:, 0, :], rh[:, s % 2, :], start=False,
                                 stop=True).then_inc(c_made, 1)

            def turn_back(g, s):
                pe.wait_ge(o_t_ready, g + 1)
                if past(g, 1):
                    pe.wait_ge(x2_ready, g)
                for j in range(T):
                    last = nc.tensor.transpose(p_o[:, j, :], o_t[:, s % 2, j * P:(j + 1) * P], c["ident"][:, :])
                last.then_inc(back_made, 1)

            def step(g, k, s):
                pe.wait_ge(u_ready, g + 1)
                pe.wait_ge(agg_in[s], 16 * (k + 1))
                if past(g, 1):
                    pe.wait_ge(h_t_ready, g)
                    pe.wait_ge(a_t_ready, g)
                for j in range(T):
                    nc.tensor.transpose(p_h[:, j * P:(j + 1) * P], u[:, s % 2, j, :], c["ident"][:, :])
                    last = nc.tensor.transpose(p_a[:, j * P:(j + 1) * P], agg[:, s, j, :], c["ident"][:, :])
                last.then_inc(flipped, 1)
                if past(g, 1):
                    candidate(g - 1, (s - 1) % RING)
                pe.wait_ge(h_t_ready, g + 1)
                pe.wait_ge(a_t_ready, g + 1)
                if past(g, 1):
                    pe.wait_ge(r_ready, g)
                    pe.wait_ge(z_ready, g)
                nc.tensor.matmul(p_r[:, :], c["gw_r"][:, 0, :], h_t[:, s % 2, :], start=True, stop=False)
                nc.tensor.matmul(p_r[:, :], c["gw_r"][:, 1, :], a_t[:, s % 2, :], start=False,
                                 stop=True).then_inc(r_made, 1)
                nc.tensor.matmul(p_z[:, :], c["gw_z"][:, 0, :], h_t[:, s % 2, :], start=True, stop=False)
                nc.tensor.matmul(p_z[:, :], c["gw_z"][:, 1, :], a_t[:, s % 2, :], start=False,
                                 stop=True).then_inc(z_made, 1)
                if past(g, 1):
                    turn_back(g - 1, (s - 1) % RING)
            sweep(pe, groups, step, RING)
            candidate(groups - 1, (groups - 1) % RING)
            turn_back(groups - 1, (groups - 1) % RING)
    sc.close()


def nodes_feedforward(nc, c, x2_v, agg_v, x3_v, groups, inv_all, off_all, isq_all):
    sc = Scope(nc, "ff")
    x = sc.sb("x", [P, RING, T, D])
    agg = sc.sb("agg", [P, RING, T, D])
    ln = sc.sb("ln", [P, 2, 3, T])
    h = sc.sb("h", [P, 2, T, D])
    y = sc.sb("y", [P, 2, T, D])
    stats = sc.sb("stats", [P, 2, T, 6])
    mom = sc.sb("mom", [P, 2, T, 2])
    std = sc.sb("std", [P, 2, T])
    inv = sc.sb("inv", [P, 2, T])
    off = sc.sb("off", [P, 2, T])
    u = sc.sb("u", [P, 2, T, D])
    u_t = sc.sb("u_t", [P, 2, W])
    pre = sc.sb("pre", [P, FC, W])
    hid = sc.sb("hid", [P, 2, FC, W])
    rest = sc.sb("rest", [P, 3, T, D])
    rest_b = sc.sb("rest_b", [P, 2, T, D])
    x3 = sc.sb("x3", [P, RING, T, X3])
    p_t = sc.ps("p_t", [P, W])
    p_hid = [sc.ps(f"p_hid{i}", [P, W]) for i in range(FC)]
    p_o = [sc.ps(f"p_o{s}", [P, T, D]) for s in range(2)]
    x_in, agg_in, x3_out = sc.sem2("x_in", RING), sc.sem2("agg_in", RING), sc.sem2("x3_out", RING)
    ln_ready, h_ready, y_ready = sc.sem("ln_ready"), sc.sem("h_ready"), sc.sem("y_ready")
    stats_ready, mom_ready, std_ready = sc.sem("stats_ready"), sc.sem("mom_ready"), sc.sem("std_ready")
    inv_ready, off_ready, u_ready = sc.sem("inv_ready"), sc.sem("off_ready"), sc.sem("u_ready")
    flipped, u_t_ready = sc.sem("flipped"), sc.sem("u_t_ready")
    hid_made, pre_ready, hid_ready = sc.sem("hid_made"), sc.sem("pre_ready"), sc.sem("hid_ready")
    rest_ready, rest_b_ready, out_made, x3_ready = (sc.sem("rest_ready"), sc.sem("rest_b_ready"),
                                                    sc.sem("out_made"), sc.sem("x3_ready"))
    with nc.Block() as block:
        @block.sync
        def _(sp):
            def step(g, k, s):
                if past(g, RING):
                    sp.wait_ge(rest_ready, g - RING + 1)
                    sp.wait_ge(h_ready, g - RING + 1)
                    sp.wait_ge(y_ready, g - RING + 1)
                    sp.sem_inc(sc.ticks, 1)
                sp.dma_start(x[:, s, :, :].rearrange("p t d -> p (t d)"), block_of(x2_v, g)).then_inc(x_in[s], 16)
                sp.dma_start(agg[:, s, :, :].rearrange("p t d -> p (t d)"), block_of(agg_v, g)).then_inc(agg_in[s], 16)
            sweep(sp, groups, step, RING)

        @block.gpsimd
        def _(pool):
            def store(g, s):
                pool.wait_ge(x3_ready, g + 1)
                pool.dma_start(block_of(x3_v, g), x3[:, s, :, :].rearrange("p t d -> p (t d)")).then_inc(x3_out[s], 16)

            def step(g, k, s):
                pool.wait_ge(x_in[s], 16 * (k + 1))
                if past(g, 2):
                    pool.wait_ge(rest_b_ready, g - 1)
                pool.wait_ge(y_ready, g + 1)
                nc.gpsimd.tensor_tensor(rest[:, s % 2, :, :], x[:, s, :, :], y[:, s % 2, :, :],
                                        ALU.add).then_inc(rest_ready, 1)
                pool.wait_ge(rest_ready, g + 1)
                if past(g, 2):
                    pool.wait_ge(x3_ready, g - 1)
                nc.gpsimd.tensor_tensor(rest_b[:, s % 2, :, :], rest[:, s % 2, :, :], c["fb2_row"][:, :, :],
                                        ALU.add).then_inc(rest_b_ready, 1)
                if past(g, 2):
                    store(g - 2, (s - 2) % RING)
            sweep(pool, groups, step, RING)
            store(groups - 2, (groups - 2) % RING)
            store(groups - 1, (groups - 1) % RING)
            for s in range(RING):
                pool.wait_ge(x3_out[s], 16 * rounds_of(groups, s))

        @block.vector
        def _(dve):
            def finish(g, k, s):
                dve.wait_ge(out_made, g + 1)
                dve.wait_ge(rest_b_ready, g + 1)
                if past(g, RING):
                    dve.wait_ge(x3_out[s], 16 * k)
                nc.vector.tensor_scalar(x3[:, s, :, D], isq_all[:, bass.ds(T * g, T)], 0.0, None, ALU.add)
                nc.vector.tensor_tensor(x3[:, s, :, 0:D], p_o[s % 2][:, :, :], rest_b[:, s % 2, :, :],
                                        ALU.add).then_inc(x3_ready, 1)

            def scales(g, s):
                if past(g, 2):
                    dve.wait_ge(h_ready, g - 1)
                nc.vector.tensor_scalar(ln[:, s % 2, 0, :], inv_all[:, bass.ds(T * g, T)], 0.0, None, ALU.add)
                nc.vector.tensor_scalar(ln[:, s % 2, 1, :], off_all[:, bass.ds(T * g, T)], 0.0, None,
                                        ALU.add).then_inc(ln_ready, 1)

            def step(g, k, s):
                if ahead(g, groups):
                    scales(g + 1, (s + 1) % RING)
                dve.wait_ge(h_ready, g + 1)
                dve.wait_ge(agg_in[s], 16 * (k + 1))
                if past(g, 2):
                    dve.wait_ge(rest_ready, g - 1)
                nc.vector.tensor_tensor(y[:, s % 2, :, :], h[:, s % 2, :, :], agg[:, s, :, :], ALU.add).then_inc(y_ready, 1)
                dve.wait_ge(y_ready, g + 1)
                for j in range(T):
                    last = nc.vector.bn_stats(stats[:, s % 2, j, :], y[:, s % 2, j, :])
                last.then_inc(stats_ready, 1)
                dve.wait_ge(stats_ready, g + 1)
                dve.sem_inc(sc.ticks, 1)
                for j in range(T):
                    last = nc.vector.bn_aggr(mom[:, s % 2, j, :], stats[:, s % 2, j, :])
                last.then_inc(mom_ready, 1)
                dve.wait_ge(std_ready, g + 1)
                nc.vector.reciprocal(inv[:, s % 2, :], std[:, s % 2, :]).then_inc(inv_ready, 1)
                dve.wait_ge(inv_ready, g + 1)
                nc.vector.scalar_tensor_tensor(off[:, s % 2, :], mom[:, s % 2, :, 0], -1.0, inv[:, s % 2, :], ALU.mult,
                                               ALU.mult).then_inc(off_ready, 1)
                dve.wait_ge(off_ready, g + 1)
                if past(g, 2):
                    dve.wait_ge(flipped, g - 1)
                for j in range(T):
                    last = nc.vector.tensor_scalar(u[:, s % 2, j, :], y[:, s % 2, j, :], inv[:, s % 2, j:j + 1],
                                                   off[:, s % 2, j:j + 1], ALU.mult, ALU.add)
                last.then_inc(u_ready, 1)
                if past(g, 2):
                    finish(g - 2, *before(k, s, 2))
                if past(g, 1):
                    leak(g - 1, (s - 1) % RING)

            def leak(g, s):
                if past(g, 2):
                    dve.wait_ge(out_made, g - 1)
                for i in range(FC):
                    dve.wait_ge(pre_ready, FC * g + i + 1)
                    nc.vector.scalar_tensor_tensor(hid[:, s % 2, i, :], pre[:, i, :], SLOPE, pre[:, i, :], ALU.mult,
                                                   ALU.max).then_inc(hid_ready, 1)
            scales(0, 0)
            sweep(dve, groups, step, RING)
            leak(groups - 1, (groups - 1) % RING)
            for g in (groups - 2, groups - 1):
                finish(g, g // RING, g % RING)

        @block.scalar
        def _(act):
            def flip_out(g, s):
                act.wait_ge(flipped, g + 1)
                if past(g, 2):
                    act.wait_ge(hid_made, FC * (g - 1))
                nc.scalar.activation(u_t[:, s % 2, :], p_t[:, :], ACT.Identity, scale=c["ln2_g"][:, :],
                                     bias=c["ln2_b"][:, :]).then_inc(u_t_ready, 1)

            def hidden(g, s):
                if past(g, 1):
                    act.wait_ge(hid_ready, FC * g)
                for i in range(FC):
                    act.wait_ge(hid_made, FC * g + i + 1)
                    nc.scalar.activation(pre[:, i, :], p_hid[i][:, :], ACT.Identity,
                                         bias=c["fb1"][:, i:i + 1]).then_inc(pre_ready, 1)

            def rows(g, k, s):
                act.wait_ge(ln_ready, g + 1)
                act.wait_ge(x_in[s], 16 * (k + 1))
                if past(g, 2):
                    act.wait_ge(y_ready, g - 1)
                for j in range(T):
                    last = nc.scalar.activation(h[:, s % 2, j, :], x[:, s, j, :], ACT.Relu, scale=ln[:, s % 2, 0, j:j + 1],
                                                bias=ln[:, s % 2, 1, j:j + 1])
                last.then_inc(h_ready, 1)

            def step(g, k, s):
                if past(g, 1):
                    flip_out(g - 1, (s - 1) % RING)
                if ahead(g, groups):
                    rows(g + 1, *after(k, s))
                act.wait_ge(mom_ready, g + 1)
                nc.scalar.activation(std[:, s % 2, :], mom[:, s % 2, :, 1], ACT.Sqrt,
                                     bias=c["ln_eps"][:, :]).then_inc(std_ready, 1)
                if past(g, 1):
                    hidden(g - 1, (s - 1) % RING)
            rows(0, 0, 0)
            sweep(act, groups, step, RING)
            flip_out(groups - 1, (groups - 1) % RING)
            hidden(groups - 1, (groups - 1) % RING)

        @block.tensor
        def _(pe):
            def outputs(g, s):
                pe.wait_ge(hid_ready, FC * (g + 1))
                if past(g, 2):
                    pe.wait_ge(x3_ready, g - 1)
                for j in range(T):
                    for i in range(FC):
                        last = nc.tensor.matmul(p_o[s % 2][:, j, :], hid[:, s % 2, i, j * P:(j + 1) * P], c["fw2"][:, i, :],
                                                start=(i == 0), stop=(i == FC - 1))
                last.then_inc(out_made, 1)

            def step(g, k, s):
                pe.wait_ge(u_ready, g + 1)
                if past(g, 1):
                    pe.wait_ge(u_t_ready, g)
                for j in range(T):
                    last = nc.tensor.transpose(p_t[:, j * P:(j + 1) * P], u[:, s % 2, j, :], c["ident"][:, :])
                last.then_inc(flipped, 1)
                if past(g, 1):
                    outputs(g - 1, (s - 1) % RING)
                pe.wait_ge(u_t_ready, g + 1)
                if past(g, 1):
                    pe.wait_ge(pre_ready, FC * g)
                for i in range(FC):
                    nc.tensor.matmul(p_hid[i][:, :], c["fw1"][:, i * D:(i + 1) * D], u_t[:, s % 2, :], start=True,
                                     stop=True).then_inc(hid_made, 1)
            sweep(pe, groups, step, RING)
            outputs(groups - 1, (groups - 1) % RING)
    sc.close()


def edges_convolution(nc, c, x3, idx_d, row_d, table, groups, targets_all):
    sc = Scope(nc, "conv")
    K = Keys(sc, "src")
    x_dst = sc.sb("x_dst", [P, 2, T, X3])
    stats = sc.sb("stats", [P, 2, T, 6])
    mom = sc.sb("mom", [P, 2, T, 2])
    std = sc.sb("std", [P, 2, T])
    inv = sc.sb("inv", [P, 2, T])
    scale = sc.sb("scale", [P, 2, T])
    off = sc.sb("off", [P, 2, T])
    val = sc.sb("val", [P, 2, T, D])
    out = sc.sb("out", [P, 2, T, D])
    sums = [sc.ps(f"sums{s}", [P, T, D]) for s in range(2)]
    dst_in = sc.sem2("dst_in")
    stats_ready, mom_ready, std_ready = sc.sem("stats_ready"), sc.sem("mom_ready"), sc.sem("std_ready")
    inv_ready, scale_ready, off_ready = sc.sem("inv_ready"), sc.sem("scale_ready"), sc.sem("off_ready")
    val_ready, summed, out_ready, added = (sc.sem("val_ready"), sc.sem("summed"), sc.sem("out_ready"),
                                           sc.sem("added"))
    with nc.Block() as block:
        @block.sync
        def _(sp):
            def step(g, k, s):
                if past(g, 2):
                    sp.wait_ge(dst_in[s], 16 * T * k)
                    sp.wait_ge(K.same_ready, g - 1)
                    sp.sem_inc(sc.ticks, 1)
                index_loads(sp, K, g, k, s, idx_d, row_d)
            sweep(sp, groups, step)

        @block.gpsimd
        def _(pool):
            def free(g):
                pool.wait_ge(scale_ready, g - 1)
                pool.wait_ge(val_ready, g - 1)
            edge_pool(pool, K, groups, [(x3, x_dst, T, dst_in)], free, table, out, out_ready, added, 3)

        @block.vector
        def _(dve):
            def step(g, k, s):
                dve.wait_ge(dst_in[s], 16 * T * (k + 1))
                for j in range(T):
                    last = nc.vector.bn_stats(stats[:, s, j, :], x_dst[:, s, j, 0:D])
                last.then_inc(stats_ready, 1)
                dve.wait_ge(stats_ready, g + 1)
                dve.sem_inc(sc.ticks, 1)
                for j in range(T):
                    last = nc.vector.bn_aggr(mom[:, s, j, :], stats[:, s, j, :])
                last.then_inc(mom_ready, 1)
                index_work(nc, dve, K, c, g, k, s, summed, targets_all, False)
                if past(g, 1):
                    stage_targets(nc, dve, K, g - 1, 1 - s, targets_all, added, False)
                dve.wait_ge(std_ready, g + 1)
                nc.vector.reciprocal(inv[:, s, :], std[:, s, :]).then_inc(inv_ready, 1)
                dve.wait_ge(inv_ready, g + 1)
                nc.vector.tensor_tensor(scale[:, s, :], inv[:, s, :], x_dst[:, s, :, D], ALU.mult
                                        ).then_inc(scale_ready, 1)
                dve.wait_ge(scale_ready, g + 1)
                nc.vector.scalar_tensor_tensor(off[:, s, :], mom[:, s, :, 0], -1.0, scale[:, s, :], ALU.mult,
                                               ALU.mult).then_inc(off_ready, 1)
            sweep(dve, groups, step)
            stage_targets(nc, dve, K, groups - 1, (groups - 1) % 2, targets_all, added, False)

        @block.scalar
        def _(act):
            def sums_out(g, s):
                act.wait_ge(summed, g + 1)
                if past(g, 2):
                    act.wait_ge(added, 16 * T * (g - 1))
                nc.scalar.activation(out[:, s, :, :], sums[s][:, :, :], ACT.Copy).then_inc(out_ready, 1)

            def step(g, k, s):
                act.wait_ge(mom_ready, g + 1)
                nc.scalar.activation(std[:, s, :], mom[:, s, :, 1], ACT.Sqrt,
                                     bias=c["ln_eps"][:, :]).then_inc(std_ready, 1)
                if past(g, 1):
                    sums_out(g - 1, 1 - s)
                act.wait_ge(off_ready, g + 1)
                if past(g, 2):
                    act.wait_ge(summed, g - 1)
                for j in range(T):
                    last = nc.scalar.activation(val[:, s, j, :], x_dst[:, s, j, 0:D], ACT.Relu,
                                                scale=scale[:, s, j:j + 1], bias=off[:, s, j:j + 1])
                last.then_inc(val_ready, 1)
            sweep(act, groups, step)
            sums_out(groups - 1, (groups - 1) % 2)

        @block.tensor
        def _(pe):
            def step(g, k, s):
                pe.wait_ge(K.same_ready, g + 1)
                pe.wait_ge(val_ready, g + 1)
                if past(g, 2):
                    pe.wait_ge(out_ready, g - 1)
                for j in range(T):
                    last = nc.tensor.matmul(sums[s][:, j, :], K.same[:, s, j, :], val[:, s, j, :], start=True,
                                            stop=True)
                last.then_inc(summed, 1)
            sweep(pe, groups, step)
    sc.close()


def nodes_convolution(nc, c, x3_v, agg_v, out_v, groups):
    sc = Scope(nc, "nconv")
    x = sc.sb("x", [P, RING, T, X3])
    agg = sc.sb("agg", [P, RING, T, D])
    stats = sc.sb("stats", [P, 2, T, 6])
    mom = sc.sb("mom", [P, 2, T, 2])
    std = sc.sb("std", [P, 2, T])
    inv = sc.sb("inv", [P, 2, T])
    scale = sc.sb("scale", [P, 2, T])
    off = sc.sb("off", [P, 2, T])
    own = sc.sb("own", [P, 2, T, D])
    both = sc.sb("both", [P, 2, T, D])
    both_t = sc.sb("both_t", [P, 2, W])
    res = sc.sb("res", [P, RING, T, D])
    p_t = [sc.ps(f"p_t{s}", [P, W]) for s in range(2)]
    p_o = [sc.ps(f"p_o{s}", [P, T, D]) for s in range(2)]
    x_in, agg_in, res_out = sc.sem2("x_in", RING), sc.sem2("agg_in", RING), sc.sem2("res_out", RING)
    stats_ready, mom_ready, std_ready = sc.sem("stats_ready"), sc.sem("mom_ready"), sc.sem("std_ready")
    inv_ready, scale_ready, off_ready = sc.sem("inv_ready"), sc.sem("scale_ready"), sc.sem("off_ready")
    own_ready, both_ready, flipped = sc.sem("own_ready"), sc.sem("both_ready"), sc.sem("flipped")
    both_t_ready, out_made, res_ready = sc.sem("both_t_ready"), sc.sem("out_made"), sc.sem("res_ready")
    with nc.Block() as block:
        @block.sync
        def _(sp):
            def step(g, k, s):
                if past(g, RING):
                    sp.wait_ge(res_ready, g - RING + 1)
                    sp.sem_inc(sc.ticks, 1)
                sp.dma_start(x[:, s, :, :].rearrange("p t d -> p (t d)"), block_of(x3_v, g)).then_inc(x_in[s], 16)
                sp.dma_start(agg[:, s, :, :].rearrange("p t d -> p (t d)"), block_of(agg_v, g)).then_inc(agg_in[s], 16)
            sweep(sp, groups, step, RING)

        @block.gpsimd
        def _(pool):
            def step(g, k, s):
                pool.wait_ge(res_ready, g + 1)
                pool.dma_start(block_of(out_v, g), res[:, s, :, :].rearrange("p t d -> p (t d)")).then_inc(res_out[s], 16)
            sweep(pool, groups, step, RING)
            for s in range(RING):
                pool.wait_ge(res_out[s], 16 * rounds_of(groups, s))

        @block.vector
        def _(dve):
            def back(g, k, s):
                dve.wait_ge(own_ready, g + 1)
                dve.wait_ge(agg_in[s], 16 * (k + 1))
                if past(g, 2):
                    dve.wait_ge(flipped, g - 1)
                nc.vector.tensor_tensor(both[:, s % 2, :, :], agg[:, s, :, :], own[:, s % 2, :, :],
                                        ALU.add).then_inc(both_ready, 1)

            def finish(g, k, s):
                dve.wait_ge(out_made, g + 1)
                if past(g, RING):
                    dve.wait_ge(res_out[s], 16 * k)
                for j in range(T):
                    last = nc.vector.scalar_tensor_tensor(res[:, s, j, :], p_o[s % 2][:, j, :], x[:, s, j, D:D + 1],
                                                          x[:, s, j, 0:D], ALU.mult, ALU.add)
                last.then_inc(res_ready, 1)

            def step(g, k, s):
                dve.wait_ge(x_in[s], 16 * (k + 1))
                for j in range(T):
                    last = nc.vector.bn_stats(stats[:, s % 2, j, :], x[:, s, j, 0:D])
                last.then_inc(stats_ready, 1)
                dve.wait_ge(stats_ready, g + 1)
                dve.sem_inc(sc.ticks, 1)
                for j in range(T):
                    last = nc.vector.bn_aggr(mom[:, s % 2, j, :], stats[:, s % 2, j, :])
                last.then_inc(mom_ready, 1)
                if past(g, 1):
                    back(g - 1, *before(k, s, 1))
                if past(g, 2):
                    finish(g - 2, *before(k, s, 2))
                dve.wait_ge(std_ready, g + 1)
                nc.vector.reciprocal(inv[:, s % 2, :], std[:, s % 2, :]).then_inc(inv_ready, 1)
                dve.wait_ge(inv_ready, g + 1)
                nc.vector.tensor_tensor(scale[:, s % 2, :], inv[:, s % 2, :], x[:, s, :, D], ALU.mult
                                        ).then_inc(scale_ready, 1)
                dve.wait_ge(scale_ready, g + 1)
                nc.vector.scalar_tensor_tensor(off[:, s % 2, :], mom[:, s % 2, :, 0], -1.0, scale[:, s % 2, :], ALU.mult,
                                               ALU.mult).then_inc(off_ready, 1)
            sweep(dve, groups, step, RING)
            back(groups - 1, (groups - 1) // RING, (groups - 1) % RING)
            finish(groups - 2, (groups - 2) // RING, (groups - 2) % RING)
            finish(groups - 1, (groups - 1) // RING, (groups - 1) % RING)

        @block.scalar
        def _(act):
            def step(g, k, s):
                act.wait_ge(mom_ready, g + 1)
                nc.scalar.activation(std[:, s % 2, :], mom[:, s % 2, :, 1], ACT.Sqrt,
                                     bias=c["ln_eps"][:, :]).then_inc(std_ready, 1)
                act.wait_ge(off_ready, g + 1)
                if past(g, 2):
                    act.wait_ge(both_ready, g - 1)
                for j in range(T):
                    last = nc.scalar.activation(own[:, s % 2, j, :], x[:, s, j, 0:D], ACT.Relu,
                                                scale=scale[:, s % 2, j:j + 1], bias=off[:, s % 2, j:j + 1])
                last.then_inc(own_ready, 1)
                if past(g, 1):
                    flip_out(g - 1, (s - 1) % RING)

            def flip_out(g, s):
                act.wait_ge(flipped, g + 1)
                if past(g, 2):
                    act.wait_ge(out_made, g - 1)
                nc.scalar.activation(both_t[:, s % 2, :], p_t[s % 2][:, :], ACT.Copy).then_inc(both_t_ready, 1)
            sweep(act, groups, step, RING)
            flip_out(groups - 1, (groups - 1) % RING)

        @block.tensor
        def _(pe):
            def step(g, k, s):
                pe.wait_ge(both_ready, g + 1)
                if past(g, 2):
                    pe.wait_ge(both_t_ready, g - 1)
                for j in range(T):
                    last = nc.tensor.transpose(p_t[s % 2][:, j * P:(j + 1) * P], both[:, s % 2, j, :], c["ident"][:, :])
                last.then_inc(flipped, 1)
                pe.wait_ge(both_t_ready, g + 1)
                if past(g, 2):
                    pe.wait_ge(res_ready, g - 1)
                for j in range(T):
                    last = nc.tensor.matmul(p_o[s % 2][:, j, :], both_t[:, s % 2, j * P:(j + 1) * P], c["w3"][:, :],
                                            start=True, stop=True)
                last.then_inc(out_made, 1)
            sweep(pe, groups, step, RING)
    sc.close()


def build(nc, a):
    n_nodes, n_edges = a["x"].shape[0], a["idx"].shape[0] * W
    NG, EG = n_nodes // W, n_edges // W
    table_rows = n_nodes + P
    ctx = ExitStack()

    def sb(name, shape, dt=fp32):
        return ctx.enter_context(nc.sbuf_tensor(name, shape, dt))

    def dram(name, shape):
        return nc.dram_tensor(name, shape, fp32, kind="Internal").ap()

    def groups_of(t, rows):
        return t[0:rows, :].rearrange("(g p t) d -> g p (t d)", p=P, t=T)

    with ctx:
        agg0 = dram("agg0", (table_rows, A0))
        clear_rows = -(-n_nodes // EG // P) * P
        agg = [dram(f"agg{i}", (max(table_rows, clear_rows * EG), D)) for i in (1, 2, 3)]
        x1, x2, x3 = dram("x1", (n_nodes, D)), dram("x2", (n_nodes, D)), dram("x3", (n_nodes, X3))

        c = {}
        loads = []
        for name, shape, src in (
                ("ident", [P, P], a["ident"]), ("below", [P, P], a["below"]), ("spare", [P, 1], a["spare"]),
                ("one", [P, 1], a["one"]),
                ("beta", [P, 1], a["beta"].partition_broadcast(P)),
                ("m1_src", [P, D], a["m1"][0:D, :]), ("m1_dst", [P, D], a["m1"][D:2 * D, :]),
                ("m1_attr", [D4, D], a["m1"][2 * D:2 * D + D4, :]),
                ("mb1", [P, 1], a["mb1"]), ("mb2_row", [P, W], a["mb2_row"].partition_broadcast(P)),
                ("gb_z", [P, 1], a["gb_z"]), ("gb_r", [P, 1], a["gb_r"]), ("gb_h", [P, 1], a["gb_h"]),
                ("ln1_g", [P, 1], a["ln1_g"]), ("ln1_b", [P, 1], a["ln1_b"]),
                ("ln2_g", [P, 1], a["ln2_g"]), ("ln2_b", [P, 1], a["ln2_b"]),
                ("cw1_dst", [P, F], a["cw1"][0:D, :]), ("cw1_src", [P, F], a["cw1"][D:2 * D, :]),
                ("cw1_attr", [D64, F], a["cw1"][2 * D:2 * D + D64, :]),
                ("cb1", [P, FC], a["cb1"]), ("cb2_row", [P, W], a["cb2_row"].partition_broadcast(P)),
                ("fw1", [P, F], a["fw1"]), ("fb1", [P, FC], a["fb1"]),
                ("fb2_row", [P, W], a["fb2_row"].partition_broadcast(P)), ("w3", [P, D], a["w3"])):
            t = sb(name, shape)
            loads.append((t[:, :], src))
            c[name] = t
        for name, chunks, src in (("m2", 1, a["m2"]), ("gw_z", 2, a["gw_z"]), ("gw_r", 2, a["gw_r"]),
                                  ("gw_h", 2, a["gw_h"]), ("cw2", FC, a["cw2"]), ("fw2", FC, a["fw2"])):
            t = sb(name, [P, chunks, D])
            loads.append((t[:, :, :], src.rearrange("(c k) n -> k c n", k=P)))
            c[name] = t
        for name in ("mb2_row", "cb2_row", "fb2_row"):
            c[name] = c[name][:, :].rearrange("p (t d) -> p t d", t=T)
        c["zero"] = sb("zero", [P, clear_rows * D // P])
        for name in ("ln_eps", "shift", "lead", "w_self"):
            c[name] = sb(name, [P, 1])
        targets_src = sb("targets_src", [P, T * EG], int32)
        targets_dst = sb("targets_dst", [P, T * EG], int32)
        isq_all = sb("isq_all", [P, T * NG])
        mom_all = sb("mom_all", [P, T * NG, 2])
        inv_all = sb("inv_all", [P, T * NG])
        off_all = sb("off_all", [P, T * NG])

        beyond = clear_rows * EG
        setup(nc, c, loads, [agg0] + [t[beyond:, :] for t in agg if t.shape[0] > beyond], c["beta"])
        clears = [t[0:clear_rows * EG, :].rearrange("(g p r) d -> g p (r d)", g=EG, p=P) for t in agg]
        edges_attention(nc, c, a["x"], a["idx"], a["src_row"], agg0, EG, targets_src, clears)
        nodes_attention(nc, c, groups_of(a["x"], n_nodes), groups_of(agg0, n_nodes), groups_of(x1, n_nodes), NG,
                        isq_all, mom_all)
        ln_of_all(nc, c, 1, mom_all, inv_all, off_all)
        edges_message(nc, c, x1, a["idx"], a["dst_row"], a["attr4"], agg[0], EG, targets_dst, 1)
        nodes_gated(nc, c, groups_of(x1, n_nodes), groups_of(agg[0], n_nodes), groups_of(x2, n_nodes), NG,
                    inv_all, off_all, mom_all)
        ln_of_all(nc, c, 2, mom_all, inv_all, off_all)
        edges_message(nc, c, x2, a["idx"], a["dst_row"], a["attr64"], agg[1], EG, targets_dst, 2)
        nodes_feedforward(nc, c, groups_of(x2, n_nodes), groups_of(agg[1], n_nodes), groups_of(x3, n_nodes), NG,
                          inv_all, off_all, isq_all)
        edges_convolution(nc, c, x3, a["idx"], a["src_row"], agg[2], EG, targets_src)
        nodes_convolution(nc, c, groups_of(x3, n_nodes), groups_of(agg[2], n_nodes), groups_of(a["out"], n_nodes), NG)


def kernel(x, src, dst, edge_attr_4, edge_attr_64, L0_gnn_beta, L1_gnn_W_msg1, L1_gnn_b_msg1, L1_gnn_W_msg2,
           L1_gnn_b_msg2, L1_gnn_W_z, L1_gnn_b_z, L1_gnn_W_r, L1_gnn_b_r, L1_gnn_W_h, L1_gnn_b_h, L2_gnn_ln1_g,
           L2_gnn_ln1_b, L2_gnn_ln2_g, L2_gnn_ln2_b, L2_gnn_conv_w1, L2_gnn_conv_b1, L2_gnn_conv_w2,
           L2_gnn_conv_b2, L2_gnn_ff_w1, L2_gnn_ff_b1, L2_gnn_ff_w2, L2_gnn_ff_b2, L3_gnn_W):
    import numpy as np
    import concourse.bacc as bacc
    from concourse.bass_utils import run_bass_kernel_spmd

    x, src, dst = np.asarray(x), np.asarray(src), np.asarray(dst)
    N, E = x.shape[0], src.shape[0]
    extra_edges = -E % W
    extra_nodes = -N % W
    if extra_edges and not extra_nodes:
        extra_nodes = W
    own = (N + np.arange(extra_edges) % max(extra_nodes, 1)).astype(src.dtype)

    def more(v, n):
        return np.concatenate([v, v[:n]]) if n else v

    def column(v):
        return np.asarray(v).reshape(-1, D).T

    def row4(v):
        return np.tile(np.asarray(v), T)

    def edge_columns(v):
        v = more(np.asarray(v), extra_edges)
        return v.reshape(-1, W, v.shape[1]).transpose(0, 2, 1)

    xp = more(x, extra_nodes)
    src, dst = np.concatenate([src, own]), np.concatenate([dst, own])
    ends = np.stack([src.reshape(-1, T, P), dst.reshape(-1, T, P)], axis=1)
    arrays = {
        "x": xp, "idx": ends.transpose(0, 3, 1, 2).reshape(-1, P, 2 * T),
        "src_row": src.reshape(-1, W), "dst_row": dst.reshape(-1, W),
        "attr4": edge_columns(edge_attr_4), "attr64": edge_columns(edge_attr_64),
        "beta": np.asarray(L0_gnn_beta),
        "m1": L1_gnn_W_msg1, "mb1": column(L1_gnn_b_msg1), "m2": L1_gnn_W_msg2, "mb2_row": row4(L1_gnn_b_msg2),
        "gw_z": L1_gnn_W_z, "gw_r": L1_gnn_W_r, "gw_h": L1_gnn_W_h,
        "gb_z": column(L1_gnn_b_z), "gb_r": column(L1_gnn_b_r), "gb_h": column(L1_gnn_b_h),
        "ln1_g": column(L2_gnn_ln1_g), "ln1_b": column(L2_gnn_ln1_b),
        "ln2_g": column(L2_gnn_ln2_g), "ln2_b": column(L2_gnn_ln2_b),
        "cw1": L2_gnn_conv_w1, "cb1": column(L2_gnn_conv_b1), "cw2": L2_gnn_conv_w2, "cb2_row": row4(L2_gnn_conv_b2),
        "fw1": L2_gnn_ff_w1, "fb1": column(L2_gnn_ff_b1), "fw2": L2_gnn_ff_w2, "fb2_row": row4(L2_gnn_ff_b2),
        "w3": np.asarray(L3_gnn_W).T,
        "ident": np.eye(P, dtype=np.float32), "below": np.tril(np.ones((P, P), np.float32), -1),
        "spare": (xp.shape[0] + np.arange(P, dtype=np.float32)).reshape(P, 1), "one": np.ones((P, 1), np.float32),
    }
    nc = bacc.Bacc("TRN2", target_bir_lowering=False, num_devices=1)
    feeds, aps = {}, {}
    for name, v in arrays.items():
        v = np.ascontiguousarray(v)
        feeds[f"in_{name}"] = v
        aps[name] = nc.dram_tensor(f"in_{name}", v.shape, mybir.dt.from_np(v.dtype), kind="ExternalInput").ap()
    aps["out"] = nc.dram_tensor("out_rows", xp.shape, fp32, kind="ExternalOutput").ap()
    build(nc, aps)
    run = run_bass_kernel_spmd(nc, [feeds], core_ids=[0])
    return run.results[0]["out_rows"][:N]
```

```python
import concourse.bass as bass
from concourse import mybir
from contextlib import ExitStack


P = 128
T = 4
D = 128
W = T * P
F = 3 * D
FC = F // D
D4 = 4
D64 = 64
A0 = D + 2
X1 = D + 2
X2 = D + 4
X3 = D + 3
LN_EPS = 1e-5
SLOPE = 0.01
HEAD = 6
SET = 2
ZEROS = 4
RING = 6

fp32 = mybir.dt.float32
int32 = mybir.dt.int32
ALU = mybir.AluOpType
ACT = mybir.ActivationFunctionType


def past(g, back):
    return not isinstance(g, int) or g >= back


def sweep(eng, groups, step, ring=2, lead=1):
    head = -(-HEAD // ring)
    for g in range(ring * head):
        step(g, g // ring, g % ring)
    rounds = (groups - lead) // ring
    with eng.Fori(head, rounds) as k:
        for s in range(ring):
            step(ring * k + s, k, s)
    for g in range(ring * rounds, groups):
        step(g, g // ring, g % ring)


def before(k, s, n):
    return (k - 1 if s < n else k), (s - n) % RING


def after(k, s, n=1):
    return (k + 1 if s + n >= RING else k), (s + n) % RING


def ahead(g, groups, n=1):
    return not isinstance(g, int) or g + n < groups


def rounds_of(groups, s):
    return (groups + RING - 1 - s) // RING


def block_of(view, g):
    return view[bass.ds(g, 1), :, :].rearrange("o p f -> (o p) f")


class Scope:

    def __init__(self, nc, tag):
        self.nc, self.tag, self.ctx, self.sems = nc, tag, ExitStack(), []
        self.ticks = self.sem("ticks")

    def sb(self, name, shape, dt=fp32):
        return self.ctx.enter_context(self.nc.sbuf_tensor(f"{self.tag}_{name}", shape, dt))

    def ps(self, name, shape):
        return self.ctx.enter_context(self.nc.psum_tensor(f"{self.tag}_{name}", shape, fp32))

    def sem(self, name):
        s = self.nc.alloc_semaphore(f"{self.tag}_{name}")
        self.sems.append(s)
        return s

    def sem2(self, name, n=2):
        return [self.sem(f"{name}{s}") for s in range(n)]

    def close(self):
        self.ctx.close()
        self.nc.clear_and_free_semaphores(self.sems)
        self.nc.all_engine_barrier()


def setup(nc, c, loads, beta_col):
    sc = Scope(nc, "setup")
    loaded = sc.sem("loaded")
    shift_ready = sc.sem("shift_ready")
    lead_ready = sc.sem("lead_ready")
    with nc.Block() as block:
        @block.scalar
        def _(act):
            for dst, src in loads:
                act.dma_start(dst, src).then_inc(loaded, 16)
            act.wait_ge(loaded, 16 * len(loads))
            act.wait_ge(lead_ready, 1)
            nc.scalar.activation(c["w_self"][:, :], c["lead"][:, :], ACT.Exp)

        @block.vector
        def _(dve):
            nc.vector.memset(c["zero"][:, :], 0.0)
            nc.vector.memset(c["ln_eps"][:, :], LN_EPS)
            nc.vector.memset(c["one"][:, :], 1.0)
            nc.vector.memset(c["power"][:, :], -0.5)
            dve.wait_ge(loaded, 16 * len(loads))
            nc.vector.tensor_scalar_max(c["shift"][:, :], beta_col[:, :], 0.0).then_inc(shift_ready, 1)
            dve.wait_ge(shift_ready, 1)
            nc.vector.tensor_tensor(c["lead"][:, :], beta_col[:, :], c["shift"][:, :],
                                    ALU.subtract).then_inc(lead_ready, 1)
    sc.close()


class Keys:

    def __init__(self, sc, which):
        self.which = which
        self.ticks = sc.ticks
        self.idx = sc.sb("idx", [P, 2, 2 * T], int32)
        self.row = sc.sb("row", [P, 2, W], int32)
        self.same = sc.sb("same", [P, 2, T, SET * P])
        self.junk = sc.sb("junk", [P, 2, T, SET * P])
        self.earlier = sc.sb("earlier", [P, 2, T])
        self.away = sc.sb("away", [P, 2, T])
        self.moved = sc.sb("moved", [P, 2, T])
        self.target = sc.sb("target", [P, 2, T], int32)
        self.idx_in = sc.sem2("idx_in")
        self.row_in = sc.sem2("row_in")
        self.same_ready = sc.sem("same_ready")
        self.earlier_ready = sc.sem("earlier_ready")
        self.away_ready = sc.sem("away_ready")
        self.moved_ready = sc.sem("moved_ready")
        self.saved = sc.sem("saved")
        self.target_ready = sc.sem("target_ready")

    def set_of(self, j):
        return range(j - j % SET, j - j % SET + SET)

    def key(self, s, j):
        at = j if self.which == "src" else T + j
        return self.idx[:, s, at:at + 1]

    def keys(self, s):
        at = 0 if self.which == "src" else T
        return self.idx[:, s, at:at + T]


def index_loads(sp, K, g, k, s, idx_d, row_d):
    sp.dma_start(K.idx[:, s, :], block_of(idx_d, g)).then_inc(K.idx_in[s], 16)
    sp.dma_start(K.row[:, s, :], row_d[bass.ds(g, 1), :].partition_broadcast(P)
                 .rearrange("p o f -> p (o f)")).then_inc(K.row_in[s], 16)


def index_work(nc, dve, K, c, g, k, s, summed, targets_all, make):
    dve.wait_ge(K.idx_in[s], 16 * (k + 1))
    dve.wait_ge(K.row_in[s], 16 * (k + 1))
    if past(g, 2):
        dve.wait_ge(summed, g - 1)
    for j in range(T):
        last = nc.vector.tensor_scalar(K.same[:, s, j, :], K.row[:, s, K.set_of(j)[0] * P:(K.set_of(j)[-1] + 1) * P],
                                       K.key(s, j), None,
                                       ALU.is_equal)
    last.then_inc(K.same_ready, 1)
    if not make:
        return
    dve.wait_ge(K.same_ready, g + 1)
    for j in range(T):
        last = nc.vector.tensor_tensor_reduce(
            out=K.junk[:, s, j, :], in0=K.same[:, s, j, :], in1=c["below"][:, j % SET, 0:SET * P],
            scale=1.0, scalar=0.0,
            op0=ALU.mult, op1=ALU.add, accum_out=K.earlier[:, s, j:j + 1])
    last.then_inc(K.earlier_ready, 1)
    nc.vector.scalar_tensor_tensor(K.away[:, s, :], K.keys(s), -1.0, c["spare"][:, :], ALU.mult,
                                   ALU.add).then_inc(K.away_ready, 1)
    dve.wait_ge(K.earlier_ready, g + 1)
    dve.wait_ge(K.away_ready, g + 1)
    nc.vector.scalar_tensor_tensor(K.moved[:, s, :], K.earlier[:, s, :], 0.0, K.away[:, s, :], ALU.is_gt,
                                   ALU.mult).then_inc(K.moved_ready, 1)
    dve.wait_ge(K.moved_ready, g + 1)
    nc.vector.tensor_tensor(targets_all[:, bass.ds(T * g, T)], K.moved[:, s, :], K.keys(s),
                            ALU.add).then_inc(K.saved, 1)


def sum_equal_keys(nc, K, s, sums, columns, rows):
    for j in range(T):
        first, last = K.set_of(j)[0], K.set_of(j)[-1]
        for i in K.set_of(j):
            product = nc.tensor.matmul(sums[:, j, 0:columns], K.same[:, s, i, (j - first) * P:(j - first + 1) * P],
                                       rows[:, s, i, :], start=(i == first), stop=(i == last))
    return product


def stage_targets(nc, dve, K, g, s, targets_all, added, make):
    if make:
        dve.wait_ge(K.saved, g + 1)
    if past(g, 2):
        dve.wait_ge(added, 16 * T * (g - 1))
    nc.vector.tensor_scalar(K.target[:, s, :], targets_all[:, bass.ds(T * g, T)], 0.0, None,
                            ALU.add).then_inc(K.target_ready, 1)


def add_rows(pool, K, table, out, out_ready, added, g, s, j):
    chained = j % SET == 0 and (not isinstance(g, int) or T * g + j > 0)
    if j == 0:
        pool.wait_ge(K.target_ready, g + 1)
        pool.wait_ge(out_ready, g + 1)
    if chained:
        pool.wait_ge(added, 16 * (T * g + j))
        pool.sem_inc(K.ticks, 1)
    pool.indirect_dma_start(table[:, :], bass.IndirectOffsetOnAxis(ap=K.target[:, s, j:j + 1], axis=0),
                            out[:, s, j, :], None, compute_op=ALU.add).then_inc(added, 16)


def edge_pool(pool, K, groups, gathers, free, table, out, out_ready, added, lag, table_clear=None):
    def step(g, k, s):
        if isinstance(g, int) and g == lag and table_clear:
            pool.wait_ge(*table_clear)
        pool.wait_ge(K.idx_in[s], 16 * (k + 1))
        if past(g, 2):
            free(g)
            pool.sem_inc(K.ticks, 1)
        for first in range(0, T, SET):
            if past(g, lag):
                for j in range(first, first + SET):
                    add_rows(pool, K, table, out, out_ready, added, g - lag, (s + lag) % 2, j)
            for j in range(first, first + SET):
                for source, rows, at, landed in gathers:
                    pool.indirect_dma_start(
                        rows[:, s, j, :], None, source[:, :],
                        bass.IndirectOffsetOnAxis(ap=K.idx[:, s, at + j:at + j + 1], axis=0)
                    ).then_inc(landed[s], 16)

    sweep(pool, groups, step)
    for g in range(groups - lag, groups):
        for j in range(T):
            add_rows(pool, K, table, out, out_ready, added, g, g % 2, j)
    pool.wait_ge(added, 16 * T * groups)


def edges_attention(nc, c, x, idx_d, row_d, table, groups, targets_all, own_clears, clears, weights_in):
    sc = Scope(nc, "att")
    K = Keys(sc, "src")
    x_src = sc.sb("x_src", [P, 2, T, D])
    x_dst = sc.sb("x_dst", [P, 2, T, D])
    h = sc.sb("h", [P, 2, 2 * T, D])
    stats = sc.sb("stats", [P, 2, 2 * T, 6])
    mom = sc.sb("mom", [P, 2, 2 * T, 2])
    std = sc.sb("std", [P, 2, 2 * T])
    inv = sc.sb("inv", [P, 2, 2 * T])
    off = sc.sb("off", [P, 2, 2 * T])
    sq = sc.sb("sq", [P, 2, 2 * T])
    sq_junk = sc.sb("sq_junk", [P, 2, 2 * T, D])
    dot_junk = sc.sb("dot_junk", [P, 2, T, D])
    dot = sc.sb("dot", [P, 2, T])
    norm2 = sc.sb("norm2", [P, 2, T])
    norm = sc.sb("norm", [P, 2, T])
    rnorm = sc.sb("rnorm", [P, 2, T])
    cos = sc.sb("cos", [P, 2, T])
    score = sc.sb("score", [P, 2, T])
    val = sc.sb("val", [P, 2, T, A0])
    out = sc.sb("out", [P, 2, T, A0])
    sums = [sc.ps(f"sums{s}", [P, T, 256]) for s in range(2)]
    src_in, dst_in = sc.sem2("src_in"), sc.sem2("dst_in")
    own_cleared, cleared, loaded = sc.sem("own_cleared"), sc.sem("cleared"), sc.sem("loaded")
    ones_ready = sc.sem("ones_ready")
    stats_ready, mom_ready, std_ready = sc.sem("stats_ready"), sc.sem("mom_ready"), sc.sem("std_ready")
    inv_ready, off_ready = sc.sem("inv_ready"), sc.sem("off_ready")
    h_ready, sq_ready, dot_ready = sc.sem("h_ready"), sc.sem("sq_ready"), sc.sem("dot_ready")
    norm2_ready, norm_ready, rnorm_ready = sc.sem("norm2_ready"), sc.sem("norm_ready"), sc.sem("rnorm_ready")
    cos_ready, score_ready = sc.sem("cos_ready"), sc.sem("score_ready")
    weight_ready, val_ready = sc.sem("weight_ready"), sc.sem("val_ready")
    summed, out_ready, added = sc.sem("summed"), sc.sem("out_ready"), sc.sem("added")

    with nc.Block() as block:
        @block.sync
        def _(sp):
            def step(g, k, s):
                if past(g, 2):
                    sp.wait_ge(src_in[s], 16 * T * k)
                    sp.wait_ge(dst_in[s], 16 * T * k)
                    sp.wait_ge(K.same_ready, g - 1)
                    sp.wait_ge(K.saved, g - 1)
                    sp.sem_inc(sc.ticks, 1)
                index_loads(sp, K, g, k, s, idx_d, row_d)
                sp.dma_start(block_of(clears, g), c["zero"][:, 0:clears.shape[2]]).then_inc(cleared, 16)
            sweep(sp, groups, step)
            for dst, src in weights_in:
                sp.dma_start(dst, src).then_inc(loaded, 16)
            sp.wait_ge(cleared, 16 * groups)
            sp.wait_ge(loaded, 16 * len(weights_in))

        @block.gpsimd
        def _(pool):
            def free(g):
                pool.wait_ge(mom_ready, g - 1)
                pool.wait_ge(h_ready, g - 1)
            edge_pool(pool, K, groups, [(x, x_src, 0, src_in), (x, x_dst, T, dst_in)], free, table, out,
                      out_ready, added, 4, (own_cleared, 16 * len(own_clears)))

        @block.vector
        def _(dve):
            for s in range(2):
                last = nc.vector.memset(val[:, s, :, D + 1:D + 2], 1.0)
            last.then_inc(ones_ready, 1)

            def back(g, s):
                dve.wait_ge(h_ready, g + 1)
                for j in range(T):
                    last = nc.vector.tensor_tensor_reduce(
                        out=dot_junk[:, s, j, :], in0=h[:, s, j, :], in1=h[:, s, T + j, :], scale=1.0, scalar=0.0,
                        op0=ALU.mult, op1=ALU.add, accum_out=dot[:, s, j:j + 1])
                last.then_inc(dot_ready, 1)
                dve.wait_ge(sq_ready, g + 1)
                nc.vector.tensor_tensor(norm2[:, s, :], sq[:, s, 0:T], sq[:, s, T:2 * T],
                                        ALU.mult).then_inc(norm2_ready, 1)

            def scores(g, s):
                dve.wait_ge(norm_ready, g + 1)
                nc.vector.reciprocal(rnorm[:, s, :], norm[:, s, :]).then_inc(rnorm_ready, 1)
                dve.wait_ge(rnorm_ready, g + 1)
                dve.wait_ge(dot_ready, g + 1)
                nc.vector.tensor_tensor(cos[:, s, :], dot[:, s, :], rnorm[:, s, :], ALU.mult).then_inc(cos_ready, 1)
                dve.wait_ge(cos_ready, g + 1)
                nc.vector.tensor_scalar(score[:, s, :], cos[:, s, :], c["beta"][:, :], c["shift"][:, :],
                                        ALU.mult, ALU.subtract).then_inc(score_ready, 1)

            def step(g, k, s):
                if past(g, 1):
                    back(g - 1, 1 - s)
                dve.wait_ge(src_in[s], 16 * T * (k + 1))
                dve.wait_ge(dst_in[s], 16 * T * (k + 1))
                for j in range(T):
                    nc.vector.bn_stats(stats[:, s, j, :], x_src[:, s, j, :])
                    last = nc.vector.bn_stats(stats[:, s, T + j, :], x_dst[:, s, j, :])
                last.then_inc(stats_ready, 1)
                dve.wait_ge(stats_ready, g + 1)
                dve.sem_inc(sc.ticks, 1)
                for j in range(2 * T):
                    last = nc.vector.bn_aggr(mom[:, s, j, :], stats[:, s, j, :])
                last.then_inc(mom_ready, 1)
                dve.wait_ge(std_ready, g + 1)
                nc.vector.reciprocal(inv[:, s, :], std[:, s, :]).then_inc(inv_ready, 1)
                dve.wait_ge(inv_ready, g + 1)
                nc.vector.scalar_tensor_tensor(off[:, s, :], mom[:, s, :, 0], -1.0, inv[:, s, :], ALU.mult,
                                               ALU.mult).then_inc(off_ready, 1)
                if past(g, 1):
                    scores(g - 1, 1 - s)
                index_work(nc, dve, K, c, g, k, s, summed, targets_all, True)
                if past(g, 2):
                    stage_targets(nc, dve, K, g - 2, s, targets_all, added, True)
            sweep(dve, groups, step)
            back(groups - 1, (groups - 1) % 2)
            scores(groups - 1, (groups - 1) % 2)
            for g in (groups - 2, groups - 1):
                stage_targets(nc, dve, K, g, g % 2, targets_all, added, True)

        @block.scalar
        def _(act):
            for part, zeros in own_clears:
                act.dma_start(part, zeros).then_inc(own_cleared, 16)
            act.wait_ge(ones_ready, 1)

            def norms(g, s):
                act.wait_ge(norm2_ready, g + 1)
                nc.scalar.activation(norm[:, s, :], norm2[:, s, :], ACT.Sqrt).then_inc(norm_ready, 1)

            def weights(g, s):
                act.wait_ge(score_ready, g + 1)
                if past(g, 2):
                    act.wait_ge(summed, g - 1)
                nc.scalar.activation(val[:, s, :, D], score[:, s, :], ACT.Exp).then_inc(weight_ready, 1)
                act.wait_ge(weight_ready, g + 1)
                for j in range(T):
                    last = nc.scalar.activation(val[:, s, j, 0:D], h[:, s, T + j, :], ACT.Copy,
                                                scale=val[:, s, j, D:D + 1])
                last.then_inc(val_ready, 1)

            def sums_out(g, s):
                act.wait_ge(summed, g + 1)
                if past(g, 2):
                    act.wait_ge(added, 16 * T * (g - 1))
                nc.scalar.activation(out[:, s, :, :], sums[s][:, :, 0:A0], ACT.Copy).then_inc(out_ready, 1)

            def step(g, k, s):
                act.wait_ge(mom_ready, g + 1)
                nc.scalar.activation(std[:, s, :], mom[:, s, :, 1], ACT.Sqrt,
                                     bias=c["ln_eps"][:, :]).then_inc(std_ready, 1)
                if past(g, 1):
                    norms(g - 1, 1 - s)
                act.wait_ge(off_ready, g + 1)
                if past(g, 2):
                    act.wait_ge(dot_ready, g - 1)
                for j in range(T):
                    nc.scalar.activation(h[:, s, j, :], x_src[:, s, j, :], ACT.Relu,
                                         scale=inv[:, s, j:j + 1], bias=off[:, s, j:j + 1])
                    last = nc.scalar.activation(h[:, s, T + j, :], x_dst[:, s, j, :], ACT.Relu,
                                                scale=inv[:, s, T + j:T + j + 1], bias=off[:, s, T + j:T + j + 1])
                last.then_inc(h_ready, 1)
                if past(g, 2):
                    sums_out(g - 2, s)
                act.wait_ge(h_ready, g + 1)
                for j in range(2 * T):
                    last = nc.scalar.activation(sq_junk[:, s, j, :], h[:, s, j, :], ACT.Square,
                                                accum_out=sq[:, s, j:j + 1])
                last.then_inc(sq_ready, 1)
                if past(g, 1):
                    weights(g - 1, 1 - s)
            sweep(act, groups, step)
            sums_out(groups - 2, (groups - 2) % 2)
            norms(groups - 1, (groups - 1) % 2)
            weights(groups - 1, (groups - 1) % 2)
            sums_out(groups - 1, (groups - 1) % 2)

        @block.tensor
        def _(pe):
            def step(g, k, s):
                pe.wait_ge(K.same_ready, g + 1)
                pe.wait_ge(val_ready, g + 1)
                if past(g, 2):
                    pe.wait_ge(out_ready, g - 1)
                sum_equal_keys(nc, K, s, sums[s], A0, val).then_inc(summed, 1)
            sweep(pe, groups, step)
    sc.close()


def nodes_attention(nc, c, x_v, agg_v, x1_v, groups, isq_all):
    sc = Scope(nc, "natt")
    x = sc.sb("x", [P, RING, T, D])
    agg = sc.sb("agg", [P, RING, T, A0])
    h = sc.sb("h", [P, 2, T, D])
    num = sc.sb("num", [P, 2, T, D])
    mean = sc.sb("mean", [P, 2, T, D])
    x1 = sc.sb("x1", [P, RING, T, X1])
    stats = sc.sb("stats", [P, 2, T, 6])
    stats1 = sc.sb("stats1", [P, 2, T, 6])
    mom = sc.sb("mom", [P, 2, T, 2])
    mom1 = sc.sb("mom1", [P, 2, T, 2])
    scale = sc.sb("scale", [P, 2, T])
    std = sc.sb("std", [P, 2, T])
    std1 = sc.sb("std1", [P, 2, T])
    sdeg = sc.sb("sdeg", [P, 2, T])
    isq = sc.sb("isq", [P, 2, T])
    inv = sc.sb("inv", [P, 2, T])
    off = sc.sb("off", [P, 2, T])
    den = sc.sb("den", [P, 2, T])
    rden = sc.sb("rden", [P, RING, T])
    x_in, agg_in, x1_out = sc.sem2("x_in", RING), sc.sem2("agg_in", RING), sc.sem2("x1_out", RING)
    stats_ready, mom_ready, scale_ready = sc.sem("stats_ready"), sc.sem("mom_ready"), sc.sem("scale_ready")
    inv_ready, off_ready, h_ready = sc.sem("inv_ready"), sc.sem("off_ready"), sc.sem("h_ready")
    den_ready, rden_ready, num_ready = sc.sem("den_ready"), sc.sem("rden_ready"), sc.sem("num_ready")
    std_ready, std1_ready, sdeg_ready = sc.sem("std_ready"), sc.sem("std1_ready"), sc.sem("sdeg_ready")
    kept, mean_ready = sc.sem("kept"), sc.sem("mean_ready")
    isq_ready, sum_ready, inv1_ready = sc.sem("isq_ready"), sc.sem("sum_ready"), sc.sem("inv1_ready")
    x1_ready, stats1_ready, mom1_ready = sc.sem("x1_ready"), sc.sem("stats1_ready"), sc.sem("mom1_ready")
    with nc.Block() as block:
        @block.sync
        def _(sp):
            def step(g, k, s):
                if past(g, RING):
                    sp.wait_ge(sum_ready, g - RING + 1)
                    sp.wait_ge(rden_ready, g - RING + 1)
                    sp.wait_ge(sdeg_ready, g - RING + 1)
                    sp.wait_ge(num_ready, g - RING + 1)
                    sp.sem_inc(sc.ticks, 1)
                sp.dma_start(x[:, s, :, :].rearrange("p t d -> p (t d)"), block_of(x_v, g)).then_inc(x_in[s], 16)
                sp.dma_start(agg[:, s, :, :].rearrange("p t d -> p (t d)"), block_of(agg_v, g)).then_inc(agg_in[s], 16)
            sweep(sp, groups, step, RING)

        @block.gpsimd
        def _(pool):
            def store(g, s):
                pool.wait_ge(x1_ready, g + 1)
                pool.dma_start(block_of(x1_v, g), x1[:, s, :, :].rearrange("p t d -> p (t d)")).then_inc(x1_out[s], 16)

            def step(g, k, s):
                if past(g, 2):
                    sums(g - 2, *before(k, s, 2))
                pool.wait_ge(h_ready, g + 1)
                pool.wait_ge(agg_in[s], 16 * (k + 1))
                if past(g, 2):
                    pool.wait_ge(mean_ready, g - 1)
                nc.gpsimd.tensor_tensor(num[:, s % 2, :, :], h[:, s % 2, :, :], agg[:, s, :, 0:D],
                                        ALU.add).then_inc(num_ready, 1)
                if past(g, 5):
                    store(g - 5, (s - 5) % RING)

            def sums(g, k, s):
                pool.wait_ge(mean_ready, g + 1)
                if past(g, RING):
                    pool.wait_ge(x1_out[s], 16 * k)
                nc.gpsimd.tensor_tensor(x1[:, s, :, 0:D], mean[:, s % 2, :, :], x[:, s, :, :],
                                        ALU.add).then_inc(sum_ready, 1)
            sweep(pool, groups, step, RING)
            for g in (groups - 2, groups - 1):
                sums(g, g // RING, g % RING)
            for g in range(groups - 5, groups):
                store(g, g % RING)
            for s in range(RING):
                pool.wait_ge(x1_out[s], 16 * rounds_of(groups, s))

        @block.vector
        def _(dve):
            def stats_of_x1(g, s):
                dve.wait_ge(sum_ready, g + 1)
                for j in range(T):
                    last = nc.vector.bn_stats(stats1[:, s % 2, j, :], x1[:, s, j, 0:D])
                last.then_inc(stats1_ready, 1)

            def moments_of_x1(g, s):
                dve.wait_ge(stats1_ready, g + 1)
                dve.sem_inc(sc.ticks, 1)
                for j in range(T):
                    last = nc.vector.bn_aggr(mom1[:, s % 2, j, :], stats1[:, s % 2, j, :])
                last.then_inc(mom1_ready, 1)

            def scale_of_x1(g, s):
                dve.wait_ge(std1_ready, g + 1)
                nc.vector.reciprocal(x1[:, s, :, D], std1[:, s % 2, :]).then_inc(inv1_ready, 1)

            def offset_of_x1(g, s):
                dve.wait_ge(inv1_ready, g + 1)
                nc.vector.scalar_tensor_tensor(x1[:, s, :, D + 1], mom1[:, s % 2, :, 0], -1.0, x1[:, s, :, D], ALU.mult,
                                               ALU.mult).then_inc(x1_ready, 1)

            def step(g, k, s):
                dve.wait_ge(x_in[s], 16 * (k + 1))
                for j in range(T):
                    last = nc.vector.bn_stats(stats[:, s % 2, j, :], x[:, s, j, :])
                last.then_inc(stats_ready, 1)
                if past(g, 5):
                    scale_of_x1(g - 5, (s - 5) % RING)
                if past(g, 4):
                    stats_of_x1(g - 4, (s - 4) % RING)
                dve.wait_ge(stats_ready, g + 1)
                dve.sem_inc(sc.ticks, 1)
                for j in range(T):
                    last = nc.vector.bn_aggr(mom[:, s % 2, j, :], stats[:, s % 2, j, :])
                last.then_inc(mom_ready, 1)
                dve.wait_ge(agg_in[s], 16 * (k + 1))
                nc.vector.tensor_scalar(den[:, s % 2, :], agg[:, s, :, D], c["w_self"][:, :], None,
                                        ALU.add).then_inc(den_ready, 1)
                if past(g, 5):
                    offset_of_x1(g - 5, (s - 5) % RING)
                if past(g, 4):
                    moments_of_x1(g - 4, (s - 4) % RING)
                dve.wait_ge(den_ready, g + 1)
                if past(g, RING):
                    dve.wait_ge(mean_ready, g - RING + 1)
                nc.vector.reciprocal(rden[:, s, :], den[:, s % 2, :]).then_inc(rden_ready, 1)
                dve.wait_ge(std_ready, g + 1)
                nc.vector.reciprocal(inv[:, s % 2, :], std[:, s % 2, :]).then_inc(inv_ready, 1)
                dve.wait_ge(sdeg_ready, g + 1)
                nc.vector.reciprocal(isq[:, s % 2, :], sdeg[:, s % 2, :]).then_inc(isq_ready, 1)
                dve.wait_ge(inv_ready, g + 1)
                if past(g, 2):
                    dve.wait_ge(h_ready, g - 1)
                nc.vector.tensor_scalar(scale[:, s % 2, :], inv[:, s % 2, :], c["w_self"][:, :], None,
                                        ALU.mult).then_inc(scale_ready, 1)
                dve.wait_ge(isq_ready, g + 1)
                nc.vector.tensor_scalar(isq_all[:, bass.ds(T * g, T)], isq[:, s % 2, :], 0.0, None,
                                        ALU.add).then_inc(kept, 1)
                dve.wait_ge(scale_ready, g + 1)
                nc.vector.scalar_tensor_tensor(off[:, s % 2, :], mom[:, s % 2, :, 0], -1.0, scale[:, s % 2, :], ALU.mult,
                                               ALU.mult).then_inc(off_ready, 1)
            sweep(dve, groups, step, RING)
            for g in range(groups - 5, groups):
                if g > groups - 5:
                    stats_of_x1(g, g % RING)
                    moments_of_x1(g, g % RING)
                scale_of_x1(g, g % RING)
                offset_of_x1(g, g % RING)

        @block.scalar
        def _(act):
            def root1(g, s):
                act.wait_ge(mom1_ready, g + 1)
                if past(g, 2):
                    act.wait_ge(inv1_ready, g - 1)
                nc.scalar.activation(std1[:, s % 2, :], mom1[:, s % 2, :, 1], ACT.Sqrt,
                                     bias=c["ln_eps"][:, :]).then_inc(std1_ready, 1)

            def step(g, k, s):
                act.wait_ge(mom_ready, g + 1)
                nc.scalar.activation(std[:, s % 2, :], mom[:, s % 2, :, 1], ACT.Sqrt,
                                     bias=c["ln_eps"][:, :]).then_inc(std_ready, 1)
                act.wait_ge(agg_in[s], 16 * (k + 1))
                nc.scalar.activation(sdeg[:, s % 2, :], agg[:, s, :, D + 1], ACT.Sqrt, bias=c["one"][:, :]
                                     ).then_inc(sdeg_ready, 1)
                if past(g, 2):
                    means(g - 2, (s - 2) % RING)
                if past(g, 4):
                    root1(g - 4, (s - 4) % RING)
                act.wait_ge(off_ready, g + 1)
                if past(g, 2):
                    act.wait_ge(num_ready, g - 1)
                for j in range(T):
                    last = nc.scalar.activation(h[:, s % 2, j, :], x[:, s, j, :], ACT.Relu,
                                                scale=scale[:, s % 2, j:j + 1], bias=off[:, s % 2, j:j + 1])
                last.then_inc(h_ready, 1)

            def means(g, s):
                act.wait_ge(num_ready, g + 1)
                act.wait_ge(rden_ready, g + 1)
                if past(g, 2):
                    act.wait_ge(sum_ready, g - 1)
                for j in range(T):
                    last = nc.scalar.activation(mean[:, s % 2, j, :], num[:, s % 2, j, :], ACT.Copy,
                                                scale=rden[:, s, j:j + 1])
                last.then_inc(mean_ready, 1)
            sweep(act, groups, step, RING)
            means(groups - 2, (groups - 2) % RING)
            means(groups - 1, (groups - 1) % RING)
            for g in range(groups - 4, groups):
                root1(g, g % RING)
    sc.close()


def edges_message(nc, c, x, idx_d, row_d, attr_d, table, groups, targets_all, layer, clears):
    two = layer == 2
    DE = D64 if two else D4
    C = FC if two else 1
    if two:
        w_src, w_dst, w_attr, w_out = c["cw1_src"], c["cw1_dst"], c["cw1_attr"], c["cw2"]
        b_hidden, b_out = c["cb1"], c["cb2_row"]
    else:
        w_src, w_dst, w_attr, w_out = c["m1_src"], c["m1_dst"], c["m1_attr"], c["m2"]
        b_hidden, b_out = c["mb1"], c["mb2_row"]
    sc = Scope(nc, f"msg{layer}")
    K = Keys(sc, "dst")
    X = X2 if two else X1
    x_src = sc.sb("x_src", [P, 2, T, X])
    x_dst = sc.sb("x_dst", [P, 2, T, X])
    attr = sc.sb("attr", [DE, 2, W])
    u = sc.sb("u", [P, 2, 2 * T, D])
    if two:
        h = sc.sb("h", [P, 2, 2 * T, D])
        pre = sc.sb("pre", [P, C, W])
        pre_ready = sc.sem("pre_ready")
        h_ready = sc.sem("h_ready")
    src_t = sc.sb("src_t", [P, 2, W])
    dst_t = sc.sb("dst_t", [P, 2, W])
    hid = sc.sb("hid", [P, 2, C, W])
    msg = sc.sb("msg", [P, 2, T, D])
    out = sc.sb("out", [P, 2, T, D])
    p_src = sc.ps("p_src", [P, W])
    p_dst = sc.ps("p_dst", [P, W])
    p_hid = [sc.ps(f"p_hid{i}", [P, W]) for i in range(C)]
    p_msg = sc.ps("p_msg", [P, T, D])
    p_sum = sc.ps("p_sum", [P, T, D])
    attr_in, src_in, dst_in = sc.sem2("attr_in"), sc.sem2("src_in"), sc.sem2("dst_in")
    u_ready, cleared = sc.sem("u_ready"), sc.sem("cleared")
    flipped, src_t_ready, dst_t_ready = sc.sem("flipped"), sc.sem("src_t_ready"), sc.sem("dst_t_ready")
    hid_made, hid_ready = sc.sem("hid_made"), sc.sem("hid_ready")
    msg_made, msg_ready = sc.sem("msg_made"), sc.sem("msg_ready")
    summed, out_ready, added = sc.sem("summed"), sc.sem("out_ready"), sc.sem("added")

    with nc.Block() as block:
        @block.sync
        def _(sp):
            def step(g, k, s):
                if past(g, 2):
                    sp.wait_ge(src_in[s], 16 * T * k)
                    sp.wait_ge(dst_in[s], 16 * T * k)
                    sp.wait_ge(K.same_ready, g - 1)
                    if not two:
                        sp.wait_ge(K.saved, g - 1)
                    sp.sem_inc(sc.ticks, 1)
                index_loads(sp, K, g, k, s, idx_d, row_d)
                sp.dma_start(block_of(clears, g), c["zero"][:, 0:clears.shape[2]]).then_inc(cleared, 16)
            sweep(sp, groups, step)
            sp.wait_ge(cleared, 16 * groups)

        @block.gpsimd
        def _(pool):
            def free(g):
                pool.wait_ge(u_ready, g - 1)
            edge_pool(pool, K, groups, [(x, x_src, 0, src_in), (x, x_dst, T, dst_in)], free, table, out,
                      out_ready, added, 4)

        @block.vector
        def _(dve):
            def scales(s, j, at):
                rows = x_src[:, s, j, :] if j < T else x_dst[:, s, j - T, :]
                return rows[:, at:at + 1], rows[:, at + 1:at + 2]

            def messages(g, s):
                dve.wait_ge(msg_made, g + 1)
                if past(g, 2):
                    dve.wait_ge(summed, g - 1)
                nc.vector.tensor_tensor(msg[:, s, :, :], p_msg[:, :, :], b_out[:, :, :],
                                        ALU.add).then_inc(msg_ready, 1)

            def leak(g, s):
                if past(g, 2):
                    dve.wait_ge(msg_made, g - 1)
                for i in range(C):
                    dve.wait_ge(pre_ready, C * g + i + 1)
                    nc.vector.scalar_tensor_tensor(hid[:, s, i, :], pre[:, i, :], SLOPE, pre[:, i, :], ALU.mult,
                                                   ALU.max).then_inc(hid_ready, 1)

            def step(g, k, s):
                dve.wait_ge(src_in[s], 16 * T * (k + 1))
                dve.wait_ge(dst_in[s], 16 * T * (k + 1))
                if past(g, 2):
                    messages(g - 2, s)
                    dve.wait_ge(flipped, g - 1)
                for j in range(2 * T):
                    if two:
                        dve.wait_ge(h_ready, 2 * T * g + j + 1)
                    rows = h[:, s, j, :] if two else x_src[:, s, j, 0:D] if j < T else x_dst[:, s, j - T, 0:D]
                    scale, offset = scales(s, j, D + 2 if two else D)
                    last = nc.vector.tensor_scalar(u[:, s, j, :], rows, scale, offset, ALU.mult, ALU.add)
                last.then_inc(u_ready, 1)
                if two and past(g, 1):
                    leak(g - 1, 1 - s)
                index_work(nc, dve, K, c, g, k, s, summed, targets_all, not two)
                if past(g, 2):
                    stage_targets(nc, dve, K, g - 2, s, targets_all, added, not two)
            sweep(dve, groups, step)
            messages(groups - 2, (groups - 2) % 2)
            if two:
                leak(groups - 1, (groups - 1) % 2)
            messages(groups - 1, (groups - 1) % 2)
            for g in (groups - 2, groups - 1):
                stage_targets(nc, dve, K, g, g % 2, targets_all, added, not two)

        @block.scalar
        def _(act):
            def sums_out(g, s):
                act.wait_ge(summed, g + 1)
                if past(g, 2):
                    act.wait_ge(added, 16 * T * (g - 1))
                nc.scalar.activation(out[:, s, :, :], p_sum[:, :, :], ACT.Copy).then_inc(out_ready, 1)

            def hidden(g, s):
                if past(g, 2) and not two:
                    act.wait_ge(msg_made, g - 1)
                for i in range(C):
                    act.wait_ge(hid_made, C * g + i + 1)
                    if two:
                        if past(g, 1):
                            act.wait_ge(hid_ready, C * g)
                        nc.scalar.activation(pre[:, i, :], p_hid[i][:, :], ACT.Identity,
                                             bias=b_hidden[:, i:i + 1]).then_inc(pre_ready, 1)
                    else:
                        nc.scalar.activation(hid[:, s, i, :], p_hid[i][:, :], ACT.Relu,
                                             bias=b_hidden[:, i:i + 1]).then_inc(hid_ready, 1)

            def attributes(g, s):
                act.dma_start(attr[:, s, :], block_of(attr_d, g)).then_inc(attr_in[s], 16)

            def step(g, k, s):
                if two:
                    act.wait_ge(src_in[s], 16 * T * (k + 1))
                    act.wait_ge(dst_in[s], 16 * T * (k + 1))
                    if past(g, 2):
                        act.wait_ge(u_ready, g - 1)
                    for j in range(2 * T):
                        rows = x_src[:, s, j, :] if j < T else x_dst[:, s, j - T, :]
                        nc.scalar.activation(h[:, s, j, :], rows[:, 0:D], ACT.Relu, scale=rows[:, D:D + 1],
                                             bias=rows[:, D + 1:D + 2]).then_inc(h_ready, 1)
                if past(g, 1):
                    hidden(g - 1, 1 - s)
                    if ahead(g, groups):
                        attributes(g + 1, 1 - s)
                if past(g, 2):
                    sums_out(g - 2, s)
                act.wait_ge(flipped, g + 1)
                if past(g, 2):
                    act.wait_ge(hid_made, C * (g - 1))
                if two:
                    nc.scalar.activation(src_t[:, s, :], p_src[:, :], ACT.Identity, scale=c["ln1_g"][:, :],
                                         bias=c["ln1_b"][:, :]).then_inc(src_t_ready, 1)
                    nc.scalar.activation(dst_t[:, s, :], p_dst[:, :], ACT.Identity, scale=c["ln1_g"][:, :],
                                         bias=c["ln1_b"][:, :]).then_inc(dst_t_ready, 1)
                else:
                    nc.scalar.activation(src_t[:, s, :], p_src[:, :], ACT.Relu).then_inc(src_t_ready, 1)
                    nc.scalar.activation(dst_t[:, s, :], p_dst[:, :], ACT.Relu).then_inc(dst_t_ready, 1)
            attributes(0, 0)
            attributes(1, 1)
            sweep(act, groups, step)
            hidden(groups - 1, (groups - 1) % 2)
            sums_out(groups - 2, (groups - 2) % 2)
            sums_out(groups - 1, (groups - 1) % 2)

        @block.tensor
        def _(pe):
            def to_messages(g, s):
                pe.wait_ge(hid_ready, C * (g + 1))
                if past(g, 1):
                    pe.wait_ge(msg_ready, g)
                for j in range(T):
                    for i in range(C):
                        last = nc.tensor.matmul(p_msg[:, j, :], hid[:, s, i, j * P:(j + 1) * P], w_out[:, i, :],
                                                start=(i == 0), stop=(i == C - 1))
                last.then_inc(msg_made, 1)

            def sum_equal(g, s):
                pe.wait_ge(msg_ready, g + 1)
                pe.wait_ge(K.same_ready, g + 1)
                if past(g, 1):
                    pe.wait_ge(out_ready, g)
                sum_equal_keys(nc, K, s, p_sum, D, msg).then_inc(summed, 1)

            def step(g, k, s):
                if past(g, 2):
                    sum_equal(g - 2, s)
                pe.wait_ge(u_ready, g + 1)
                if past(g, 1):
                    pe.wait_ge(src_t_ready, g)
                    pe.wait_ge(dst_t_ready, g)
                for j in range(T):
                    nc.tensor.transpose(p_src[:, j * P:(j + 1) * P], u[:, s, j, :], c["ident"][:, :])
                    last = nc.tensor.transpose(p_dst[:, j * P:(j + 1) * P], u[:, s, T + j, :], c["ident"][:, :])
                last.then_inc(flipped, 1)
                if past(g, 1):
                    to_messages(g - 1, 1 - s)
                pe.wait_ge(src_t_ready, g + 1)
                pe.wait_ge(dst_t_ready, g + 1)
                pe.wait_ge(attr_in[s], 16 * (k + 1))
                if past(g, 1):
                    pe.wait_ge(pre_ready if two else hid_ready, C * g)
                for i in range(C):
                    cols = slice(i * D, (i + 1) * D)
                    nc.tensor.matmul(p_hid[i][:, :], w_src[:, cols], src_t[:, s, :], start=True, stop=False)
                    nc.tensor.matmul(p_hid[i][:, :], w_dst[:, cols], dst_t[:, s, :], start=False, stop=False)
                    nc.tensor.matmul(p_hid[i][:, :], w_attr[:, cols], attr[:, s, :], start=False,
                                     stop=True).then_inc(hid_made, 1)
            sweep(pe, groups, step)
            sum_equal(groups - 2, (groups - 2) % 2)
            to_messages(groups - 1, (groups - 1) % 2)
            sum_equal(groups - 1, (groups - 1) % 2)
    sc.close()


def nodes_gated(nc, c, x1_v, agg_v, x2_v, groups):
    sc = Scope(nc, "gru")
    x = sc.sb("x", [P, RING, T, X1])
    agg = sc.sb("agg", [P, RING, T, D])
    u = sc.sb("u", [P, 2, T, D])
    h_t = sc.sb("h_t", [P, 2, W])
    a_t = sc.sb("a_t", [P, 2, W])
    z = sc.sb("z", [P, 2, W])
    r = sc.sb("r", [P, 2, W])
    rh = sc.sb("rh", [P, 2, W])
    cand = sc.sb("cand", [P, 2, W])
    step_t = sc.sb("step_t", [P, 2, W])
    gated = sc.sb("gated", [P, 2, W])
    o_t = sc.sb("o_t", [P, 2, W])
    x2 = sc.sb("x2", [P, RING, T, X2])
    h2 = sc.sb("h2", [P, 2, T, D])
    stats = sc.sb("stats", [P, 2, T, 6])
    mom = sc.sb("mom", [P, 2, T, 2])
    var = sc.sb("var", [P, 2, T])
    var_b = sc.sb("var_b", [P, 2, T])
    stats_b = sc.sb("stats_b", [P, 2, T, 6])
    mom_b = sc.sb("mom_b", [P, 2, T, 2])
    p_h, p_a, p_z, p_r, p_c = (sc.ps(n, [P, W]) for n in ("p_h", "p_a", "p_z", "p_r", "p_c"))
    p_o = sc.ps("p_o", [P, T, D])
    x_in, agg_in, x2_out = sc.sem2("x_in", RING), sc.sem2("agg_in", RING), sc.sem2("x2_out", RING)
    u_ready, flipped = sc.sem("u_ready"), sc.sem("flipped")
    h_t_ready, a_t_ready = sc.sem("h_t_ready"), sc.sem("a_t_ready")
    r_made, r_ready, z_made, z_ready = sc.sem("r_made"), sc.sem("r_ready"), sc.sem("z_made"), sc.sem("z_ready")
    rh_ready, c_made, c_ready = sc.sem("rh_ready"), sc.sem("c_made"), sc.sem("c_ready")
    step_ready, gated_ready, o_t_ready = sc.sem("step_ready"), sc.sem("gated_ready"), sc.sem("o_t_ready")
    back_made, x2_ready = sc.sem("back_made"), sc.sem("x2_ready")
    sum_ready, stats_ready, mom_ready = sc.sem("sum_ready"), sc.sem("stats_ready"), sc.sem("mom_ready")
    inv_ready, off_ready, h2_ready = sc.sem("inv_ready"), sc.sem("off_ready"), sc.sem("h2_ready")
    var_ready, var_b_ready = sc.sem("var_ready"), sc.sem("var_b_ready")
    stats_b_ready, mom_b_ready, inv_b_ready = (sc.sem("stats_b_ready"), sc.sem("mom_b_ready"),
                                               sc.sem("inv_b_ready"))
    with nc.Block() as block:
        @block.sync
        def _(sp):
            def step(g, k, s):
                if past(g, RING):
                    sp.wait_ge(sum_ready, g - RING + 1)
                    sp.wait_ge(flipped, g - RING + 1)
                    sp.sem_inc(sc.ticks, 1)
                sp.dma_start(x[:, s, :, :].rearrange("p t d -> p (t d)"), block_of(x1_v, g)).then_inc(x_in[s], 16)
                sp.dma_start(agg[:, s, :, :].rearrange("p t d -> p (t d)"), block_of(agg_v, g)).then_inc(agg_in[s], 16)
            sweep(sp, groups, step, RING)

        @block.gpsimd
        def _(pool):
            def blend(g, s):
                pool.wait_ge(c_ready, g + 1)
                nc.gpsimd.tensor_tensor(step_t[:, s % 2, :], cand[:, s % 2, :], h_t[:, s % 2, :],
                                        ALU.subtract).then_inc(step_ready, 1)
                pool.wait_ge(step_ready, g + 1)
                pool.wait_ge(z_ready, g + 1)
                if past(g, 2):
                    pool.wait_ge(o_t_ready, g - 1)
                nc.gpsimd.tensor_tensor(gated[:, s % 2, :], z[:, s % 2, :], step_t[:, s % 2, :],
                                        ALU.mult).then_inc(gated_ready, 1)

            def scale(g, s):
                pool.wait_ge(var_ready, g + 1)
                nc.gpsimd.tensor_tensor(x2[:, s, :, D], var[:, s % 2, :], c["power"][:, 0:T],
                                        ALU.pow).then_inc(inv_ready, 1)

            def scale_b(g, s):
                pool.wait_ge(var_b_ready, g + 1)
                nc.gpsimd.tensor_tensor(x2[:, s, :, D + 2], var_b[:, s % 2, :], c["power"][:, 0:T],
                                        ALU.pow).then_inc(inv_b_ready, 1)

            def store(g, s):
                pool.wait_ge(x2_ready, g + 1)
                pool.dma_start(block_of(x2_v, g), x2[:, s, :, :].rearrange("p t d -> p (t d)")).then_inc(x2_out[s], 16)

            def step(g, k, s):
                blend(g, s)
                if past(g, 1):
                    scale(g - 1, (s - 1) % RING)
                if past(g, 2):
                    scale_b(g - 2, (s - 2) % RING)
                if past(g, 3):
                    store(g - 3, (s - 3) % RING)
            sweep(pool, groups, step, RING)
            scale(groups - 1, (groups - 1) % RING)
            scale_b(groups - 2, (groups - 2) % RING)
            store(groups - 3, (groups - 3) % RING)
            scale_b(groups - 1, (groups - 1) % RING)
            store(groups - 2, (groups - 2) % RING)
            store(groups - 1, (groups - 1) % RING)
            for s in range(RING):
                pool.wait_ge(x2_out[s], 16 * rounds_of(groups, s))

        @block.vector
        def _(dve):
            def back(g, k, s):
                dve.wait_ge(gated_ready, g + 1)
                if past(g, 2):
                    dve.wait_ge(back_made, g - 1)
                nc.vector.tensor_tensor(o_t[:, s % 2, :], gated[:, s % 2, :], h_t[:, s % 2, :], ALU.add).then_inc(o_t_ready, 1)

            def finish(g, k, s):
                dve.wait_ge(back_made, g + 1)
                if past(g, RING):
                    dve.wait_ge(x2_out[s], 16 * k)
                nc.vector.tensor_tensor(x2[:, s, :, 0:D], p_o[:, :, :], x[:, s, :, 0:D], ALU.add).then_inc(sum_ready, 1)
                dve.wait_ge(sum_ready, g + 1)
                for j in range(T):
                    last = nc.vector.bn_stats(stats[:, s % 2, j, :], x2[:, s, j, 0:D])
                last.then_inc(stats_ready, 1)
                dve.wait_ge(stats_ready, g + 1)
                dve.sem_inc(sc.ticks, 1)
                for j in range(T):
                    last = nc.vector.bn_aggr(mom[:, s % 2, j, :], stats[:, s % 2, j, :])
                last.then_inc(mom_ready, 1)
                dve.wait_ge(mom_ready, g + 1)
                if past(g, 2):
                    dve.wait_ge(inv_ready, g - 1)
                nc.vector.tensor_scalar(var[:, s % 2, :], mom[:, s % 2, :, 1], LN_EPS, None,
                                        ALU.add).then_inc(var_ready, 1)

            def offset(g, s):
                dve.wait_ge(inv_ready, g + 1)
                nc.vector.scalar_tensor_tensor(x2[:, s, :, D + 1], mom[:, s % 2, :, 0], -1.0, x2[:, s, :, D], ALU.mult,
                                               ALU.mult).then_inc(off_ready, 1)

            def again(g, s):
                dve.wait_ge(h2_ready, g + 1)
                for j in range(T):
                    last = nc.vector.bn_stats(stats_b[:, s % 2, j, :], h2[:, s % 2, j, :])
                last.then_inc(stats_b_ready, 1)
                dve.wait_ge(stats_b_ready, g + 1)
                dve.sem_inc(sc.ticks, 1)
                for j in range(T):
                    last = nc.vector.bn_aggr(mom_b[:, s % 2, j, :], stats_b[:, s % 2, j, :])
                last.then_inc(mom_b_ready, 1)
                dve.wait_ge(mom_b_ready, g + 1)
                if past(g, 2):
                    dve.wait_ge(inv_b_ready, g - 1)
                nc.vector.tensor_scalar(var_b[:, s % 2, :], mom_b[:, s % 2, :, 1], LN_EPS, None,
                                        ALU.add).then_inc(var_b_ready, 1)

            def offset_b(g, s):
                dve.wait_ge(inv_b_ready, g + 1)
                nc.vector.scalar_tensor_tensor(x2[:, s, :, D + 3], mom_b[:, s % 2, :, 0], -1.0, x2[:, s, :, D + 2],
                                               ALU.mult, ALU.mult).then_inc(x2_ready, 1)

            def step(g, k, s):
                dve.wait_ge(flipped, g + 1)
                if past(g, 2):
                    dve.wait_ge(o_t_ready, g - 1)
                nc.vector.tensor_scalar_max(h_t[:, s % 2, :], p_h[:, :], 0.0).then_inc(h_t_ready, 1)
                if past(g, 3):
                    offset(g - 3, (s - 3) % RING)
                if past(g, 4):
                    offset_b(g - 4, (s - 4) % RING)
                if past(g, 2):
                    finish(g - 2, *before(k, s, 2))
                if past(g, 3):
                    again(g - 3, (s - 3) % RING)
                dve.wait_ge(r_ready, g + 1)
                dve.wait_ge(h_t_ready, g + 1)
                if past(g, 2):
                    dve.wait_ge(c_made, g - 1)
                nc.vector.tensor_tensor(rh[:, s % 2, :], r[:, s % 2, :], h_t[:, s % 2, :], ALU.mult).then_inc(rh_ready, 1)
                if past(g, 1):
                    back(g - 1, *before(k, s, 1))
            sweep(dve, groups, step, RING)
            back(groups - 1, (groups - 1) // RING, (groups - 1) % RING)
            offset(groups - 3, (groups - 3) % RING)
            offset_b(groups - 4, (groups - 4) % RING)
            finish(groups - 2, (groups - 2) // RING, (groups - 2) % RING)
            again(groups - 3, (groups - 3) % RING)
            offset(groups - 2, (groups - 2) % RING)
            offset_b(groups - 3, (groups - 3) % RING)
            finish(groups - 1, (groups - 1) // RING, (groups - 1) % RING)
            again(groups - 2, (groups - 2) % RING)
            offset(groups - 1, (groups - 1) % RING)
            offset_b(groups - 2, (groups - 2) % RING)
            again(groups - 1, (groups - 1) % RING)
            offset_b(groups - 1, (groups - 1) % RING)

        @block.scalar
        def _(act):
            def candidate(g, s):
                act.wait_ge(c_made, g + 1)
                if past(g, 2):
                    act.wait_ge(step_ready, g - 1)
                nc.scalar.activation(cand[:, s % 2, :], p_c[:, :], ACT.Tanh, bias=c["gb_h"][:, :]).then_inc(c_ready, 1)

            def rows(g, k, s):
                act.wait_ge(x_in[s], 16 * (k + 1))
                if past(g, 2):
                    act.wait_ge(flipped, g - 1)
                for j in range(T):
                    last = nc.scalar.activation(u[:, s % 2, j, :], x[:, s, j, 0:D], ACT.Identity,
                                                scale=x[:, s, j, D:D + 1], bias=x[:, s, j, D + 1:D + 2])
                last.then_inc(u_ready, 1)

            def rectify(g, s):
                act.wait_ge(off_ready, g + 1)
                if past(g, 2):
                    act.wait_ge(stats_b_ready, g - 1)
                for j in range(T):
                    last = nc.scalar.activation(h2[:, s % 2, j, :], x2[:, s, j, 0:D], ACT.Relu,
                                                scale=x2[:, s, j, D:D + 1], bias=x2[:, s, j, D + 1:D + 2])
                last.then_inc(h2_ready, 1)

            def step(g, k, s):
                act.wait_ge(flipped, g + 1)
                if past(g, 2):
                    act.wait_ge(c_made, g - 1)
                nc.scalar.activation(a_t[:, s % 2, :], p_a[:, :], ACT.Copy).then_inc(a_t_ready, 1)
                if past(g, 3):
                    rectify(g - 3, (s - 3) % RING)
                if past(g, 1):
                    candidate(g - 1, (s - 1) % RING)
                if ahead(g, groups):
                    rows(g + 1, *after(k, s))
                act.wait_ge(r_made, g + 1)
                if past(g, 2):
                    act.wait_ge(rh_ready, g - 1)
                nc.scalar.activation(r[:, s % 2, :], p_r[:, :], ACT.Sigmoid, bias=c["gb_r"][:, :]).then_inc(r_ready, 1)
                act.wait_ge(z_made, g + 1)
                if past(g, 2):
                    act.wait_ge(gated_ready, g - 1)
                nc.scalar.activation(z[:, s % 2, :], p_z[:, :], ACT.Sigmoid, bias=c["gb_z"][:, :]).then_inc(z_ready, 1)
            rows(0, 0, 0)
            sweep(act, groups, step, RING)
            candidate(groups - 1, (groups - 1) % RING)
            rectify(groups - 3, (groups - 3) % RING)
            rectify(groups - 2, (groups - 2) % RING)
            rectify(groups - 1, (groups - 1) % RING)

        @block.tensor
        def _(pe):
            def candidate(g, s):
                pe.wait_ge(rh_ready, g + 1)
                if past(g, 1):
                    pe.wait_ge(c_ready, g)
                nc.tensor.matmul(p_c[:, :], c["gw_h"][:, 1, :], a_t[:, s % 2, :], start=True, stop=False)
                nc.tensor.matmul(p_c[:, :], c["gw_h"][:, 0, :], rh[:, s % 2, :], start=False,
                                 stop=True).then_inc(c_made, 1)

            def turn_back(g, s):
                pe.wait_ge(o_t_ready, g + 1)
                if past(g, 1):
                    pe.wait_ge(sum_ready, g)
                for j in range(T):
                    last = nc.tensor.transpose(p_o[:, j, :], o_t[:, s % 2, j * P:(j + 1) * P], c["ident"][:, :])
                last.then_inc(back_made, 1)

            def step(g, k, s):
                pe.wait_ge(u_ready, g + 1)
                pe.wait_ge(agg_in[s], 16 * (k + 1))
                if past(g, 1):
                    pe.wait_ge(h_t_ready, g)
                    pe.wait_ge(a_t_ready, g)
                for j in range(T):
                    nc.tensor.transpose(p_h[:, j * P:(j + 1) * P], u[:, s % 2, j, :], c["ident"][:, :])
                    last = nc.tensor.transpose(p_a[:, j * P:(j + 1) * P], agg[:, s, j, :], c["ident"][:, :])
                last.then_inc(flipped, 1)
                if past(g, 2):
                    turn_back(g - 2, (s - 2) % RING)
                if past(g, 1):
                    candidate(g - 1, (s - 1) % RING)
                pe.wait_ge(h_t_ready, g + 1)
                pe.wait_ge(a_t_ready, g + 1)
                if past(g, 1):
                    pe.wait_ge(r_ready, g)
                    pe.wait_ge(z_ready, g)
                nc.tensor.matmul(p_r[:, :], c["gw_r"][:, 0, :], h_t[:, s % 2, :], start=True, stop=False)
                nc.tensor.matmul(p_r[:, :], c["gw_r"][:, 1, :], a_t[:, s % 2, :], start=False,
                                 stop=True).then_inc(r_made, 1)
                nc.tensor.matmul(p_z[:, :], c["gw_z"][:, 0, :], h_t[:, s % 2, :], start=True, stop=False)
                nc.tensor.matmul(p_z[:, :], c["gw_z"][:, 1, :], a_t[:, s % 2, :], start=False,
                                 stop=True).then_inc(z_made, 1)
            sweep(pe, groups, step, RING)
            candidate(groups - 1, (groups - 1) % RING)
            turn_back(groups - 2, (groups - 2) % RING)
            turn_back(groups - 1, (groups - 1) % RING)
    sc.close()


def nodes_feedforward(nc, c, x2_v, agg_v, x3_v, groups, isq_all):
    sc = Scope(nc, "ff")
    x = sc.sb("x", [P, RING, T, X2])
    agg = sc.sb("agg", [P, RING, T, D])
    h = sc.sb("h", [P, 2, T, D])
    y = sc.sb("y", [P, RING, T, D])
    stats = sc.sb("stats", [P, 2, T, 6])
    mom = sc.sb("mom", [P, 2, T, 2])
    stats3 = sc.sb("stats3", [P, 2, T, 6])
    mom3 = sc.sb("mom3", [P, 2, T, 2])
    std3 = sc.sb("std3", [P, 2, T])
    inv3 = sc.sb("inv3", [P, 2, T])
    std = sc.sb("std", [P, 2, T])
    inv = sc.sb("inv", [P, 2, T])
    off = sc.sb("off", [P, 2, T])
    u = sc.sb("u", [P, 2, T, D])
    u_t = sc.sb("u_t", [P, 2, W])
    pre = sc.sb("pre", [P, FC, W])
    hid = sc.sb("hid", [P, 2, FC, W])
    rest = sc.sb("rest", [P, 2, T, D])
    rest_b = sc.sb("rest_b", [P, RING, T, D])
    x3 = sc.sb("x3", [P, RING, T, X3])
    p_t = sc.ps("p_t", [P, W])
    p_hid = [sc.ps(f"p_hid{i}", [P, W]) for i in range(FC)]
    p_o = [sc.ps(f"p_o{s}", [P, T, D]) for s in range(2)]
    x_in, agg_in, x3_out = sc.sem2("x_in", RING), sc.sem2("agg_in", RING), sc.sem2("x3_out", RING)
    h_ready, y_ready, std_ready, std3_ready = (sc.sem("h_ready"), sc.sem("y_ready"), sc.sem("std_ready"),
                                               sc.sem("std3_ready"))
    stats_ready, mom_ready = sc.sem("stats_ready"), sc.sem("mom_ready")
    isq_ready, sum_ready, stats3_ready = sc.sem("isq_ready"), sc.sem("sum_ready"), sc.sem("stats3_ready")
    mom3_ready, inv3_ready, scale3_ready = sc.sem("mom3_ready"), sc.sem("inv3_ready"), sc.sem("scale3_ready")
    inv_ready, off_ready, u_ready = sc.sem("inv_ready"), sc.sem("off_ready"), sc.sem("u_ready")
    flipped, u_t_ready = sc.sem("flipped"), sc.sem("u_t_ready")
    hid_made, pre_ready, hid_ready = sc.sem("hid_made"), sc.sem("pre_ready"), sc.sem("hid_ready")
    rest_ready, rest_b_ready, out_made, x3_ready = (sc.sem("rest_ready"), sc.sem("rest_b_ready"),
                                                    sc.sem("out_made"), sc.sem("x3_ready"))
    with nc.Block() as block:
        @block.sync
        def _(sp):
            def step(g, k, s):
                if past(g, RING):
                    sp.wait_ge(rest_ready, g - RING + 1)
                    sp.wait_ge(h_ready, g - RING + 1)
                    sp.wait_ge(y_ready, g - RING + 1)
                    sp.sem_inc(sc.ticks, 1)
                sp.dma_start(x[:, s, :, :].rearrange("p t d -> p (t d)"), block_of(x2_v, g)).then_inc(x_in[s], 16)
                sp.dma_start(agg[:, s, :, :].rearrange("p t d -> p (t d)"), block_of(agg_v, g)).then_inc(agg_in[s], 16)
            sweep(sp, groups, step, RING)

        @block.gpsimd
        def _(pool):
            def store(g, s):
                pool.wait_ge(x3_ready, g + 1)
                pool.dma_start(block_of(x3_v, g), x3[:, s, :, :].rearrange("p t d -> p (t d)")).then_inc(x3_out[s], 16)

            def sums(g, k, s):
                pool.wait_ge(h_ready, g + 1)
                pool.wait_ge(agg_in[s], 16 * (k + 1))
                if past(g, RING):
                    pool.wait_ge(u_ready, g - RING + 1)
                nc.gpsimd.tensor_tensor(y[:, s, :, :], h[:, s % 2, :, :], agg[:, s, :, :],
                                        ALU.add).then_inc(y_ready, 1)

            def rests(g, s):
                if past(g, 2):
                    pool.wait_ge(rest_b_ready, g - 1)
                pool.wait_ge(y_ready, g + 1)
                nc.gpsimd.tensor_tensor(rest[:, s % 2, :, :], x[:, s, :, 0:D], y[:, s, :, :],
                                        ALU.add).then_inc(rest_ready, 1)
                pool.wait_ge(rest_ready, g + 1)
                if past(g, RING):
                    pool.wait_ge(sum_ready, g - RING + 1)
                nc.gpsimd.tensor_tensor(rest_b[:, s, :, :], rest[:, s % 2, :, :], c["fb2_row"][:, :, :],
                                        ALU.add).then_inc(rest_b_ready, 1)

            def step(g, k, s):
                if ahead(g, groups, 1):
                    rests(g + 1, (s + 1) % RING)
                if ahead(g, groups, 3):
                    sums(g + 3, *after(k, s, 3))
                if past(g, 3):
                    store(g - 3, (s - 3) % RING)
            sums(0, 0, 0)
            rests(0, 0)
            sums(1, 0, 1)
            sums(2, 0, 2)
            sweep(pool, groups, step, RING, 3)
            for g in (groups - 3, groups - 2, groups - 1):
                store(g, g % RING)
            for s in range(RING):
                pool.wait_ge(x3_out[s], 16 * rounds_of(groups, s))

        @block.vector
        def _(dve):
            def finish(g, k, s):
                dve.wait_ge(out_made, g + 1)
                dve.wait_ge(rest_b_ready, g + 1)
                if past(g, RING):
                    dve.wait_ge(x3_out[s], 16 * k)
                nc.vector.tensor_tensor(x3[:, s, :, 0:D], p_o[s % 2][:, :, :], rest_b[:, s, :, :],
                                        ALU.add).then_inc(sum_ready, 1)
                nc.vector.tensor_scalar(x3[:, s, :, D], isq_all[:, bass.ds(T * g, T)], 0.0, None,
                                        ALU.add).then_inc(isq_ready, 1)
                dve.wait_ge(sum_ready, g + 1)
                for j in range(T):
                    last = nc.vector.bn_stats(stats3[:, s % 2, j, :], x3[:, s, j, 0:D])
                last.then_inc(stats3_ready, 1)
                dve.wait_ge(stats3_ready, g + 1)
                dve.sem_inc(sc.ticks, 1)
                for j in range(T):
                    last = nc.vector.bn_aggr(mom3[:, s % 2, j, :], stats3[:, s % 2, j, :])
                last.then_inc(mom3_ready, 1)

            def append(g, s):
                dve.wait_ge(std3_ready, g + 1)
                nc.vector.reciprocal(inv3[:, s % 2, :], std3[:, s % 2, :]).then_inc(inv3_ready, 1)
                dve.wait_ge(inv3_ready, g + 1)
                dve.wait_ge(isq_ready, g + 1)
                nc.vector.tensor_tensor(x3[:, s, :, D + 1], inv3[:, s % 2, :], x3[:, s, :, D],
                                        ALU.mult).then_inc(scale3_ready, 1)
                dve.wait_ge(scale3_ready, g + 1)
                nc.vector.scalar_tensor_tensor(x3[:, s, :, D + 2], mom3[:, s % 2, :, 0], -1.0, x3[:, s, :, D + 1],
                                               ALU.mult, ALU.mult).then_inc(x3_ready, 1)

            def moments(g, s):
                dve.wait_ge(y_ready, g + 1)
                for j in range(T):
                    last = nc.vector.bn_stats(stats[:, s % 2, j, :], y[:, s, j, :])
                last.then_inc(stats_ready, 1)
                dve.wait_ge(stats_ready, g + 1)
                dve.sem_inc(sc.ticks, 1)
                for j in range(T):
                    last = nc.vector.bn_aggr(mom[:, s % 2, j, :], stats[:, s % 2, j, :])
                last.then_inc(mom_ready, 1)

            def affine(g, s):
                dve.wait_ge(std_ready, g + 1)
                if past(g, 2):
                    dve.wait_ge(u_ready, g - 1)
                nc.vector.reciprocal(inv[:, s % 2, :], std[:, s % 2, :]).then_inc(inv_ready, 1)
                dve.wait_ge(inv_ready, g + 1)
                nc.vector.scalar_tensor_tensor(off[:, s % 2, :], mom[:, s % 2, :, 0], -1.0, inv[:, s % 2, :], ALU.mult,
                                               ALU.mult).then_inc(off_ready, 1)

            def step(g, k, s):
                if ahead(g, groups, 2):
                    moments(g + 2, (s + 2) % RING)
                if past(g, 3):
                    append(g - 3, (s - 3) % RING)
                if past(g, 2):
                    finish(g - 2, *before(k, s, 2))
                if ahead(g, groups, 2):
                    affine(g + 2, (s + 2) % RING)
                leak(g, s)

            def leak(g, s):
                if past(g, 2):
                    dve.wait_ge(out_made, g - 1)
                for i in range(FC):
                    dve.wait_ge(pre_ready, FC * g + i + 1)
                    nc.vector.scalar_tensor_tensor(hid[:, s % 2, i, :], pre[:, i, :], SLOPE, pre[:, i, :], ALU.mult,
                                                   ALU.max).then_inc(hid_ready, 1)
            for g in (0, 1):
                moments(g, g)
                affine(g, g)
            sweep(dve, groups, step, RING, 3)
            append(groups - 3, (groups - 3) % RING)
            for g in (groups - 2, groups - 1):
                finish(g, g // RING, g % RING)
                append(g, g % RING)

        @block.scalar
        def _(act):
            def flip_out(g, s):
                act.wait_ge(flipped, g + 1)
                if past(g, 2):
                    act.wait_ge(hid_made, FC * (g - 1))
                nc.scalar.activation(u_t[:, s % 2, :], p_t[:, :], ACT.Identity, scale=c["ln2_g"][:, :],
                                     bias=c["ln2_b"][:, :]).then_inc(u_t_ready, 1)

            def hidden(g, s):
                if past(g, 1):
                    act.wait_ge(hid_ready, FC * g)
                for i in range(FC):
                    act.wait_ge(hid_made, FC * g + i + 1)
                    nc.scalar.activation(pre[:, i, :], p_hid[i][:, :], ACT.Identity,
                                         bias=c["fb1"][:, i:i + 1]).then_inc(pre_ready, 1)

            def rows(g, k, s):
                act.wait_ge(x_in[s], 16 * (k + 1))
                if past(g, 2):
                    act.wait_ge(y_ready, g - 1)
                for j in range(T):
                    last = nc.scalar.activation(h[:, s % 2, j, :], x[:, s, j, 0:D], ACT.Relu,
                                                scale=x[:, s, j, D:D + 1], bias=x[:, s, j, D + 1:D + 2])
                last.then_inc(h_ready, 1)

            def normalise(g, s):
                act.wait_ge(off_ready, g + 1)
                if past(g, 2):
                    act.wait_ge(flipped, g - 1)
                for j in range(T):
                    last = nc.scalar.activation(u[:, s % 2, j, :], y[:, s, j, :], ACT.Identity,
                                                scale=inv[:, s % 2, j:j + 1], bias=off[:, s % 2, j:j + 1])
                last.then_inc(u_ready, 1)

            def root(g, s):
                act.wait_ge(mom_ready, g + 1)
                nc.scalar.activation(std[:, s % 2, :], mom[:, s % 2, :, 1], ACT.Sqrt,
                                     bias=c["ln_eps"][:, :]).then_inc(std_ready, 1)

            def root3(g, s):
                act.wait_ge(mom3_ready, g + 1)
                if past(g, 2):
                    act.wait_ge(inv3_ready, g - 1)
                nc.scalar.activation(std3[:, s % 2, :], mom3[:, s % 2, :, 1], ACT.Sqrt,
                                     bias=c["ln_eps"][:, :]).then_inc(std3_ready, 1)

            def step(g, k, s):
                hidden(g, s)
                if ahead(g, groups, 1):
                    flip_out(g + 1, (s + 1) % RING)
                if ahead(g, groups, 2):
                    root(g + 2, (s + 2) % RING)
                if ahead(g, groups, 3):
                    rows(g + 3, *after(k, s, 3))
                if ahead(g, groups, 2):
                    normalise(g + 2, (s + 2) % RING)
                if past(g, 2):
                    root3(g - 2, (s - 2) % RING)
            for g in (0, 1, 2):
                rows(g, 0, g)
            for g in (0, 1):
                root(g, g)
                normalise(g, g)
            flip_out(0, 0)
            sweep(act, groups, step, RING, 3)
            root3(groups - 2, (groups - 2) % RING)
            root3(groups - 1, (groups - 1) % RING)

        @block.tensor
        def _(pe):
            def outputs(g, s):
                pe.wait_ge(hid_ready, FC * (g + 1))
                if past(g, 2):
                    pe.wait_ge(sum_ready, g - 1)
                for j in range(T):
                    for i in range(FC):
                        last = nc.tensor.matmul(p_o[s % 2][:, j, :], hid[:, s % 2, i, j * P:(j + 1) * P], c["fw2"][:, i, :],
                                                start=(i == 0), stop=(i == FC - 1))
                last.then_inc(out_made, 1)

            def flip(g, s):
                pe.wait_ge(u_ready, g + 1)
                if past(g, 1):
                    pe.wait_ge(u_t_ready, g)
                for j in range(T):
                    last = nc.tensor.transpose(p_t[:, j * P:(j + 1) * P], u[:, s % 2, j, :], c["ident"][:, :])
                last.then_inc(flipped, 1)

            def step(g, k, s):
                pe.wait_ge(u_t_ready, g + 1)
                if past(g, 1):
                    pe.wait_ge(pre_ready, FC * g)
                for i in range(FC):
                    nc.tensor.matmul(p_hid[i][:, :], c["fw1"][:, i * D:(i + 1) * D], u_t[:, s % 2, :], start=True,
                                     stop=True).then_inc(hid_made, 1)
                if ahead(g, groups, 1):
                    flip(g + 1, (s + 1) % RING)
                if past(g, 1):
                    outputs(g - 1, (s - 1) % RING)
            flip(0, 0)
            sweep(pe, groups, step, RING, 3)
            outputs(groups - 1, (groups - 1) % RING)
    sc.close()


def edges_convolution(nc, c, x3, idx_d, row_d, table, groups, targets_all):
    sc = Scope(nc, "conv")
    K = Keys(sc, "src")
    x_dst = sc.sb("x_dst", [P, 2, T, X3])
    val = sc.sb("val", [P, 2, T, D])
    out = sc.sb("out", [P, 2, T, D])
    sums = [sc.ps(f"sums{s}", [P, T, D]) for s in range(2)]
    dst_in = sc.sem2("dst_in")
    val_ready, summed, out_ready, added = (sc.sem("val_ready"), sc.sem("summed"), sc.sem("out_ready"),
                                           sc.sem("added"))
    with nc.Block() as block:
        @block.sync
        def _(sp):
            def step(g, k, s):
                if past(g, 2):
                    sp.wait_ge(dst_in[s], 16 * T * k)
                    sp.wait_ge(K.same_ready, g - 1)
                    sp.sem_inc(sc.ticks, 1)
                index_loads(sp, K, g, k, s, idx_d, row_d)
            sweep(sp, groups, step)

        @block.gpsimd
        def _(pool):
            def free(g):
                pool.wait_ge(val_ready, g - 1)
            edge_pool(pool, K, groups, [(x3, x_dst, T, dst_in)], free, table, out, out_ready, added, 3)

        @block.vector
        def _(dve):
            def step(g, k, s):
                index_work(nc, dve, K, c, g, k, s, summed, targets_all, False)
                if past(g, 1):
                    stage_targets(nc, dve, K, g - 1, 1 - s, targets_all, added, False)
            sweep(dve, groups, step)
            stage_targets(nc, dve, K, groups - 1, (groups - 1) % 2, targets_all, added, False)

        @block.scalar
        def _(act):
            def sums_out(g, s):
                act.wait_ge(summed, g + 1)
                if past(g, 2):
                    act.wait_ge(added, 16 * T * (g - 1))
                nc.scalar.activation(out[:, s, :, :], sums[s][:, :, :], ACT.Copy).then_inc(out_ready, 1)

            def step(g, k, s):
                if past(g, 1):
                    sums_out(g - 1, 1 - s)
                act.wait_ge(dst_in[s], 16 * T * (k + 1))
                if past(g, 2):
                    act.wait_ge(summed, g - 1)
                for j in range(T):
                    last = nc.scalar.activation(val[:, s, j, :], x_dst[:, s, j, 0:D], ACT.Relu,
                                                scale=x_dst[:, s, j, D + 1:D + 2], bias=x_dst[:, s, j, D + 2:D + 3])
                last.then_inc(val_ready, 1)
            sweep(act, groups, step)
            sums_out(groups - 1, (groups - 1) % 2)

        @block.tensor
        def _(pe):
            def step(g, k, s):
                pe.wait_ge(K.same_ready, g + 1)
                pe.wait_ge(val_ready, g + 1)
                if past(g, 2):
                    pe.wait_ge(out_ready, g - 1)
                sum_equal_keys(nc, K, s, sums[s], D, val).then_inc(summed, 1)
            sweep(pe, groups, step)
    sc.close()


def nodes_convolution(nc, c, x3_v, agg_v, out_v, groups):
    sc = Scope(nc, "nconv")
    x = sc.sb("x", [P, RING, T, X3])
    agg = sc.sb("agg", [P, RING, T, D])
    own = sc.sb("own", [P, 2, T, D])
    both = sc.sb("both", [P, 2, T, D])
    both_t = sc.sb("both_t", [P, 2, W])
    res = sc.sb("res", [P, RING, T, D])
    p_t = [sc.ps(f"p_t{s}", [P, W]) for s in range(2)]
    p_o = [sc.ps(f"p_o{s}", [P, T, D]) for s in range(2)]
    x_in, agg_in, res_out = sc.sem2("x_in", RING), sc.sem2("agg_in", RING), sc.sem2("res_out", RING)
    own_ready, both_ready, flipped = sc.sem("own_ready"), sc.sem("both_ready"), sc.sem("flipped")
    both_t_ready, out_made, res_ready = sc.sem("both_t_ready"), sc.sem("out_made"), sc.sem("res_ready")
    with nc.Block() as block:
        @block.sync
        def _(sp):
            def step(g, k, s):
                if past(g, RING):
                    sp.wait_ge(res_ready, g - RING + 1)
                    sp.sem_inc(sc.ticks, 1)
                sp.dma_start(x[:, s, :, :].rearrange("p t d -> p (t d)"), block_of(x3_v, g)).then_inc(x_in[s], 16)
                sp.dma_start(agg[:, s, :, :].rearrange("p t d -> p (t d)"), block_of(agg_v, g)).then_inc(agg_in[s], 16)
            sweep(sp, groups, step, RING)

        @block.gpsimd
        def _(pool):
            def step(g, k, s):
                pool.wait_ge(res_ready, g + 1)
                pool.dma_start(block_of(out_v, g), res[:, s, :, :].rearrange("p t d -> p (t d)")).then_inc(res_out[s], 16)
            sweep(pool, groups, step, RING)
            for s in range(RING):
                pool.wait_ge(res_out[s], 16 * rounds_of(groups, s))

        @block.vector
        def _(dve):
            def back(g, k, s):
                dve.wait_ge(own_ready, g + 1)
                dve.wait_ge(agg_in[s], 16 * (k + 1))
                if past(g, 2):
                    dve.wait_ge(flipped, g - 1)
                nc.vector.tensor_tensor(both[:, s % 2, :, :], agg[:, s, :, :], own[:, s % 2, :, :],
                                        ALU.add).then_inc(both_ready, 1)

            def finish(g, k, s):
                dve.wait_ge(out_made, g + 1)
                if past(g, RING):
                    dve.wait_ge(res_out[s], 16 * k)
                for j in range(T):
                    last = nc.vector.scalar_tensor_tensor(res[:, s, j, :], p_o[s % 2][:, j, :], x[:, s, j, D:D + 1],
                                                          x[:, s, j, 0:D], ALU.mult, ALU.add)
                last.then_inc(res_ready, 1)

            def step(g, k, s):
                back(g, k, s)
                if past(g, 2):
                    finish(g - 2, *before(k, s, 2))
            sweep(dve, groups, step, RING)
            finish(groups - 2, (groups - 2) // RING, (groups - 2) % RING)
            finish(groups - 1, (groups - 1) // RING, (groups - 1) % RING)

        @block.scalar
        def _(act):
            def step(g, k, s):
                act.wait_ge(x_in[s], 16 * (k + 1))
                if past(g, 2):
                    act.wait_ge(both_ready, g - 1)
                for j in range(T):
                    last = nc.scalar.activation(own[:, s % 2, j, :], x[:, s, j, 0:D], ACT.Relu,
                                                scale=x[:, s, j, D + 1:D + 2], bias=x[:, s, j, D + 2:D + 3])
                last.then_inc(own_ready, 1)
                if past(g, 1):
                    flip_out(g - 1, (s - 1) % RING)

            def flip_out(g, s):
                act.wait_ge(flipped, g + 1)
                if past(g, 2):
                    act.wait_ge(out_made, g - 1)
                nc.scalar.activation(both_t[:, s % 2, :], p_t[s % 2][:, :], ACT.Copy).then_inc(both_t_ready, 1)
            sweep(act, groups, step, RING)
            flip_out(groups - 1, (groups - 1) % RING)

        @block.tensor
        def _(pe):
            def step(g, k, s):
                pe.wait_ge(both_ready, g + 1)
                if past(g, 2):
                    pe.wait_ge(both_t_ready, g - 1)
                for j in range(T):
                    last = nc.tensor.transpose(p_t[s % 2][:, j * P:(j + 1) * P], both[:, s % 2, j, :], c["ident"][:, :])
                last.then_inc(flipped, 1)
                pe.wait_ge(both_t_ready, g + 1)
                if past(g, 2):
                    pe.wait_ge(res_ready, g - 1)
                for j in range(T):
                    last = nc.tensor.matmul(p_o[s % 2][:, j, :], both_t[:, s % 2, j * P:(j + 1) * P], c["w3"][:, :],
                                            start=True, stop=True)
                last.then_inc(out_made, 1)
            sweep(pe, groups, step, RING)
    sc.close()


def build(nc, a):
    n_nodes, n_edges = a["x"].shape[0], a["idx"].shape[0] * W
    NG, EG = n_nodes // W, n_edges // W
    table_rows = n_nodes + SET * P
    ctx = ExitStack()

    def sb(name, shape, dt=fp32):
        return ctx.enter_context(nc.sbuf_tensor(name, shape, dt))

    def dram(name, shape):
        return nc.dram_tensor(name, shape, fp32, kind="Internal").ap()

    def groups_of(t, rows):
        return t[0:rows, :].rearrange("(g p t) d -> g p (t d)", p=P, t=T)

    with ctx:
        agg0 = dram("agg0", (table_rows, A0))
        clear_rows = -(-n_nodes // EG // P) * P
        agg = [dram(f"agg{i}", (max(table_rows, clear_rows * EG), D)) for i in (1, 2, 3)]
        x1, x2, x3 = dram("x1", (n_nodes, X1)), dram("x2", (n_nodes, X2)), dram("x3", (n_nodes, X3))

        c = {}
        loads = []
        for name, shape, src in (
                ("ident", [P, P], a["ident"]), ("spare", [P, T], a["spare"]),
                ("beta", [P, 1], a["beta"].partition_broadcast(P)),
                ("m1_src", [P, D], a["m1"][0:D, :]), ("m1_dst", [P, D], a["m1"][D:2 * D, :]),
                ("m1_attr", [D4, D], a["m1"][2 * D:2 * D + D4, :]),
                ("mb1", [P, 1], a["mb1"]), ("mb2_row", [P, W], a["mb2_row"].partition_broadcast(P)),
                ("gb_z", [P, 1], a["gb_z"]), ("gb_r", [P, 1], a["gb_r"]), ("gb_h", [P, 1], a["gb_h"]),
                ("ln1_g", [P, 1], a["ln1_g"]), ("ln1_b", [P, 1], a["ln1_b"]),
                ("ln2_g", [P, 1], a["ln2_g"]), ("ln2_b", [P, 1], a["ln2_b"]),
                ("cw1_dst", [P, F], a["cw1"][0:D, :]), ("cw1_src", [P, F], a["cw1"][D:2 * D, :]),
                ("cw1_attr", [D64, F], a["cw1"][2 * D:2 * D + D64, :]),
                ("cb1", [P, FC], a["cb1"]), ("cb2_row", [P, W], a["cb2_row"].partition_broadcast(P)),
                ("fw1", [P, F], a["fw1"]), ("fb1", [P, FC], a["fb1"]),
                ("fb2_row", [P, W], a["fb2_row"].partition_broadcast(P)), ("w3", [P, D], a["w3"])):
            t = sb(name, shape)
            loads.append((t[:, :], src))
            c[name] = t
        c["below"] = sb("below", [P, SET, SET * P])
        loads.insert(0, (c["below"][:, :, :], a["below"].rearrange("s p k -> p s k")))
        for name, chunks, src in (("m2", 1, a["m2"]), ("gw_z", 2, a["gw_z"]), ("gw_r", 2, a["gw_r"]),
                                  ("gw_h", 2, a["gw_h"]), ("cw2", FC, a["cw2"]), ("fw2", FC, a["fw2"])):
            t = sb(name, [P, chunks, D])
            loads.append((t[:, :, :], src.rearrange("(c k) n -> k c n", k=P)))
            c[name] = t
        for name in ("mb2_row", "cb2_row", "fb2_row"):
            c[name] = c[name][:, :].rearrange("p (t d) -> p t d", t=T)
        c["zero"] = sb("zero", [P, ZEROS * clear_rows * D // P])
        c["power"] = sb("power", [P, T])
        for name in ("ln_eps", "one", "shift", "lead", "w_self"):
            c[name] = sb(name, [P, 1])
        targets_src = sb("targets_src", [P, T * EG], int32)
        targets_dst = sb("targets_dst", [P, T * EG], int32)
        isq_all = sb("isq_all", [P, T * NG])

        def zero_pieces(part):
            flat = part.rearrange("r c -> (r c)")
            piece = P * c["zero"].shape[1]
            for at in range(0, flat.shape[0], piece):
                size = min(piece, flat.shape[0] - at)
                yield flat[at:at + size].rearrange("(p f) -> p f", p=P), c["zero"][:, 0:size // P]

        beyond = clear_rows * EG
        own_clears = [piece for t in [agg0] + [t[beyond:, :] for t in agg if t.shape[0] > beyond]
                      for piece in zero_pieces(t)]
        clears = [t[0:beyond, :].rearrange("(g p r) d -> g p (r d)", g=EG, p=P) for t in agg]
        first = 4
        setup(nc, c, loads[:first], c["beta"])
        edges_attention(nc, c, a["x"], a["idx"], a["src_row"], agg0, EG, targets_src, own_clears, clears[0],
                        loads[first:])
        nodes_attention(nc, c, groups_of(a["x"], n_nodes), groups_of(agg0, n_nodes), groups_of(x1, n_nodes), NG,
                        isq_all)
        edges_message(nc, c, x1, a["idx"], a["dst_row"], a["attr4"], agg[0], EG, targets_dst, 1, clears[1])
        nodes_gated(nc, c, groups_of(x1, n_nodes), groups_of(agg[0], n_nodes), groups_of(x2, n_nodes), NG)
        edges_message(nc, c, x2, a["idx"], a["dst_row"], a["attr64"], agg[1], EG, targets_dst, 2, clears[2])
        nodes_feedforward(nc, c, groups_of(x2, n_nodes), groups_of(agg[1], n_nodes), groups_of(x3, n_nodes), NG,
                          isq_all)
        edges_convolution(nc, c, x3, a["idx"], a["src_row"], agg[2], EG, targets_src)
        nodes_convolution(nc, c, groups_of(x3, n_nodes), groups_of(agg[2], n_nodes), groups_of(a["out"], n_nodes), NG)


def kernel(x, src, dst, edge_attr_4, edge_attr_64, L0_gnn_beta, L1_gnn_W_msg1, L1_gnn_b_msg1, L1_gnn_W_msg2,
           L1_gnn_b_msg2, L1_gnn_W_z, L1_gnn_b_z, L1_gnn_W_r, L1_gnn_b_r, L1_gnn_W_h, L1_gnn_b_h, L2_gnn_ln1_g,
           L2_gnn_ln1_b, L2_gnn_ln2_g, L2_gnn_ln2_b, L2_gnn_conv_w1, L2_gnn_conv_b1, L2_gnn_conv_w2,
           L2_gnn_conv_b2, L2_gnn_ff_w1, L2_gnn_ff_b1, L2_gnn_ff_w2, L2_gnn_ff_b2, L3_gnn_W):
    import numpy as np
    import concourse.bacc as bacc
    from concourse.bass_utils import run_bass_kernel_spmd

    x, src, dst = np.asarray(x), np.asarray(src), np.asarray(dst)
    N, E = x.shape[0], src.shape[0]
    extra_edges = -E % W
    extra_nodes = -N % W
    if extra_edges and not extra_nodes:
        extra_nodes = W
    own = (N + np.arange(extra_edges) % max(extra_nodes, 1)).astype(src.dtype)

    def more(v, n):
        return np.concatenate([v, v[:n]]) if n else v

    def column(v):
        return np.asarray(v).reshape(-1, D).T

    def row4(v):
        return np.tile(np.asarray(v), T)

    def edge_columns(v):
        v = more(np.asarray(v), extra_edges)
        return v.reshape(-1, W, v.shape[1]).transpose(0, 2, 1)

    xp = more(x, extra_nodes)
    src, dst = np.concatenate([src, own]), np.concatenate([dst, own])
    ends = np.stack([src.reshape(-1, T, P), dst.reshape(-1, T, P)], axis=1)
    arrays = {
        "x": xp, "idx": ends.transpose(0, 3, 1, 2).reshape(-1, P, 2 * T),
        "src_row": src.reshape(-1, W), "dst_row": dst.reshape(-1, W),
        "attr4": edge_columns(edge_attr_4), "attr64": edge_columns(edge_attr_64),
        "beta": np.asarray(L0_gnn_beta),
        "m1": L1_gnn_W_msg1, "mb1": column(L1_gnn_b_msg1), "m2": L1_gnn_W_msg2, "mb2_row": row4(L1_gnn_b_msg2),
        "gw_z": L1_gnn_W_z, "gw_r": L1_gnn_W_r, "gw_h": L1_gnn_W_h,
        "gb_z": column(L1_gnn_b_z), "gb_r": column(L1_gnn_b_r), "gb_h": column(L1_gnn_b_h),
        "ln1_g": column(L2_gnn_ln1_g), "ln1_b": column(L2_gnn_ln1_b),
        "ln2_g": column(L2_gnn_ln2_g), "ln2_b": column(L2_gnn_ln2_b),
        "cw1": L2_gnn_conv_w1, "cb1": column(L2_gnn_conv_b1), "cw2": L2_gnn_conv_w2, "cb2_row": row4(L2_gnn_conv_b2),
        "fw1": L2_gnn_ff_w1, "fb1": column(L2_gnn_ff_b1), "fw2": L2_gnn_ff_w2, "fb2_row": row4(L2_gnn_ff_b2),
        "w3": np.asarray(L3_gnn_W).T,
        "ident": np.eye(P, dtype=np.float32), "below": np.tril(np.ones((SET * P, SET * P), np.float32), -1).reshape(SET, P, SET * P),
        "spare": (xp.shape[0] + np.arange(P)[:, None] + P * (np.arange(T) % SET)).astype(np.float32),
    }
    nc = bacc.Bacc("TRN2", target_bir_lowering=False, num_devices=1)
    feeds, aps = {}, {}
    for name, v in arrays.items():
        v = np.ascontiguousarray(v)
        feeds[f"in_{name}"] = v
        aps[name] = nc.dram_tensor(f"in_{name}", v.shape, mybir.dt.from_np(v.dtype), kind="ExternalInput").ap()
    aps["out"] = nc.dram_tensor("out_rows", xp.shape, fp32, kind="ExternalOutput").ap()
    build(nc, aps)
    run = run_bass_kernel_spmd(nc, [feeds], core_ids=[0])
    return run.results[0]["out_rows"][:N]
```
